# Optimizing a Trainium2 kernel written in Bass

```python
import numpy as np
import jax
import jax.numpy as jnp

def _softmax(x, axis=-1):
    return jax.nn.softmax(x, axis=axis)

def _gelu(x):
    return jax.nn.gelu(x, approximate=True)

def _silu(x):
    return jax.nn.silu(x)

def _sigmoid(x):
    return jax.nn.sigmoid(x)

def _layernorm(x, axis=-1, eps=1e-05):
    m = jnp.mean(x, axis=axis, keepdims=True)
    v = jnp.var(x, axis=axis, keepdims=True)
    return (x - m) / jnp.sqrt(v + eps)

def _scatter_add(tgt, idx, src, axis=0):
    return tgt.at[idx].add(src)

def _segment_sum(src, seg, n):
    return jax.ops.segment_sum(src, seg, n)
kernel_name = 'mk_seq_preln_d4_jaxref_r8_5b3041'

def setup_inputs(seed: int=0):
    np.random.seed(seed)
    _w = jnp.asarray

    def _L0_attn_setup():
        import math
        import jax, jax.numpy as jnp
        import numpy as np
        NUM_HEADS = 32
        NUM_KV_HEADS = 8
        HEAD_DIM = 128
        HIDDEN = 512
        ROPE_THETA = 500000.0
        ROPE_FACTOR = 8.0
        HIGH_FF = 4.0
        LOW_FF = 1.0
        ORIG_MAX_POS = 1024

        def _llama3_inv_freq():
            inv = 1.0 / ROPE_THETA ** (np.arange(0, HEAD_DIM, 2, dtype=np.float32) / HEAD_DIM)
            wavelen = 2.0 * np.pi / inv
            low_wl = ORIG_MAX_POS / LOW_FF
            high_wl = ORIG_MAX_POS / HIGH_FF
            inv_scaled = np.where(wavelen > low_wl, inv / ROPE_FACTOR, inv)
            smooth = (ORIG_MAX_POS / wavelen - LOW_FF) / (HIGH_FF - LOW_FF)
            smoothed = (1.0 - smooth) / ROPE_FACTOR * inv + smooth * inv
            is_medium = (wavelen <= low_wl) & (wavelen >= high_wl)
            return jnp.asarray(np.where(is_medium, smoothed, inv_scaled), dtype=jnp.float32)

        def _rotate_half(x):
            h = x.shape[-1] // 2
            return jnp.concatenate([-x[..., h:], x[..., :h]], axis=-1)
        key = jax.random.key(seed)
        ks = jax.random.split(key, 5)
        s = 0.02
        return {'x': jax.random.normal(ks[0], (1, 256, HIDDEN), dtype=jnp.float32), 'Wq': jax.random.normal(ks[1], (NUM_HEADS * HEAD_DIM, HIDDEN), dtype=jnp.float32) * s, 'Wk': jax.random.normal(ks[2], (NUM_KV_HEADS * HEAD_DIM, HIDDEN), dtype=jnp.float32) * s, 'Wv': jax.random.normal(ks[3], (NUM_KV_HEADS * HEAD_DIM, HIDDEN), dtype=jnp.float32) * s, 'Wo': jax.random.normal(ks[4], (HIDDEN, NUM_HEADS * HEAD_DIM), dtype=jnp.float32) * s}
    _L0_attn_in = _L0_attn_setup()

    def _L0_ffn_setup():
        import jax, jax.numpy as jnp
        import numpy as np
        LORA_SCALE = 16.0 / jnp.sqrt(16.0)
        TOP_K = 2
        key = jax.random.key(seed)
        k1, k2, k3, k4 = jax.random.split(key, 4)
        B_, S, D, O, E, R = (4, 256, 512, 512, 4, 16)
        x = jax.random.normal(k1, (B_, S, D), dtype=jnp.float32)
        router_w = jax.random.normal(k2, (E, D), dtype=jnp.float32) * 0.02
        A = jax.random.normal(k3, (E, R, D), dtype=jnp.float32) * 0.02
        B = jax.random.normal(k4, (O,), dtype=jnp.float32)
        B = jax.random.normal(k4, (E, O, R), dtype=jnp.float32) * 0.02
        return {'x': x, 'router_w': router_w, 'A': A, 'B': B}
    _L0_ffn_in = _L0_ffn_setup()

    def _L1_attn_setup():
        import jax, jax.numpy as jnp
        import numpy as np
        DIM = 512
        N_HEADS = 32
        N_KV_HEADS = 8
        HEAD_DIM = DIM // N_HEADS
        N_REP = N_HEADS // N_KV_HEADS
        THETA = 10000.0
        B, S = (4, 128)

        def _rope_cos_sin(seq_len):
            freqs = 1.0 / THETA ** (jnp.arange(0, HEAD_DIM, 2, dtype=jnp.float32) / HEAD_DIM)
            t = jnp.arange(seq_len, dtype=jnp.float32)
            ang = jnp.outer(t, freqs)
            return (jnp.cos(ang), jnp.sin(ang))

        def _apply_rope(x, cos, sin):
            xr = x[..., 0::2]
            xi = x[..., 1::2]
            c = cos[None, :, None, :]
            s = sin[None, :, None, :]
            out_r = xr * c - xi * s
            out_i = xr * s + xi * c
            return jnp.stack([out_r, out_i], axis=-1).reshape(x.shape)
        key = jax.random.key(seed)
        ks = jax.random.split(key, 5)
        sc = 1.0 / np.sqrt(DIM).astype(np.float32)
        x = jax.random.normal(ks[0], (B, S, DIM), jnp.float32)
        wq = jax.random.normal(ks[1], (DIM, N_HEADS * HEAD_DIM), jnp.float32) * sc
        wk = jax.random.normal(ks[2], (DIM, N_KV_HEADS * HEAD_DIM), jnp.float32) * sc
        wv = jax.random.normal(ks[3], (DIM, N_KV_HEADS * HEAD_DIM), jnp.float32) * sc
        wo = jax.random.normal(ks[4], (N_HEADS * HEAD_DIM, DIM), jnp.float32) * sc
        return {'x': x, 'wq': wq, 'wk': wk, 'wv': wv, 'wo': wo}
    _L1_attn_in = _L1_attn_setup()

    def _L1_ffn_setup():
        import jax, jax.numpy as jnp
        import numpy as np
        B, S, IN, OUT = (4, 256, 512, 512)
        E, K, R = (8, 2, 16)
        CAP_FACTOR = 3.0
        ALPHA = 1.0 / R
        LN_EPS = 1e-05
        key = jax.random.key(seed)
        ks = jax.random.split(key, 6)
        return {'x': jax.random.normal(ks[0], (B, S, IN), dtype=jnp.float32), 'weight': jax.random.normal(ks[1], (OUT, IN), dtype=jnp.float32) * 0.02, 'lora_A': jax.random.normal(ks[2], (E, IN, R), dtype=jnp.float32) / np.sqrt(R), 'lora_B': jax.random.normal(ks[3], (E, R, OUT), dtype=jnp.float32) * 0.02, 'gw1': jax.random.normal(ks[4], (4 * E, IN), dtype=jnp.float32) * 0.02, 'gb1': jnp.zeros((4 * E,), dtype=jnp.float32), 'ln_gamma': jnp.ones((4 * E,), dtype=jnp.float32), 'ln_beta': jnp.zeros((4 * E,), dtype=jnp.float32), 'gw2': jax.random.normal(ks[5], (E, 4 * E), dtype=jnp.float32) * 0.02, 'gb2': jnp.zeros((E,), dtype=jnp.float32)}
    _L1_ffn_in = _L1_ffn_setup()

    def _L2_attn_setup():
        import jax, jax.numpy as jnp
        import numpy as np
        HIDDEN = 512
        N_HEADS = 32
        N_KV_HEADS = 8
        HEAD_DIM = HIDDEN // N_HEADS
        ROPE_THETA = 10000.0
        B, S = (1, 256)

        def _rotate_half(x):
            x1, x2 = jnp.split(x, 2, axis=-1)
            return jnp.concatenate([-x2, x1], axis=-1)

        def _rope_cos_sin(seq_len, dtype):
            inv_freq = 1.0 / ROPE_THETA ** (jnp.arange(0, HEAD_DIM, 2, dtype=jnp.float32) / HEAD_DIM)
            pos = jnp.arange(seq_len, dtype=jnp.float32)
            freqs = pos[:, None] * inv_freq[None, :]
            emb = jnp.concatenate([freqs, freqs], axis=-1)
            return (jnp.cos(emb).astype(dtype), jnp.sin(emb).astype(dtype))
        key = jax.random.key(seed)
        k1, k2, k3, k4, k5 = jax.random.split(key, 5)
        scale = 1.0 / np.sqrt(HIDDEN)
        return {'hidden_states': jax.random.normal(k1, (B, S, HIDDEN), dtype=jnp.float32), 'wq': jax.random.normal(k2, (HIDDEN, HIDDEN), dtype=jnp.float32) * scale, 'wk': jax.random.normal(k3, (N_KV_HEADS * HEAD_DIM, HIDDEN), dtype=jnp.float32) * scale, 'wv': jax.random.normal(k4, (N_KV_HEADS * HEAD_DIM, HIDDEN), dtype=jnp.float32) * scale, 'wo': jax.random.normal(k5, (HIDDEN, HIDDEN), dtype=jnp.float32) * scale}
    _L2_attn_in = _L2_attn_setup()

    def _L2_ffn_setup():
        import jax, jax.numpy as jnp
        import numpy as np
        DIM = 512
        HID = 1376
        R = 16
        SCALING = 32.0 / 16.0

        def _lora_linear(x, w, a, b):
            base = jnp.einsum('bsd,od->bso', x, w)
            low = jnp.einsum('bsr,or->bso', jnp.einsum('bsd,rd->bsr', x, a), b)
            return base + low * SCALING
        key = jax.random.key(seed)
        ks = jax.random.split(key, 10)
        s_in = 1.0 / np.sqrt(DIM)
        s_hid = 1.0 / np.sqrt(HID)
        return {'x': jax.random.normal(ks[0], (4, 256, DIM), jnp.float32), 'w1': jax.random.normal(ks[1], (HID, DIM), jnp.float32) * s_in, 'w3': jax.random.normal(ks[2], (HID, DIM), jnp.float32) * s_in, 'w2': jax.random.normal(ks[3], (DIM, HID), jnp.float32) * s_hid, 'lora_A1': jax.random.normal(ks[4], (R, DIM), jnp.float32) * s_in, 'lora_B1': jax.random.normal(ks[5], (HID, R), jnp.float32) * 0.02, 'lora_A3': jax.random.normal(ks[6], (R, DIM), jnp.float32) * s_in, 'lora_B3': jax.random.normal(ks[7], (HID, R), jnp.float32) * 0.02, 'lora_A2': jax.random.normal(ks[8], (R, HID), jnp.float32) * s_hid, 'lora_B2': jax.random.normal(ks[9], (DIM, R), jnp.float32) * 0.02}
    _L2_ffn_in = _L2_ffn_setup()

    def _L3_attn_setup():
        import jax, jax.numpy as jnp
        import numpy as np
        N_HEADS = 32
        N_KV_HEADS = 16
        N_EMBD = 512
        HEAD_DIM = N_EMBD // N_HEADS
        GROUPS = N_HEADS // N_KV_HEADS
        KV_DIM = N_KV_HEADS * HEAD_DIM
        SCALE = 1.0 / np.sqrt(np.float32(N_HEADS))
        key = jax.random.key(seed)
        ks = jax.random.split(key, 4)
        B, T, C = (1, 256, N_EMBD)
        s = 1.0 / np.sqrt(np.float32(C))
        return {'x': jax.random.normal(ks[0], (B, T, C), dtype=jnp.float32), 'Wq': jax.random.normal(ks[1], (C, C), dtype=jnp.float32) * s, 'bq': jnp.zeros((C,), dtype=jnp.float32), 'Wk': jax.random.normal(ks[2], (KV_DIM, C), dtype=jnp.float32) * s, 'bk': jnp.zeros((KV_DIM,), dtype=jnp.float32), 'Wv': jax.random.normal(ks[3], (KV_DIM, C), dtype=jnp.float32) * s, 'bv': jnp.zeros((KV_DIM,), dtype=jnp.float32)}
    _L3_attn_in = _L3_attn_setup()

    def _L3_ffn_setup():
        import jax, jax.numpy as jnp
        import numpy as np
        HID, INT, LAT, NE, K = (512, 1024, 256, 8, 2)
        LN_EPS = 1e-05

        def _layernorm(x, gamma, beta):
            mu = jnp.mean(x, axis=-1, keepdims=True)
            var = jnp.var(x, axis=-1, keepdims=True)
            return (x - mu) * jax.lax.rsqrt(var + LN_EPS) * gamma + beta
        key = jax.random.key(seed)
        ks = jax.random.split(key, 8)
        s = lambda d: 1.0 / np.sqrt(d)
        return {'hidden_states': jax.random.normal(ks[0], (4, 256, HID), jnp.float32), 'gate_w': jax.random.normal(ks[1], (HID, NE), jnp.float32) * s(HID), 'up_w': jax.random.normal(ks[2], (HID, INT), jnp.float32) * s(HID), 'down_w': jax.random.normal(ks[3], (INT, HID), jnp.float32) * s(INT), 'fc1_w': jax.random.normal(ks[4], (HID, LAT), jnp.float32) * s(HID), 'fc2_w': jax.random.normal(ks[5], (LAT, HID), jnp.float32) * s(LAT), 'expert_w': jax.random.normal(ks[6], (LAT, LAT), jnp.float32), 'ln_gamma': jnp.ones((HID,), jnp.float32), 'ln_beta': jnp.zeros((HID,), jnp.float32)}
    _L3_ffn_in = _L3_ffn_setup()
    _d = {'L0_attn_x': _L0_attn_in['x'], 'L0_attn_Wq': _L0_attn_in['Wq'], 'L0_attn_Wk': _L0_attn_in['Wk'], 'L0_attn_Wv': _L0_attn_in['Wv'], 'L0_attn_Wo': _L0_attn_in['Wo'], 'L0_ffn_router_w': _L0_ffn_in['router_w'], 'L0_ffn_A': _L0_ffn_in['A'], 'L0_ffn_B': _L0_ffn_in['B'], 'L1_attn_wq': _L1_attn_in['wq'], 'L1_attn_wk': _L1_attn_in['wk'], 'L1_attn_wv': _L1_attn_in['wv'], 'L1_attn_wo': _L1_attn_in['wo'], 'L1_ffn_weight': _L1_ffn_in['weight'], 'L1_ffn_lora_A': _L1_ffn_in['lora_A'], 'L1_ffn_lora_B': _L1_ffn_in['lora_B'], 'L1_ffn_gw1': _L1_ffn_in['gw1'], 'L1_ffn_gb1': _L1_ffn_in['gb1'], 'L1_ffn_ln_gamma': _L1_ffn_in['ln_gamma'], 'L1_ffn_ln_beta': _L1_ffn_in['ln_beta'], 'L1_ffn_gw2': _L1_ffn_in['gw2'], 'L1_ffn_gb2': _L1_ffn_in['gb2'], 'L2_attn_wq': _L2_attn_in['wq'], 'L2_attn_wk': _L2_attn_in['wk'], 'L2_attn_wv': _L2_attn_in['wv'], 'L2_attn_wo': _L2_attn_in['wo'], 'L2_ffn_w1': _L2_ffn_in['w1'], 'L2_ffn_w3': _L2_ffn_in['w3'], 'L2_ffn_w2': _L2_ffn_in['w2'], 'L2_ffn_lora_A1': _L2_ffn_in['lora_A1'], 'L2_ffn_lora_B1': _L2_ffn_in['lora_B1'], 'L2_ffn_lora_A3': _L2_ffn_in['lora_A3'], 'L2_ffn_lora_B3': _L2_ffn_in['lora_B3'], 'L2_ffn_lora_A2': _L2_ffn_in['lora_A2'], 'L2_ffn_lora_B2': _L2_ffn_in['lora_B2'], 'L3_attn_Wq': _L3_attn_in['Wq'], 'L3_attn_bq': _L3_attn_in['bq'], 'L3_attn_Wk': _L3_attn_in['Wk'], 'L3_attn_bk': _L3_attn_in['bk'], 'L3_attn_Wv': _L3_attn_in['Wv'], 'L3_attn_bv': _L3_attn_in['bv'], 'L3_ffn_gate_w': _L3_ffn_in['gate_w'], 'L3_ffn_up_w': _L3_ffn_in['up_w'], 'L3_ffn_down_w': _L3_ffn_in['down_w'], 'L3_ffn_fc1_w': _L3_ffn_in['fc1_w'], 'L3_ffn_fc2_w': _L3_ffn_in['fc2_w'], 'L3_ffn_expert_w': _L3_ffn_in['expert_w'], 'L3_ffn_ln_gamma': _L3_ffn_in['ln_gamma'], 'L3_ffn_ln_beta': _L3_ffn_in['ln_beta']}
    _x0 = _d['L0_attn_x']
    _d['L0_attn_x'] = jax.random.normal(jax.random.fold_in(jax.random.key(seed), 1), (4, 256, 512), dtype=_x0.dtype)
    del _x0
    return _d

def reference(L0_attn_x, L0_attn_Wq, L0_attn_Wk, L0_attn_Wv, L0_attn_Wo, L0_ffn_router_w, L0_ffn_A, L0_ffn_B, L1_attn_wq, L1_attn_wk, L1_attn_wv, L1_attn_wo, L1_ffn_weight, L1_ffn_lora_A, L1_ffn_lora_B, L1_ffn_gw1, L1_ffn_gb1, L1_ffn_ln_gamma, L1_ffn_ln_beta, L1_ffn_gw2, L1_ffn_gb2, L2_attn_wq, L2_attn_wk, L2_attn_wv, L2_attn_wo, L2_ffn_w1, L2_ffn_w3, L2_ffn_w2, L2_ffn_lora_A1, L2_ffn_lora_B1, L2_ffn_lora_A3, L2_ffn_lora_B3, L2_ffn_lora_A2, L2_ffn_lora_B2, L3_attn_Wq, L3_attn_bq, L3_attn_Wk, L3_attn_bk, L3_attn_Wv, L3_attn_bv, L3_ffn_gate_w, L3_ffn_up_w, L3_ffn_down_w, L3_ffn_fc1_w, L3_ffn_fc2_w, L3_ffn_expert_w, L3_ffn_ln_gamma, L3_ffn_ln_beta):

    def _L0_attn_ref(x, Wq, Wk, Wv, Wo):
        import math
        import jax, jax.numpy as jnp
        import numpy as np
        NUM_HEADS = 32
        NUM_KV_HEADS = 8
        HEAD_DIM = 128
        HIDDEN = 512
        ROPE_THETA = 500000.0
        ROPE_FACTOR = 8.0
        HIGH_FF = 4.0
        LOW_FF = 1.0
        ORIG_MAX_POS = 1024

        def _llama3_inv_freq():
            inv = 1.0 / ROPE_THETA ** (np.arange(0, HEAD_DIM, 2, dtype=np.float32) / HEAD_DIM)
            wavelen = 2.0 * np.pi / inv
            low_wl = ORIG_MAX_POS / LOW_FF
            high_wl = ORIG_MAX_POS / HIGH_FF
            inv_scaled = np.where(wavelen > low_wl, inv / ROPE_FACTOR, inv)
            smooth = (ORIG_MAX_POS / wavelen - LOW_FF) / (HIGH_FF - LOW_FF)
            smoothed = (1.0 - smooth) / ROPE_FACTOR * inv + smooth * inv
            is_medium = (wavelen <= low_wl) & (wavelen >= high_wl)
            return jnp.asarray(np.where(is_medium, smoothed, inv_scaled), dtype=jnp.float32)

        def _rotate_half(x):
            h = x.shape[-1] // 2
            return jnp.concatenate([-x[..., h:], x[..., :h]], axis=-1)
        B, T, _ = x.shape
        G = NUM_HEADS // NUM_KV_HEADS
        q = jnp.einsum('bth,oh->bto', x, Wq).reshape(B, T, NUM_HEADS, HEAD_DIM).transpose(0, 2, 1, 3)
        k = jnp.einsum('bth,oh->bto', x, Wk).reshape(B, T, NUM_KV_HEADS, HEAD_DIM).transpose(0, 2, 1, 3)
        v = jnp.einsum('bth,oh->bto', x, Wv).reshape(B, T, NUM_KV_HEADS, HEAD_DIM).transpose(0, 2, 1, 3)
        inv_freq = _llama3_inv_freq()
        pos = jnp.arange(T, dtype=jnp.float32)
        freqs = pos[:, None] * inv_freq[None, :]
        emb = jnp.concatenate([freqs, freqs], axis=-1)
        cos, sin = (jnp.cos(emb), jnp.sin(emb))
        q = q * cos + _rotate_half(q) * sin
        k = k * cos + _rotate_half(k) * sin
        qg = q.reshape(B, NUM_KV_HEADS, G, T, HEAD_DIM)
        scale = 1.0 / math.sqrt(HEAD_DIM)
        scores = jnp.einsum('bkgtd,bksd->bkgts', qg, k) * scale
        causal = jnp.tril(jnp.ones((T, T), dtype=bool))
        scores = jnp.where(causal, scores, -jnp.inf)
        attn = jax.nn.softmax(scores, axis=-1)
        out = jnp.einsum('bkgts,bksd->bkgtd', attn, v)
        out = out.reshape(B, NUM_HEADS, T, HEAD_DIM).transpose(0, 2, 1, 3).reshape(B, T, NUM_HEADS * HEAD_DIM)
        return jnp.einsum('bto,ho->bth', out, Wo)

    def _L0_ffn_ref(x, router_w, A, B):
        import jax, jax.numpy as jnp
        import numpy as np
        LORA_SCALE = 16.0 / jnp.sqrt(16.0)
        TOP_K = 2
        D = x.shape[-1]
        flat = x.reshape(-1, D)
        logits = flat @ router_w.T
        topk_vals, topk_idx = jax.lax.top_k(logits, TOP_K)
        sparse = jnp.full_like(logits, -jnp.inf)
        rows = jnp.arange(logits.shape[0])[:, None]
        sparse = sparse.at[rows, topk_idx].set(topk_vals)
        gates = jax.nn.softmax(sparse, axis=-1)
        mid = jnp.einsum('tf,erf->ter', flat, A)
        all_deltas = jnp.einsum('ter,eor->teo', mid, B) * LORA_SCALE
        delta = jnp.einsum('te,teo->to', gates, all_deltas)
        return delta.reshape(*x.shape[:-1], -1)

    def _L1_attn_ref(x, wq, wk, wv, wo):
        import jax, jax.numpy as jnp
        import numpy as np
        DIM = 512
        N_HEADS = 32
        N_KV_HEADS = 8
        HEAD_DIM = DIM // N_HEADS
        N_REP = N_HEADS // N_KV_HEADS
        THETA = 10000.0
        B, S = (4, 128)

        def _rope_cos_sin(seq_len):
            freqs = 1.0 / THETA ** (jnp.arange(0, HEAD_DIM, 2, dtype=jnp.float32) / HEAD_DIM)
            t = jnp.arange(seq_len, dtype=jnp.float32)
            ang = jnp.outer(t, freqs)
            return (jnp.cos(ang), jnp.sin(ang))

        def _apply_rope(x, cos, sin):
            xr = x[..., 0::2]
            xi = x[..., 1::2]
            c = cos[None, :, None, :]
            s = sin[None, :, None, :]
            out_r = xr * c - xi * s
            out_i = xr * s + xi * c
            return jnp.stack([out_r, out_i], axis=-1).reshape(x.shape)
        bsz, seq_len, _ = x.shape
        q = (x @ wq).reshape(bsz, seq_len, N_HEADS, HEAD_DIM)
        k = (x @ wk).reshape(bsz, seq_len, N_KV_HEADS, HEAD_DIM)
        v = (x @ wv).reshape(bsz, seq_len, N_KV_HEADS, HEAD_DIM)
        cos, sin = _rope_cos_sin(seq_len)
        q = _apply_rope(q, cos, sin)
        k = _apply_rope(k, cos, sin)
        k = jnp.repeat(k, N_REP, axis=2)
        v = jnp.repeat(v, N_REP, axis=2)
        scores = jnp.einsum('bqhd,bkhd->bhqk', q, k) / np.float32(np.sqrt(HEAD_DIM))
        mask = jnp.triu(jnp.full((seq_len, seq_len), -jnp.inf, dtype=scores.dtype), k=1)
        scores = scores + mask
        attn = jax.nn.softmax(scores.astype(jnp.float32), axis=-1).astype(q.dtype)
        out = jnp.einsum('bhqk,bkhd->bqhd', attn, v).reshape(bsz, seq_len, N_HEADS * HEAD_DIM)
        return out @ wo

    def _L1_ffn_ref(x, weight, lora_A, lora_B, gw1, gb1, ln_gamma, ln_beta, gw2, gb2):
        import jax, jax.numpy as jnp
        import numpy as np
        B, S, IN, OUT = (4, 256, 512, 512)
        E, K, R = (8, 2, 16)
        CAP_FACTOR = 3.0
        ALPHA = 1.0 / R
        LN_EPS = 1e-05
        orig_shape = x.shape
        xf = x.reshape(-1, orig_shape[-1])
        N = xf.shape[0]
        capacity = int(CAP_FACTOR * N / E)
        h = xf @ gw1.T + gb1
        mu = jnp.mean(h, axis=-1, keepdims=True)
        var = jnp.mean((h - mu) ** 2, axis=-1, keepdims=True)
        h = (h - mu) * jax.lax.rsqrt(var + LN_EPS) * ln_gamma + ln_beta
        h = jax.nn.relu(h)
        gates = h @ gw2.T + gb2
        top_v, top_i = jax.lax.top_k(gates, K)
        top_g = jax.nn.softmax(top_v, axis=-1)
        onehot = (top_i[..., None] == jnp.arange(E)).astype(xf.dtype)
        counts = onehot.sum(axis=0)
        allowed = (counts <= capacity).astype(xf.dtype)
        w = jnp.einsum('nke,nk,ke->ne', onehot, top_g, allowed)
        main = xf @ weight.T
        tmp = jnp.einsum('ni,eir->enr', xf, lora_A)
        tmp = tmp * w.T[:, :, None]
        lora = jnp.einsum('enr,ero->no', tmp, lora_B) * ALPHA
        out = main + lora
        return out.reshape(*orig_shape[:-1], weight.shape[0])

    def _L2_attn_ref(hidden_states, wq, wk, wv, wo):
        import jax, jax.numpy as jnp
        import numpy as np
        HIDDEN = 512
        N_HEADS = 32
        N_KV_HEADS = 8
        HEAD_DIM = HIDDEN // N_HEADS
        ROPE_THETA = 10000.0
        B, S = (1, 256)

        def _rotate_half(x):
            x1, x2 = jnp.split(x, 2, axis=-1)
            return jnp.concatenate([-x2, x1], axis=-1)

        def _rope_cos_sin(seq_len, dtype):
            inv_freq = 1.0 / ROPE_THETA ** (jnp.arange(0, HEAD_DIM, 2, dtype=jnp.float32) / HEAD_DIM)
            pos = jnp.arange(seq_len, dtype=jnp.float32)
            freqs = pos[:, None] * inv_freq[None, :]
            emb = jnp.concatenate([freqs, freqs], axis=-1)
            return (jnp.cos(emb).astype(dtype), jnp.sin(emb).astype(dtype))
        bsz, q_len, _ = hidden_states.shape
        q = hidden_states @ wq.T
        k = hidden_states @ wk.T
        v = hidden_states @ wv.T
        q = q.reshape(bsz, q_len, N_HEADS, HEAD_DIM).transpose(0, 2, 1, 3)
        k = k.reshape(bsz, q_len, N_KV_HEADS, HEAD_DIM).transpose(0, 2, 1, 3)
        v = v.reshape(bsz, q_len, N_KV_HEADS, HEAD_DIM).transpose(0, 2, 1, 3)
        cos, sin = _rope_cos_sin(q_len, hidden_states.dtype)
        cos = cos[None, None]
        sin = sin[None, None]
        q = q * cos + _rotate_half(q) * sin
        k = k * cos + _rotate_half(k) * sin
        groups = N_HEADS // N_KV_HEADS
        k = jnp.repeat(k, groups, axis=1)
        v = jnp.repeat(v, groups, axis=1)
        scale = 1.0 / np.sqrt(HEAD_DIM)
        attn = jnp.einsum('bhqd,bhkd->bhqk', q, k) * scale
        causal = jnp.triu(jnp.full((q_len, q_len), jnp.finfo(jnp.float32).min, dtype=jnp.float32), k=1)
        attn = attn + causal[None, None]
        attn = jax.nn.softmax(attn.astype(jnp.float32), axis=-1).astype(q.dtype)
        out = jnp.einsum('bhqk,bhkd->bhqd', attn, v)
        out = out.transpose(0, 2, 1, 3).reshape(bsz, q_len, HIDDEN)
        return out @ wo.T

    def _L2_ffn_ref(x, w1, w3, w2, lora_A1, lora_B1, lora_A3, lora_B3, lora_A2, lora_B2):
        import jax, jax.numpy as jnp
        import numpy as np
        DIM = 512
        HID = 1376
        R = 16
        SCALING = 32.0 / 16.0

        def _lora_linear(x, w, a, b):
            base = jnp.einsum('bsd,od->bso', x, w)
            low = jnp.einsum('bsr,or->bso', jnp.einsum('bsd,rd->bsr', x, a), b)
            return base + low * SCALING
        h1 = _lora_linear(x, w1, lora_A1, lora_B1)
        h3 = _lora_linear(x, w3, lora_A3, lora_B3)
        g = jax.nn.silu(h1) * h3
        return _lora_linear(g, w2, lora_A2, lora_B2)

    def _L3_attn_ref(x, Wq, bq, Wk, bk, Wv, bv):
        import jax, jax.numpy as jnp
        import numpy as np
        N_HEADS = 32
        N_KV_HEADS = 16
        N_EMBD = 512
        HEAD_DIM = N_EMBD // N_HEADS
        GROUPS = N_HEADS // N_KV_HEADS
        KV_DIM = N_KV_HEADS * HEAD_DIM
        SCALE = 1.0 / np.sqrt(np.float32(N_HEADS))
        B, T, C = x.shape
        q = (x @ Wq.T + bq).reshape(B, T, N_HEADS, HEAD_DIM)
        k = (x @ Wk.T + bk).reshape(B, T, N_KV_HEADS, HEAD_DIM)
        v = (x @ Wv.T + bv).reshape(B, T, N_KV_HEADS, HEAD_DIM)
        q = q.transpose(0, 2, 1, 3).reshape(B, GROUPS, N_KV_HEADS, T, HEAD_DIM)
        k = k.transpose(0, 2, 1, 3)
        v = v.transpose(0, 2, 1, 3)
        scores = jnp.einsum('bgkqd,bkld->bgkql', q, k) * SCALE
        causal = jnp.tril(jnp.ones((T, T), dtype=bool))
        scores = jnp.where(causal, scores, jnp.float32(-jnp.inf))
        w = jax.nn.softmax(scores, axis=-1)
        out = jnp.einsum('bgkql,bkld->bgkqd', w, v)
        out = out.reshape(B, N_HEADS, T, HEAD_DIM).transpose(0, 2, 1, 3).reshape(B, T, C)
        return out

    def _L3_ffn_ref(hidden_states, gate_w, up_w, down_w, fc1_w, fc2_w, expert_w, ln_gamma, ln_beta):
        import jax, jax.numpy as jnp
        import numpy as np
        HID, INT, LAT, NE, K = (512, 1024, 256, 8, 2)
        LN_EPS = 1e-05

        def _layernorm(x, gamma, beta):
            mu = jnp.mean(x, axis=-1, keepdims=True)
            var = jnp.var(x, axis=-1, keepdims=True)
            return (x - mu) * jax.lax.rsqrt(var + LN_EPS) * gamma + beta
        logits = jnp.einsum('bsh,he->bse', hidden_states, gate_w)
        routing_weights, selected_experts = jax.lax.top_k(logits, K)
        h = jax.nn.relu(jnp.einsum('bsh,hi->bsi', hidden_states, up_w)) ** 2
        shared_out = jnp.einsum('bsi,ih->bsh', h, down_w)
        x_latent = jnp.einsum('bsh,hl->bsl', hidden_states, fc1_w)
        expert_out = jnp.einsum('bsl,lm->bsm', x_latent, expert_w)
        moe_out = expert_out * jnp.sum(routing_weights, axis=-1, keepdims=True)
        routed_out = jnp.einsum('bsl,lh->bsh', moe_out, fc2_w)
        return _layernorm(shared_out + routed_out, ln_gamma, ln_beta)
    x = L0_attn_x
    x = x + _L0_attn_ref(_layernorm(x, axis=-1), L0_attn_Wq, L0_attn_Wk, L0_attn_Wv, L0_attn_Wo)
    x = x + _L0_ffn_ref(_layernorm(x, axis=-1), L0_ffn_router_w, L0_ffn_A, L0_ffn_B)
    x = x + _L1_attn_ref(_layernorm(x, axis=-1), L1_attn_wq, L1_attn_wk, L1_attn_wv, L1_attn_wo)
    x = x + _L1_ffn_ref(_layernorm(x, axis=-1), L1_ffn_weight, L1_ffn_lora_A, L1_ffn_lora_B, L1_ffn_gw1, L1_ffn_gb1, L1_ffn_ln_gamma, L1_ffn_ln_beta, L1_ffn_gw2, L1_ffn_gb2)
    x = x + _L2_attn_ref(_layernorm(x, axis=-1), L2_attn_wq, L2_attn_wk, L2_attn_wv, L2_attn_wo)
    x = x + _L2_ffn_ref(_layernorm(x, axis=-1), L2_ffn_w1, L2_ffn_w3, L2_ffn_w2, L2_ffn_lora_A1, L2_ffn_lora_B1, L2_ffn_lora_A3, L2_ffn_lora_B3, L2_ffn_lora_A2, L2_ffn_lora_B2)
    x = x + _L3_attn_ref(_layernorm(x, axis=-1), L3_attn_Wq, L3_attn_bq, L3_attn_Wk, L3_attn_bk, L3_attn_Wv, L3_attn_bv)
    x = x + _L3_ffn_ref(_layernorm(x, axis=-1), L3_ffn_gate_w, L3_ffn_up_w, L3_ffn_down_w, L3_ffn_fc1_w, L3_ffn_fc2_w, L3_ffn_expert_w, L3_ffn_ln_gamma, L3_ffn_ln_beta)
    return x

_drawn_inputs = setup_inputs


def setup_inputs(seed=0):
    import zlib

    import numpy as np

    out = dict(_drawn_inputs(seed))
    spreads = {'L1_ffn_gb1': (0.0, 0.8),
     'L1_ffn_ln_gamma': (1.0, 0.6),
     'L1_ffn_ln_beta': (0.0, 0.8),
     'L1_ffn_gb2': (0.0, 0.38),
     'L3_attn_bq': (0.0, 0.8),
     'L3_attn_bk': (0.0, 0.8),
     'L3_attn_bv': (0.0, 0.1),
     'L3_ffn_ln_gamma': (1.0, 0.2),
     'L3_ffn_ln_beta': (0.0, 0.1)}
    factors = {'L1_ffn_lora_A': 3.906, 'L1_ffn_lora_B': 4.099, 'L1_ffn_gw1': 4.558, 'L1_ffn_gw2': 4.093}
    for name, (base, spread) in spreads.items():
        noise = np.random.default_rng([zlib.crc32(name.encode()), seed]).standard_normal(out[name].shape)
        drawn = base * np.exp(spread * noise) if base else spread * noise
        out[name] = jnp.asarray(drawn.astype(out[name].dtype))
    for name, factor in factors.items():
        out[name] = (out[name] * factor).astype(out[name].dtype)
    return out
```

```python
from contextlib import ExitStack

import concourse.bass as bass
from concourse import mybir

F32 = mybir.dt.float32
BF16 = mybir.dt.bfloat16
ALU = mybir.AluOpType
ACT = mybir.ActivationFunctionType
AX = mybir.AxisListType

BATCH, SEQ, DIM = 4, 256, 512
P = 128
KC = DIM // P
QT = SEQ // P
TILES = BATCH * QT
EPS = 1e-5
MASKED = -1.0e30

H0, G0, D0 = 32, 8, 128
R0 = H0 // G0
SCALE0 = 1.0 / float(D0) ** 0.5
PROJ0 = G0 * (R0 + 1)

HEADS, HD = 32, 16
KV_HEADS = (8, 8, 16)
SCALES = (0.25, 0.25, 1.0 / 32.0 ** 0.5)
STACK = 6 * HD
UNITS = HEADS // 4
VPAD = 32

E0, RANK = 4, 16
E1 = 8
CAPACITY = int(3.0 * TILES * P / E1)
HID2 = 1376
HC2 = (HID2 + P - 1) // P
HLAST2 = HID2 - (HC2 - 1) * P
INT3, LAT3, E3 = 1024, 256, 8
IC3, LC3 = INT3 // P, LAT3 // P


class Chain:

    def __init__(self, eng, sem, per_turn, before=0):
        self.eng, self.sem, self.per, self.before, self.k = eng, sem, per_turn, before, 0

    def start(self, turn):
        self.turn, self.k = turn, 0

    def link(self, ins):
        self.k += 1
        ins.then_inc(self.sem, 1)
        self.eng.wait_ge(self.sem, self.turn * self.per + (self.before + self.k))

    def end(self):
        assert self.k == self.per, (self.k, self.per)


def four_layers(nc, dram, out):
    with ExitStack() as stack:
        def sem(name):
            return stack.enter_context(nc.semaphore(name))

        def keep(name, shape, dtype=F32):
            return stack.enter_context(nc.sbuf_tensor(name, shape, dtype))

        def words(t):
            return t[...].bitcast(mybir.dt.uint16) if t.dtype == BF16 else t[...]

        x = keep("x", [P, TILES, DIM])
        ident = keep("ident", [P, P])
        ident_bf = keep("ident_bf", [P, P], BF16)
        masks = keep("masks", [P, 2, P], BF16)
        stats = keep("stats", [P, QT, 6])
        mean_var = keep("mean_var", [P, QT, 2])
        rstd = keep("rstd", [P, QT, 1])
        minus_half = keep("minus_half", [P, 1])
        eps = keep("eps", [P, 1])

        base = (nc.sbuf_base + 63) // 64 * 64
        top = [base]

        def place(name, shape, dtype=F32, at=None):
            size = 1
            for s in shape[1:]:
                size *= s
            size = (size * (4 if dtype == F32 else 2) + 63) // 64 * 64
            if at is None:
                at = top[0]
                top[0] += size
            return nc.alloc_sbuf_tensor_at(name, shape, dtype, offset=at), at + size

        ps = stack.enter_context(nc.psum_tensor("ps", [P, 8, 512], F32))
        ps_bf = ps[:, :, :].bitcast(BF16)

        consts_in = sem("consts_in")
        x_in = sem("x_in")
        norm_chain = sem("norm_chain")
        normed = sem("normed")
        rstd_ready = sem("rstd_ready")
        var_ready = sem("var_ready")
        pool_norm_chain = sem("pool_norm_chain")
        flipped = sem("flipped")
        xT_ready = sem("xT_ready")
        residual = sem("residual")
        half_ready = sem("half_ready")

        def norm_vector(dve, sub, b, xn):
            turn = sub * BATCH + b
            for i in range(QT):
                if sub == 0:
                    dve.wait_ge(x_in, 16 * TILES)
                else:
                    dve.wait_ge(residual, (sub * BATCH) * QT)
                tile = x[:, bass.ds(b * QT + i, 1), :].rearrange("p a d -> p (a d)")
                nc.vector.bn_stats(stats[:, i, :], tile).then_inc(norm_chain, 1)
                dve.drain()
                nc.vector.bn_aggr(mean_var[:, i, :], stats[:, i, :]).then_inc(var_ready, 1)
            for i in range(QT):
                tile = x[:, bass.ds(b * QT + i, 1), :].rearrange("p a d -> p (a d)")
                dve.wait_ge(rstd_ready, turn * QT + (i + 1))
                nc.vector.tensor_scalar(xn[:, i, :], tile, mean_var[:, i, 0:1], rstd[:, i, :],
                                        ALU.subtract, ALU.mult).then_inc(normed, 1)

        def norm_gpsimd(pool, sub, b):
            turn = sub * BATCH + b
            for i in range(QT):
                pool.wait_ge(var_ready, turn * QT + (i + 1))
                nc.gpsimd.tensor_tensor(rstd[:, i, :], mean_var[:, i, 1:2], eps[:, :], ALU.add).then_inc(pool_norm_chain, 1)
                pool.wait_ge(pool_norm_chain, turn * QT + (i + 1))
                nc.gpsimd.tensor_tensor(rstd[:, i, :], rstd[:, i, :], minus_half[:, :], ALU.pow).then_inc(rstd_ready, 1)

        def norm_tensor(pe, sub, b, xn):
            turn = sub * BATCH + b
            for i in range(QT):
                pe.wait_ge(normed, turn * QT + (i + 1))
                for k in range(KC):
                    last = nc.tensor.transpose(ps[:, i, k * P:(k + 1) * P], xn[:, i, k * P:(k + 1) * P], ident[:, :])
                last.then_inc(flipped, 1)

        def norm_scalar(act, sub, b, xT):
            turn = sub * BATCH + b
            for i in range(QT):
                act.wait_ge(flipped, turn * QT + (i + 1))
                nc.scalar.activation(xT[:, :, i * P:(i + 1) * P], ps[:, i, :].rearrange("p (k t) -> p k t", k=KC),
                                     ACT.Copy).then_inc(xT_ready, 1)

        def layer0_attention():
            top[0] = base
            wq, _ = place("l0_wq", [P, G0, KC, R0 * D0])
            wk, _ = place("l0_wk", [P, KC, G0 * D0])
            wv, _ = place("l0_wv", [P, KC, G0 * D0])
            wo, _ = place("l0_wo", [P, H0, DIM])
            cos, _ = place("l0_cos", [P, SEQ])
            sin, _ = place("l0_sin", [P, SEQ])
            xT, _ = place("l0_xT", [P, KC, SEQ])
            val, _ = place("l0_val", [P, QT, G0 * D0])
            qT, _ = place("l0_qT", [P, R0, SEQ])
            kT, _ = place("l0_kT", [P, 2, SEQ])
            t_sin, _ = place("l0_t_sin", [P, 2, SEQ])
            oT, _ = place("l0_oT", [P, 2, SEQ])
            rowmax, _ = place("l0_rowmax", [P, 2, QT])
            rowsum, _ = place("l0_rowsum", [P, 2, QT])
            share = top[0]
            prob, _ = place("l0_prob", [P, 2, 3 * P])
            probT, _ = place("l0_probT", [P, 2, 3 * P])
            xn, _ = place("l0_xn", [P, QT, DIM], at=share)

            wq_in = [sem(f"l0_wq_in{g}") for g in range(G0)]
            wk_in = sem("l0_wk_in")
            wv_in = sem("l0_wv_in")
            wo_in = [sem(f"l0_wo_in{g}") for g in range(G0)]
            v_done = sem("l0_v_done")
            v_kept = sem("l0_v_kept")
            projected = sem("l0_projected")
            rope_muled = sem("l0_rope_muled")
            roped = sem("l0_roped")
            scored = sem("l0_scored")
            max_chain = sem("l0_max_chain")
            max_ready = sem("l0_max_ready")
            exped = sem("l0_exped")
            sum_inverted = sem("l0_sum_inverted")
            scaled = sem("l0_scaled")
            prob_flipped = sem("l0_prob_flipped")
            probT_ready = sem("l0_probT_ready")
            attended = sem("l0_attended")
            oT_ready = sem("l0_oT_ready")
            out_used = sem("l0_out_used")

            PROJ, SCORE, FLIP, OUT, ACC = 6, 2, 4, 5, 0
            ORDER = [(g, h) for g in range(G0) for h in [None] + list(range(R0))]

            def unit_of(n):
                return (n // R0) * (R0 + 1) + 1 + n % R0

            with nc.Block() as block:
                @block.sync
                def _(sp):
                    for T in range(TILES):
                        sp.dma_start(x[:, T, :], dram["x"][T, :, :]).then_inc(x_in, 16)
                        if T == 1:
                            for dst, name in ((ident, "ident"), (ident_bf, "ident_bf"), (masks, "masks"), (cos, "l0_cos"), (sin, "l0_sin")):
                                sp.dma_start(words(dst), dram[name]).then_inc(consts_in, 16)
                    sp.dma_start(wv[:, :, :], dram["l0_wv"]).then_inc(wv_in, 16)
                    sp.dma_start(wk[:, :, :], dram["l0_wk"]).then_inc(wk_in, 16)
                    for g in range(G0):
                        sp.dma_start(wq[:, g, :, :], dram["l0_wq"][g]).then_inc(wq_in[g], 16)
                        sp.dma_start(wo[:, g * R0:(g + 1) * R0, :], dram["l0_wo"][g]).then_inc(wo_in[g], 16)

                @block.gpsimd
                def _(pool):
                    nc.gpsimd.memset(minus_half[:, :], -0.5).then_inc(half_ready, 1)
                    nc.gpsimd.memset(eps[:, :], EPS).then_inc(half_ready, 1)
                    pool.wait_ge(half_ready, 2)
                    with pool.Fori(0, BATCH) as b:
                        norm_gpsimd(pool, 0, b)

                        def add_rope(u):
                            g, h = ORDER[u]
                            pool.wait_ge(rope_muled, b * PROJ0 + (u + 1))
                            dst = kT[:, g % 2, :] if h is None else qT[:, h, :]
                            nc.gpsimd.tensor_tensor(dst, dst, t_sin[:, u % 2, :], ALU.add).then_inc(roped, 1)

                        add_rope(0)
                        add_rope(1)
                        for n in range(H0):
                            if n + 1 < H0:
                                if (n + 1) % R0 == 0:
                                    add_rope(unit_of(n + 1) - 1)
                                add_rope(unit_of(n + 1))
                            s = n % 2
                            pool.wait_ge(sum_inverted, b * H0 + (n + 1))
                            nc.gpsimd.tensor_tensor(prob[:, s, 0:P], prob[:, s, 0:P],
                                                    rowsum[:, s, 0:1].to_broadcast([P, P]), ALU.mult)
                            nc.gpsimd.tensor_tensor(prob[:, s, P:3 * P], prob[:, s, P:3 * P],
                                                    rowsum[:, s, 1:2].to_broadcast([P, 2 * P]), ALU.mult).then_inc(scaled, 1)

                @block.vector
                def _(dve):
                    def keep_out(b, n):
                        dve.wait_ge(attended, b * H0 + (n + 1))
                        if n >= 2:
                            dve.wait_ge(out_used, b * H0 + (n - 1))
                        nc.vector.tensor_copy(oT[:, n % 2, :], ps[:, OUT, 0:SEQ]).then_inc(oT_ready, 1)

                    dve.wait_ge(consts_in, 16 * 5)
                    with dve.Fori(0, BATCH) as b:
                        norm_vector(dve, 0, b, xn)

                        def mul_rope(u):
                            s = u % 2
                            pr = ps[:, PROJ + s, 0:SEQ]
                            dve.wait_ge(projected, b * PROJ0 + (u + 1))
                            if u >= 2:
                                dve.wait_ge(roped, b * PROJ0 + (u - 1))
                            g, h = ORDER[u]
                            if h is None and g >= 2:
                                dve.wait_ge(scored, b * H0 + R0 * (g - 1))
                            if h is not None and g >= 1:
                                dve.wait_ge(scored, b * H0 + (g * R0 + h - R0 + 1))
                            dst = kT[:, g % 2, :] if h is None else qT[:, h, :]
                            nc.vector.tensor_tensor(dst, pr, cos[:, :], ALU.mult)
                            nc.vector.tensor_tensor(t_sin[0:64, s, :], ps[64:128, PROJ + s, 0:SEQ], sin[0:64, :], ALU.mult)
                            nc.vector.tensor_tensor(t_sin[64:128, s, :], ps[0:64, PROJ + s, 0:SEQ], sin[64:128, :],
                                                    ALU.mult).then_inc(rope_muled, 1)

                        mul_rope(0)
                        mul_rope(1)
                        for n in range(H0):
                            s = n % 2
                            dve.wait_ge(scored, b * H0 + (n + 1))
                            nc.vector.reduce_max(rowmax[:, s, 0:1], ps[:, SCORE + s, 0:P], AX.X).then_inc(max_chain, 1)
                            nc.vector.reduce_max(rowmax[:, s, 1:2], ps[:, SCORE + s, P:3 * P], AX.X).then_inc(max_chain, 1)
                            dve.wait_ge(max_chain, b * 2 * H0 + 2 * (n + 1))
                            nc.vector.tensor_scalar(rowmax[:, s, :], rowmax[:, s, :], -SCALE0, None, ALU.mult).then_inc(max_ready, 1)
                            if n + 1 < H0:
                                if (n + 1) % R0 == 0:
                                    mul_rope(unit_of(n + 1) - 1)
                                mul_rope(unit_of(n + 1))
                            if n >= 1:
                                keep_out(b, n - 1)
                            dve.wait_ge(exped, b * H0 + (n + 1))
                            nc.vector.reciprocal(rowsum[:, s, :], rowsum[:, s, :]).then_inc(sum_inverted, 1)
                        keep_out(b, H0 - 1)
                        dve.wait_ge(out_used, (b + 1) * H0)
                        for i in range(QT):
                            tile = x[:, bass.ds(b * QT + i, 1), :].rearrange("p a d -> p (a d)")
                            nc.vector.tensor_tensor(tile, ps[:, ACC + i, :], tile, ALU.add).then_inc(residual, 1)

                @block.scalar
                def _(act):
                    with act.Fori(0, BATCH) as b:
                        norm_scalar(act, 0, b, xT)
                        for c in range(4):
                            act.wait_ge(v_done, b * 4 + (c + 1))
                            nc.scalar.activation(val[:, c // 2, (c % 2) * 512:(c % 2 + 1) * 512],
                                                 ps[:, 2 + c, :], ACT.Copy).then_inc(v_kept, 1)

                        def keep_probT(n):
                            act.wait_ge(prob_flipped, b * H0 + (n + 1))
                            if n >= 2:
                                act.wait_ge(attended, b * H0 + (n - 1))
                            nc.scalar.activation(probT[:, n % 2, :], ps[:, FLIP, 0:3 * P], ACT.Copy).then_inc(probT_ready, 1)

                        for n in range(H0):
                            s = n % 2
                            act.wait_ge(max_ready, b * H0 + (n + 1))
                            if n >= 2:
                                act.wait_ge(prob_flipped, b * H0 + (n - 1))
                            nc.scalar.activation(prob[:, s, 0:P], ps[:, SCORE + s, 0:P], ACT.Exp, bias=rowmax[:, s, 0:1],
                                                 scale=SCALE0, accum_out=rowsum[:, s, 0:1])
                            nc.scalar.activation(prob[:, s, P:3 * P], ps[:, SCORE + s, P:3 * P], ACT.Exp, bias=rowmax[:, s, 1:2],
                                                 scale=SCALE0, accum_out=rowsum[:, s, 1:2]).then_inc(exped, 1)
                            if n >= 1:
                                keep_probT(n - 1)
                        keep_probT(H0 - 1)

                @block.tensor
                def _(pe):
                    pe.wait_ge(consts_in, 16 * 5)
                    with pe.Fori(0, BATCH) as b:
                        norm_tensor(pe, 0, b, xn)
                        pe.wait_ge(xT_ready, b * QT + QT)
                        pe.wait_ge(wv_in, 16)
                        for c in range(4):
                            for k in range(KC):
                                last = nc.tensor.matmul(ps[:, 2 + c, :], xT[:, k, (c // 2) * P:(c // 2 + 1) * P],
                                                        wv[:, k, (c % 2) * 512:(c % 2 + 1) * 512], start=(k == 0), stop=(k == KC - 1))
                            last.then_inc(v_done, 1)
                        pe.wait_ge(wk_in, 16)

                        def project(u):
                            g, h = ORDER[u]
                            if u >= 2:
                                pe.wait_ge(rope_muled, b * PROJ0 + (u - 1))
                            if h == 0:
                                pe.wait_ge(wq_in[g], 16)
                            for k in range(KC):
                                w = wk[:, k, g * D0:(g + 1) * D0] if h is None else wq[:, g, k, h * D0:(h + 1) * D0]
                                last = nc.tensor.matmul(ps[:, PROJ + u % 2, 0:SEQ], w, xT[:, k, :], start=(k == 0), stop=(k == KC - 1))
                            last.then_inc(projected, 1)

                        def score(n):
                            g, s = n // R0, n % 2
                            pe.wait_ge(roped, b * PROJ0 + (unit_of(n) + 1))
                            if n >= 2:
                                pe.wait_ge(exped, b * H0 + (n - 1))
                            q, k_, bank = qT[:, n % R0, :], kT[:, g % 2, :], ps[:, SCORE + s, :]
                            nc.tensor.matmul(bank[:, 0:P], q[:, 0:P], k_[:, 0:P], start=True, stop=False)
                            nc.tensor.matmul(bank[:, 0:P], ident_bf[:, :], masks[:, 0, :], start=False, stop=True)
                            nc.tensor.matmul(bank[:, P:3 * P], q[:, P:SEQ], k_, start=True, stop=False)
                            nc.tensor.matmul(bank[:, 2 * P:3 * P], ident_bf[:, :], masks[:, 0, :], start=False,
                                             stop=True).then_inc(scored, 1)

                        def flip(n):
                            pe.wait_ge(scaled, b * H0 + (n + 1))
                            if n >= 1:
                                pe.wait_ge(probT_ready, b * H0 + n)
                            for c in range(3):
                                last = nc.tensor.transpose(ps[:, FLIP, c * P:(c + 1) * P], prob[:, n % 2, c * P:(c + 1) * P], ident[:, :])
                            last.then_inc(prob_flipped, 1)

                        def attend(n):
                            g, s = n // R0, n % 2
                            pe.wait_ge(probT_ready, b * H0 + (n + 1))
                            if n >= 1:
                                pe.wait_ge(oT_ready, b * H0 + n)
                            if n == 0:
                                pe.wait_ge(v_kept, b * 4 + 4)
                            nc.tensor.matmul(ps[:, OUT, 0:2 * P], val[:, 0, g * D0:(g + 1) * D0], probT[:, s, 0:2 * P],
                                             start=True, stop=False)
                            nc.tensor.matmul(ps[:, OUT, P:2 * P], val[:, 1, g * D0:(g + 1) * D0], probT[:, s, 2 * P:3 * P],
                                             start=False, stop=True).then_inc(attended, 1)

                        def project_out(n):
                            pe.wait_ge(oT_ready, b * H0 + (n + 1))
                            if n % R0 == 0:
                                pe.wait_ge(wo_in[n // R0], 16)
                            for i in range(QT):
                                last = nc.tensor.matmul(ps[:, ACC + i, :], oT[:, n % 2, i * P:(i + 1) * P], wo[:, n, :],
                                                        start=(n == 0), stop=(n == H0 - 1))
                            last.then_inc(out_used, 1)

                        project(0)
                        project(1)
                        for n in range(H0 + 2):
                            if n < H0:
                                if n == 0:
                                    pe.wait_ge(v_kept, b * 4 + 4)
                                score(n)
                            if n + 1 < H0:
                                if (n + 1) % R0 == 0:
                                    project(unit_of(n + 1) - 1)
                                project(unit_of(n + 1))
                            if 1 <= n <= H0:
                                flip(n - 1)
                            if n >= 2:
                                project_out(n - 2)
                            if 1 <= n <= H0:
                                attend(n - 1)

        top[0] = base
        l0_ar, _ = place("l0_ar", [P, KC, E0 * RANK + E0])
        l0_b, _ = place("l0_b", [P, DIM])
        l1_qkv, _ = place("l1_qkv", [P, KC, DIM + 2 * KV_HEADS[0] * HD])
        l1_wo, _ = place("l1_wo", [P, KC, DIM])
        l1_w, _ = place("l1_w", [P, KC, DIM])
        l1_ag, _ = place("l1_ag", [P, KC, E1 * RANK + 4 * E1])
        l1_b, _ = place("l1_b", [P, DIM])
        l1_gvec, _ = place("l1_gvec", [P, 3 * 4 * E1 + E1])
        l1_gw2, _ = place("l1_gw2", [4 * E1, E1])
        top[0] = base
        l2_w13, _ = place("l2_w13", [P, KC, 2 * HID2])
        l2_w2, _ = place("l2_w2", [P, HC2, DIM])
        l2_a13, _ = place("l2_a13", [P, KC, 2 * RANK])
        l2_b13, _ = place("l2_b13", [96, HID2])
        l2_a2, _ = place("l2_a2", [P, HC2, RANK])
        l2_b2, _ = place("l2_b2", [96, DIM])
        after = top[0]
        top[0] = base
        l3_up, _ = place("l3_up", [P, KC, INT3])
        l3_down, _ = place("l3_down", [P, IC3, DIM])
        l3_fc1, _ = place("l3_fc1", [P, KC, LAT3 + E3])
        l3_expert, _ = place("l3_expert", [P, LC3, LAT3])
        l3_fc2, _ = place("l3_fc2", [P, LC3, DIM])
        l3_gb, _ = place("l3_gb", [P, 2 * DIM])
        top[0] = after
        l2_qkv, _ = place("l2_qkv", [P, KC, DIM + 2 * KV_HEADS[1] * HD])
        l2_wo, _ = place("l2_wo", [P, KC, DIM])
        l3_qkv, _ = place("l3_qkv", [P, KC, DIM + 2 * KV_HEADS[2] * HD])
        l3_bias, _ = place("l3_bias", [P, DIM + 2 * KV_HEADS[2] * HD])
        rope, _ = place("rope", [P, QT, 2, HD])
        lower4, _ = place("lower4", [P, E0 * E0])
        lower8, _ = place("lower8", [P, E1 * E1])
        onehot, _ = place("onehot", [96, HEADS, P], BF16)
        work = top[0]

        loads = {}
        for name, dst in (("l0_ar", l0_ar), ("l0_b", l0_b), ("lower4", lower4),
                          ("l1_qkv", l1_qkv), ("rope", rope), ("onehot", onehot), ("l1_wo", l1_wo),
                          ("l1_w", l1_w), ("l1_ag", l1_ag), ("l1_b", l1_b), ("l1_gvec", l1_gvec), ("l1_gw2", l1_gw2),
                          ("lower8", lower8), ("l2_qkv", l2_qkv), ("l2_wo", l2_wo), ("l3_qkv", l3_qkv), ("l3_bias", l3_bias),
                          ("l2_w13", l2_w13), ("l2_w2", l2_w2), ("l2_a13", l2_a13), ("l2_b13", l2_b13), ("l2_a2", l2_a2),
                          ("l2_b2", l2_b2), ("l3_up", l3_up), ("l3_down", l3_down), ("l3_fc1", l3_fc1),
                          ("l3_expert", l3_expert), ("l3_fc2", l3_fc2), ("l3_gb", l3_gb)):
            loads[name] = (dst, sem(f"{name}_in"))

        def load(sp, *names):
            for name in names:
                dst, arrived = loads[name]
                sp.dma_start(words(dst), dram[name]).then_inc(arrived, 16)

        def await_load(eng, *names):
            for name in names:
                eng.wait_ge(loads[name][1], 16)

        top[0] = work
        xn, _ = place("xn", [P, QT, DIM])
        xT, _ = place("xT", [P, KC, SEQ])
        oT, _ = place("oT", [P, UNITS, SEQ], at=work)
        qsT, _ = place("qsT", [STACK, HEADS, SEQ], BF16)
        ksT, _ = place("ksT", [STACK, 16, SEQ], BF16)
        val, _ = place("val", [P, QT, 16, VPAD])
        negmaxT, _ = place("negmaxT", [96, SEQ], BF16)
        negmax, _ = place("negmax", [P, QT, 3, HEADS], BF16)
        rowmax, _ = place("rowmax", [P, QT, HEADS])
        maxrest, _ = place("maxrest", [P, QT, HEADS])
        rowrcp, _ = place("rowrcp", [P, QT, HEADS])
        here = top[0]
        qs, _ = place("qs", [P, QT, HEADS, STACK], BF16)
        ks, _ = place("ks", [P, QT, 16, STACK], BF16)
        probT, _ = place("probT", [P, 2, 3 * DIM], at=here)
        here = top[0]
        qf, _ = place("qf", [P, QT, DIM])
        kf, _ = place("kf", [P, QT, 256])
        rot, _ = place("rot", [P, DIM + 256])
        rest, _ = place("rest", [P, DIM + 256])
        attn, _ = place("attn", [P, QT, DIM], at=here)
        aT, _ = place("aT", [P, KC, SEQ], at=here + QT * DIM * 4)

        qkv_done = sem("qkv_done")
        v_kept = sem("v_kept")
        rope_muled = sem("rope_muled")
        qk_float = sem("qk_float")
        part_cut = sem("part_cut")
        rest_ready = sem("rest_ready")
        stack_flipped = sem("stack_flipped")
        stackT_vector = sem("stackT_vector")
        stackT_scalar = sem("stackT_scalar")
        scored = sem("scored")
        maxed = sem("maxed")
        max_chain = sem("max_chain")
        negmax_ready = sem("negmax_ready")
        negmax_flipped = sem("negmax_flipped")
        negmaxT_ready = sem("negmaxT_ready")
        key_scored = sem("key_scored")
        exped = sem("exped")
        attended = sem("attended")
        oT_ready = sem("oT_ready")
        o_flipped = sem("o_flipped")
        rcp_chain = sem("rcp_chain")
        attn_ready = sem("attn_ready")
        attn_flipped = sem("attn_flipped")
        aT_ready = sem("aT_ready")
        out_done = sem("out_done")
        val_set = sem("val_set")

        def attention(a, sub, wqkv, wqkv_name, wo, wo_name, first_loads, later_loads):
            kv = KV_HEADS[a]
            rep = HEADS // kv
            kvd = kv * HD
            rotary = wo is not None
            t0 = a * BATCH
            SU = kv // 8 + 4
            su0 = t0 * 5
            SORDER = [(i, kind, c) for i in range(QT) for kind, c in
                      [("k", c) for c in range(kv // 8)] + [("q", c) for c in range(4)]]

            with nc.Block() as block:
                @block.sync
                def _(sp):
                    load(sp, *first_loads)
                    load(sp, *later_loads)

                @block.gpsimd
                def _(pool):
                    nc.gpsimd.memset(val[:, :, :, HD:VPAD], 0.0).then_inc(val_set, 1)
                    pool.wait_ge(val_set, 2 * a + 1)
                    nc.gpsimd.memset(val[:, :, :, HD:HD + 1], 1.0).then_inc(val_set, 1)
                    with pool.Fori(0, BATCH) as b:
                        norm_gpsimd(pool, sub, b)
                        turn = b + t0
                        for i in range(QT):
                            if rotary:
                                pool.wait_ge(rope_muled, turn * QT + (i + 1))
                                nc.gpsimd.tensor_tensor(qf[:, i, :], qf[:, i, :], rot[:, 0:DIM], ALU.add)
                                nc.gpsimd.tensor_tensor(kf[:, i, 0:kvd], kf[:, i, 0:kvd], rot[:, DIM:DIM + kvd],
                                                        ALU.add).then_inc(qk_float, 1)
                            pool.wait_ge(part_cut, turn * 6 + (3 * i + 1))
                            restq = rest[:, 0:DIM].rearrange("p (h d) -> p h d", d=HD)
                            restk = rest[:, DIM:DIM + kvd].rearrange("p (h d) -> p h d", d=HD)
                            nc.gpsimd.tensor_tensor(restq, qf[:, i, :].rearrange("p (h d) -> p h d", d=HD),
                                                    qs[:, i, :, 0:HD], ALU.subtract)
                            nc.gpsimd.tensor_tensor(restk, kf[:, i, 0:kvd].rearrange("p (h d) -> p h d", d=HD),
                                                    ks[:, i, 0:kv, HD:2 * HD], ALU.subtract).then_inc(rest_ready, 1)
                            pool.wait_ge(part_cut, turn * 6 + (3 * i + 2))
                            nc.gpsimd.tensor_tensor(restq, restq, qs[:, i, :, 3 * HD:4 * HD], ALU.subtract)
                            nc.gpsimd.tensor_tensor(restk, restk, ks[:, i, 0:kv, 2 * HD:3 * HD],
                                                    ALU.subtract).then_inc(rest_ready, 1)

                @block.vector
                def _(dve):
                    if rotary:
                        await_load(dve, "rope")
                    else:
                        await_load(dve, "l3_bias")
                    with dve.Fori(0, BATCH) as b:
                        norm_vector(dve, sub, b, xn)
                        turn = b + t0
                        for i in range(QT):
                            dve.wait_ge(qkv_done, turn * QT + (i + 1))
                            pq, pk = ps[:, 2 + i, :], ps[:, 4 + i, 0:kvd]
                            if rotary:
                                if i == 1:
                                    dve.wait_ge(qk_float, turn * QT + 1)
                                cos = rope[:, i, 0:1, :]
                                for src, dst, tmp, n in ((pq, qf[:, i, :], rot[:, 0:DIM], HEADS),
                                                         (pk, kf[:, i, 0:kvd], rot[:, DIM:DIM + kvd], kv)):
                                    s3 = src.rearrange("p (h d) -> p h d", d=HD)
                                    t3 = tmp.rearrange("p (h d) -> p h d", d=HD)
                                    nc.vector.tensor_tensor(dst.rearrange("p (h d) -> p h d", d=HD), s3,
                                                            cos.to_broadcast([P, n, HD]), ALU.mult)
                                    nc.vector.tensor_tensor(t3[:, :, 0:8], s3[:, :, 8:16],
                                                            rope[:, i, 1:2, 0:8].to_broadcast([P, n, 8]), ALU.mult)
                                    last = nc.vector.tensor_tensor(t3[:, :, 8:16], s3[:, :, 0:8],
                                                                   rope[:, i, 1:2, 8:16].to_broadcast([P, n, 8]), ALU.mult)
                                last.then_inc(rope_muled, 1)
                            else:
                                nc.vector.tensor_tensor(qf[:, i, :], pq, l3_bias[:, 0:DIM], ALU.add)
                                nc.vector.tensor_tensor(val[:, i, 0:kv, 0:HD],
                                                        ps[:, 4 + i, kvd:2 * kvd].rearrange("p (h d) -> p h d", d=HD),
                                                        l3_bias[:, DIM + kvd:DIM + 2 * kvd].rearrange("p (h d) -> p h d", d=HD),
                                                        ALU.add).then_inc(v_kept, 1)
                                nc.vector.tensor_tensor(kf[:, i, 0:kvd], pk, l3_bias[:, DIM:DIM + kvd], ALU.add).then_inc(qk_float, 1)
                        for u in range(0, 2 * SU, 2):
                            i, kind, c = SORDER[u]
                            dst = (ksT if kind == "k" else qsT)[:, 8 * c:8 * c + 8, i * P:(i + 1) * P]
                            dve.wait_ge(stack_flipped, b * (2 * SU) + (2 * su0 + u + 1))
                            nc.vector.tensor_copy(dst, ps_bf[0:STACK, 4 + u % 4, :].rearrange("p (h t) -> p h t", t=P))\
                                .then_inc(stackT_vector, 1)
                        for i in range(QT):
                            for hg in range(UNITS):
                                v = i * UNITS + hg
                                dve.wait_ge(scored, turn * (2 * UNITS) + (v + 1))
                                s = ps[:, 2 * (v % 2):2 * (v % 2) + 2, :].rearrange("p a (h t) -> p a h t", h=2)
                                out_ = rowmax[:, i, 4 * hg:4 * hg + 4].rearrange("p (a h) -> p a h", h=2)
                                nc.vector.reduce_max(out_, s[:, :, :, 0:(i + 1) * P], AX.X).then_inc(maxed, 1)
                            dve.wait_ge(maxed, turn * (2 * UNITS) + (i + 1) * UNITS)
                            nc.vector.tensor_scalar(negmax[:, i, 0, :], rowmax[:, i, :], -1.0, None, ALU.mult).then_inc(max_chain, 1)
                            dve.wait_ge(max_chain, turn * (3 * QT) + (3 * i + 1))
                            nc.vector.scalar_tensor_tensor(maxrest[:, i, :], rowmax[:, i, :], -1.0, negmax[:, i, 0, :],
                                                           ALU.mult, ALU.subtract).then_inc(max_chain, 1)
                            dve.wait_ge(max_chain, turn * (3 * QT) + (3 * i + 2))
                            nc.vector.tensor_copy(negmax[:, i, 1, :], maxrest[:, i, :]).then_inc(max_chain, 1)
                            dve.wait_ge(max_chain, turn * (3 * QT) + (3 * i + 3))
                            nc.vector.tensor_tensor(negmax[:, i, 2, :], maxrest[:, i, :], negmax[:, i, 1, :],
                                                    ALU.subtract).then_inc(negmax_ready, 1)
                        for e in range(UNITS):
                            dve.wait_ge(attended, turn * UNITS + (e + 1))
                            nc.vector.tensor_copy(oT[:, e, :], ps[:, 6 + e % 2, 0:SEQ]).then_inc(oT_ready, 1)
                        for c in range(4):
                            half, i = c // 2, c % 2
                            o = ps[:, c, :].rearrange("p (h d) -> p h d", d=VPAD)
                            rcp = rowrcp[:, i, 16 * half:16 * half + 16]
                            dve.wait_ge(o_flipped, turn * 4 + (c + 1))
                            nc.vector.reciprocal(rcp, o[:, :, HD]).then_inc(rcp_chain, 1)
                            dve.wait_ge(rcp_chain, turn * 4 + (c + 1))
                            nc.vector.tensor_tensor(attn[:, i, 256 * half:256 * half + 256].rearrange("p (h d) -> p h d", d=HD),
                                                    o[:, :, 0:HD], rcp.unsqueeze(2).to_broadcast([P, 16, HD]), ALU.mult)\
                                .then_inc(attn_ready, 1)
                        for i in range(QT):
                            tile = x[:, bass.ds(b * QT + i, 1), :].rearrange("p a d -> p (a d)")
                            if rotary:
                                dve.wait_ge(out_done, turn * QT + (i + 1))
                                nc.vector.tensor_tensor(tile, ps[:, 6 + i, :], tile, ALU.add).then_inc(residual, 1)
                            else:
                                dve.wait_ge(attn_ready, turn * 4 + 4)
                                view = tile.rearrange("p (g k d) -> p k g d", g=rep, d=HD)
                                nc.vector.tensor_tensor(view, view, attn[:, i, :].rearrange("p (k g d) -> p k g d", g=rep, d=HD),
                                                        ALU.add).then_inc(residual, 1)

                @block.scalar
                def _(act):
                    with act.Fori(0, BATCH) as b:
                        norm_scalar(act, sub, b, xT)
                        turn = b + t0
                        for i in range(QT):
                            if rotary:
                                act.wait_ge(rope_muled, turn * QT + (i + 1))
                                nc.scalar.activation(val[:, i, 0:kv, 0:HD],
                                                     ps[:, 4 + i, kvd:2 * kvd].rearrange("p (h d) -> p h d", d=HD),
                                                     ACT.Copy).then_inc(v_kept, 1)
                        for i in range(QT):
                            q3 = qf[:, i, :].rearrange("p (h r d) -> p h r d", r=1, d=HD)
                            k3 = kf[:, i, 0:kvd].rearrange("p (h r d) -> p h r d", r=1, d=HD)
                            rq3 = rest[:, 0:DIM].rearrange("p (h r d) -> p h r d", r=1, d=HD)
                            rk3 = rest[:, DIM:DIM + kvd].rearrange("p (h r d) -> p h r d", r=1, d=HD)
                            q4 = qs[:, i, :, :].rearrange("p h (r d) -> p h r d", d=HD)
                            k4 = ks[:, i, 0:kv, :].rearrange("p h (r d) -> p h r d", d=HD)
                            act.wait_ge(qk_float, turn * QT + (i + 1))
                            nc.scalar.activation(q4[:, :, 0:3, :], q3.to_broadcast([P, HEADS, 3, HD]), ACT.Copy)
                            nc.scalar.activation(k4[:, :, 1:6:2, :], k3.to_broadcast([P, kv, 3, HD]), ACT.Copy).then_inc(part_cut, 1)
                            act.wait_ge(rest_ready, turn * 4 + (2 * i + 1))
                            nc.scalar.activation(q4[:, :, 3:5, :], rq3.to_broadcast([P, HEADS, 2, HD]), ACT.Copy)
                            nc.scalar.activation(k4[:, :, 2:5:2, :], rk3.to_broadcast([P, kv, 2, HD]), ACT.Copy).then_inc(part_cut, 1)
                            act.wait_ge(rest_ready, turn * 4 + (2 * i + 2))
                            nc.scalar.activation(q4[:, :, 5:6, :], rq3, ACT.Copy)
                            nc.scalar.activation(k4[:, :, 0:1, :], rk3, ACT.Copy).then_inc(part_cut, 1)
                        for u in range(1, 2 * SU, 2):
                            i, kind, c = SORDER[u]
                            dst = (ksT if kind == "k" else qsT)[:, 8 * c:8 * c + 8, i * P:(i + 1) * P]
                            act.wait_ge(stack_flipped, b * (2 * SU) + (2 * su0 + u + 1))
                            nc.scalar.activation(dst, ps_bf[0:STACK, 4 + u % 4, :].rearrange("p (h t) -> p h t", t=P), ACT.Copy)\
                                .then_inc(stackT_scalar, 1)
                        for i in range(QT):
                            act.wait_ge(negmax_flipped, turn * QT + (i + 1))
                            nc.scalar.activation(negmaxT[:, i * P:(i + 1) * P], ps_bf[0:96, 6 + i, 0:P], ACT.Copy)\
                                .then_inc(negmaxT_ready, 1)
                        for e in range(UNITS):
                            act.wait_ge(key_scored, turn * UNITS + (e + 1))
                            if e >= 2:
                                act.wait_ge(attended, turn * UNITS + (e - 1))
                            bank = 3 * (e % 2)
                            nc.scalar.activation(probT[:, e % 2, :].rearrange("p (a t) -> p a t", a=3),
                                                 ps[:, bank:bank + 3, :], ACT.Exp, scale=SCALES[a]).then_inc(exped, 1)
                        if rotary:
                            for i in range(QT):
                                act.wait_ge(attn_flipped, turn * QT + (i + 1))
                                nc.scalar.activation(aT[:, :, i * P:(i + 1) * P], ps[:, 4 + i, :].rearrange("p (k t) -> p k t", k=KC),
                                                     ACT.Copy).then_inc(aT_ready, 1)

                @block.tensor
                def _(pe):
                    await_load(pe, wqkv_name, "onehot")
                    if rotary:
                        await_load(pe, wo_name)
                    pe.wait_ge(val_set, 2 * a + 2)
                    with pe.Fori(0, BATCH) as b:
                        norm_tensor(pe, sub, b, xn)
                        turn = b + t0
                        pe.wait_ge(xT_ready, (b + sub * BATCH) * QT + QT)
                        for i in range(QT):
                            lhs = [xT[:, k, i * P:(i + 1) * P] for k in range(KC)]
                            for k in range(KC):
                                nc.tensor.matmul(ps[:, 2 + i, :], lhs[k], wqkv[:, k, 0:DIM], start=(k == 0), stop=(k == KC - 1))
                            for k in range(KC):
                                last = nc.tensor.matmul(ps[:, 4 + i, 0:2 * kvd], lhs[k], wqkv[:, k, DIM:DIM + 2 * kvd],
                                                        start=(k == 0), stop=(k == KC - 1))
                            last.then_inc(qkv_done, 1)
                        pe.wait_ge(v_kept, turn * QT + QT)
                        for u in range(2 * SU):
                            i, kind, c = SORDER[u]
                            if u % SU == 0:
                                pe.wait_ge(part_cut, turn * 6 + 3 * (i + 1))
                                if u == 0:
                                    pe.wait_ge(qk_float, turn * QT + QT)
                            if u >= 4:
                                kept = stackT_scalar if u % 2 else stackT_vector
                                pe.wait_ge(kept, b * SU + (su0 + (u - 4) // 2 + 1))
                            src = ks if kind == "k" else qs
                            for h in range(8):
                                last = nc.tensor.transpose(ps_bf[0:STACK, 4 + u % 4, h * P:(h + 1) * P],
                                                           src[:, i, 8 * c + h, :], ident_bf[:, :])
                            last.then_inc(stack_flipped, 1)
                        pe.wait_ge(stackT_vector, b * SU + (su0 + SU))
                        pe.wait_ge(stackT_scalar, b * SU + (su0 + SU))
                        for i in range(QT):
                            keys = (i + 1) * P
                            for hg in range(UNITS):
                                v = i * UNITS + hg
                                if v >= 2:
                                    pe.wait_ge(maxed, turn * (2 * UNITS) + (v - 1))
                                for half in range(2):
                                    bank = ps[:, 2 * (v % 2) + half, :].rearrange("p (h t) -> p h t", h=2)
                                    nc.tensor.matmul(bank[:, :, i * P:keys], ident_bf[:, :], masks[:, 0:1, :].to_broadcast([P, 2, P]),
                                                     start=True, stop=False, skip_group_check=True)
                                    for j in range(2):
                                        h = 4 * hg + 2 * half + j
                                        last = nc.tensor.matmul(bank[:, j, 0:keys], qsT[:, h, i * P:(i + 1) * P],
                                                                ksT[:, h // rep, 0:keys], start=False, stop=(j == 1),
                                                                skip_group_check=True)
                                last.then_inc(scored, 1)
                            pe.wait_ge(negmax_ready, turn * QT + (i + 1))
                            nc.tensor.transpose(ps_bf[0:96, 6 + i, 0:P], negmax[:, i, :, :].rearrange("p c h -> p (c h)"),
                                                ident_bf[:, :]).then_inc(negmax_flipped, 1)
                        pe.wait_ge(negmaxT_ready, turn * QT + QT)

                        def key_score(e):
                            if e >= 2:
                                pe.wait_ge(exped, turn * UNITS + (e - 1))
                            bank = 3 * (e % 2)
                            for half in range(2):
                                o = ps[:, bank + half, :].rearrange("p (h t) -> p h t", h=2)
                                nc.tensor.matmul(o[:, :, 0:P], ident_bf[:, :], masks[:, 1:2, :].to_broadcast([P, 2, P]),
                                                 start=True, stop=False, skip_group_check=True)
                                for j in range(2):
                                    h = 4 * e + 2 * half + j
                                    nc.tensor.matmul(o[:, j, :], onehot[:, h, :], negmaxT[:, :], start=False, stop=False,
                                                     skip_group_check=True)
                                    nc.tensor.matmul(o[:, j, :], ksT[:, h // rep, 0:P], qsT[:, h, :], start=False, stop=(j == 1),
                                                     skip_group_check=True)
                            o = ps[:, bank + 2, :].rearrange("p (h t) -> p h t", h=4)
                            nc.tensor.matmul(o, ident_bf[:, :], masks[:, 1:2, :].to_broadcast([P, 4, P]), start=True, stop=False,
                                             skip_group_check=True)
                            for j in range(4):
                                h = 4 * e + j
                                nc.tensor.matmul(o[:, j, :], onehot[:, h, :], negmaxT[:, P:SEQ], start=False, stop=False,
                                                 skip_group_check=True)
                                last = nc.tensor.matmul(o[:, j, :], ksT[:, h // rep, P:SEQ], qsT[:, h, P:SEQ], start=False,
                                                        stop=(j == 3), skip_group_check=True)
                            last.then_inc(key_scored, 1)

                        def attend(e):
                            pe.wait_ge(exped, turn * UNITS + (e + 1))
                            if e >= 2:
                                pe.wait_ge(oT_ready, turn * UNITS + (e - 1))
                            for j in range(4):
                                nc.tensor.matmul(ps[32 * j:32 * j + 32, 6 + e % 2, 0:SEQ], val[:, 0, (4 * e + j) // rep, :],
                                                 probT[:, e % 2, j * SEQ:(j + 1) * SEQ], start=True, stop=False)
                            for j in range(4):
                                last = nc.tensor.matmul(ps[32 * j:32 * j + 32, 6 + e % 2, P:SEQ], val[:, 1, (4 * e + j) // rep, :],
                                                        probT[:, e % 2, 4 * SEQ + j * P:4 * SEQ + (j + 1) * P],
                                                        start=False, stop=True)
                            last.then_inc(attended, 1)

                        for e in range(UNITS):
                            key_score(e)
                            if e >= 1:
                                attend(e - 1)
                        attend(UNITS - 1)
                        for c in range(4):
                            half, i = c // 2, c % 2
                            if c == 0:
                                pe.wait_ge(exped, turn * UNITS + UNITS)
                            pe.wait_ge(oT_ready, turn * UNITS + 4 * (half + 1))
                            for e in range(4 * half, 4 * half + 4):
                                last = nc.tensor.transpose(ps[:, c, (e % 4) * P:(e % 4 + 1) * P], oT[:, e, i * P:(i + 1) * P],
                                                           ident[:, :])
                            last.then_inc(o_flipped, 1)
                        if rotary:
                            for i in range(QT):
                                pe.wait_ge(attn_ready, turn * 4 + (3 + i))
                                for k in range(KC):
                                    last = nc.tensor.transpose(ps[:, 4 + i, k * P:(k + 1) * P], attn[:, i, k * P:(k + 1) * P], ident[:, :])
                                last.then_inc(attn_flipped, 1)
                            for i in range(QT):
                                pe.wait_ge(aT_ready, turn * QT + (i + 1))
                                for k in range(KC):
                                    last = nc.tensor.matmul(ps[:, 6 + i, :], aT[:, k, i * P:(i + 1) * P], wo[:, k, :],
                                                            start=(k == 0), stop=(k == KC - 1))
                                last.then_inc(out_done, 1)

        top[0] = work + QT * DIM * 4 + KC * SEQ * 4
        logits, _ = place("logits", [P, QT, E1])
        beats, _ = place("beats", [P, QT, E1 * E1])
        ties, _ = place("ties", [P, QT, E1 * E1])
        ranks, _ = place("ranks", [P, QT, E1])
        gates, _ = place("gates", [P, QT, E1])
        top_logit, _ = place("top_logit", [P, QT])
        gate_sum, _ = place("gate_sum", [P, QT])
        mid, _ = place("mid", [P, QT, P])
        midT, _ = place("midT", [P, SEQ])
        here = top[0]
        tmp1, _ = place("tmp1", [P, TILES, E1 * RANK])
        midT1, _ = place("midT1", [P, TILES, P])
        chosen, _ = place("chosen", [P, TILES, 2, E1])
        topg, _ = place("topg", [P, TILES, 2])
        weighed, _ = place("weighed", [P, TILES, 2, E1])
        wexp, _ = place("wexp", [P, TILES, E1])
        counts, _ = place("counts", [P, 2 * E1])
        ones, _ = place("ones", [P, P])
        hid, _ = place("hid", [P, QT, 4 * E1])
        hidT, _ = place("hidT", [4 * E1, SEQ])
        hstats, _ = place("hstats", [P, QT, 6])
        hmv, _ = place("hmv", [P, QT, 2])
        hrstd, _ = place("hrstd", [P, QT, 1])
        gap, _ = place("gap", [P, QT, 2])
        top[0] = here
        lowT, _ = place("lowT", [96, 2, SEQ])
        low2T, _ = place("low2T", [96, SEQ])
        lmask, _ = place("lmask", [2 * RANK, 2])
        tanh_, _ = place("tanh_", [P, 2, SEQ])
        half_silu, _ = place("half_silu", [P, 2, SEQ])
        gT, _ = place("gT", [P, HC2, SEQ])
        top[0] = here
        latT, _ = place("latT", [P, LC3, SEQ])
        expT, _ = place("expT", [P, LC3, SEQ])
        top8, _ = place("top8", [P, QT, E3])
        routing, _ = place("routing", [P, QT])
        relu_, _ = place("relu_", [P, 2, SEQ])
        hT, _ = place("hT", [P, IC3, SEQ])
        shared, _ = place("shared", [P, QT, DIM])
        ystats, _ = place("ystats", [P, QT, 6])
        ymv, _ = place("ymv", [P, QT, 2])
        yrstd, _ = place("yrstd", [P, QT, 1])
        loads["lmask"] = (lmask, sem("lmask_in"))

        def tile_of(b, i):
            return x[:, bass.ds(b * QT + i, 1), :].rearrange("p a d -> p (a d)")

        def rank_experts(chain, E, lower):
            lg = logits[:, :, 0:E]
            f = lg.unsqueeze(2).to_broadcast([P, QT, E, E])
            e = lg.unsqueeze(3).to_broadcast([P, QT, E, E])
            bt = beats[:, :, 0:E * E].rearrange("p i (e f) -> p i e f", f=E)
            ti = ties[:, :, 0:E * E].rearrange("p i (e f) -> p i e f", f=E)
            for i in range(QT):
                nc.vector.tensor_tensor(bt[:, i], f[:, i], e[:, i], ALU.is_gt)
                last = nc.vector.tensor_tensor(ti[:, i], f[:, i], e[:, i], ALU.is_equal)
            chain.link(last)
            low = lower[:, :].unsqueeze(1).to_broadcast([P, QT, E * E])
            chain.link(nc.vector.tensor_tensor(ties[:, :, 0:E * E], ties[:, :, 0:E * E], low, ALU.mult))
            chain.link(nc.vector.tensor_tensor(beats[:, :, 0:E * E], beats[:, :, 0:E * E], ties[:, :, 0:E * E], ALU.add))
            chain.link(nc.vector.reduce_sum(ranks[:, :, 0:E], bt, AX.X))

        def layer0_feed_forward(sub):
            mid_done = sem("f0_mid_done")
            chain_sem = sem("f0_chain")
            shifted = sem("f0_shifted")
            exped0 = sem("f0_exped")
            gated = sem("f0_gated")
            mid_flipped = sem("f0_mid_flipped")
            midT_ready = sem("f0_midT_ready")
            done = sem("f0_done")
            EA = E0 * RANK

            with nc.Block() as block:
                @block.sync
                def _(sp):
                    load(sp, "l0_ar", "l0_b", "lower4", "l1_qkv", "rope", "onehot", "l1_wo")

                @block.gpsimd
                def _(pool):
                    nc.gpsimd.memset(mid[:, :, :], 0.0).then_inc(val_set0, 1)
                    with pool.Fori(0, BATCH) as b:
                        norm_gpsimd(pool, sub, b)

                @block.vector
                def _(dve):
                    await_load(dve, "lower4")
                    dve.wait_ge(val_set0, 1)
                    chain = Chain(dve, chain_sem, 11)
                    with dve.Fori(0, BATCH) as b:
                        norm_vector(dve, sub, b, xn)
                        chain.start(b)
                        dve.wait_ge(mid_done, b + 1)
                        lg, gt = logits[:, :, 0:E0], gates[:, :, 0:E0]
                        chain.link(nc.vector.tensor_copy(lg, ps[:, 2:4, EA:EA + E0]))
                        rank_experts(chain, E0, lower4)
                        chain.link(nc.vector.tensor_scalar(ranks[:, :, 0:E0], ranks[:, :, 0:E0], 1.5, None, ALU.is_lt))
                        chain.link(nc.vector.reduce_max(top_logit[:, :], lg, AX.X))
                        nc.vector.tensor_tensor(gt, lg, top_logit[:, :].unsqueeze(2).to_broadcast([P, QT, E0]),
                                                ALU.subtract).then_inc(shifted, 1)
                        dve.wait_ge(exped0, b + 1)
                        chain.link(nc.vector.tensor_tensor(gt, gt, ranks[:, :, 0:E0], ALU.mult))
                        chain.link(nc.vector.reduce_sum(gate_sum[:, :], gt, AX.X))
                        chain.link(nc.vector.reciprocal(gate_sum[:, :], gate_sum[:, :]))
                        chain.link(nc.vector.scalar_tensor_tensor(gt, gt, 4.0, gate_sum[:, :].unsqueeze(2).to_broadcast([P, QT, E0]),
                                                                  ALU.mult, ALU.mult))
                        for i in range(QT):
                            last = nc.vector.tensor_tensor(mid[:, i, 0:EA].rearrange("p (e r) -> p e r", r=RANK),
                                                           ps[:, 2 + i, 0:EA].rearrange("p (e r) -> p e r", r=RANK),
                                                           gt[:, i, :].unsqueeze(2).to_broadcast([P, E0, RANK]), ALU.mult)
                        last.then_inc(gated, 1)
                        chain.end()
                        dve.wait_ge(done, b + 1)
                        for i in range(QT):
                            nc.vector.tensor_tensor(tile_of(b, i), ps[:, 6 + i, :], tile_of(b, i), ALU.add).then_inc(residual, 1)

                @block.scalar
                def _(act):
                    with act.Fori(0, BATCH) as b:
                        norm_scalar(act, sub, b, xT)
                        act.wait_ge(shifted, b + 1)
                        nc.scalar.activation(gates[:, :, 0:E0], gates[:, :, 0:E0], ACT.Exp).then_inc(exped0, 1)
                        act.wait_ge(mid_flipped, b + 1)
                        nc.scalar.activation(midT[:, :], ps[:, 4, 0:SEQ], ACT.Copy).then_inc(midT_ready, 1)

                @block.tensor
                def _(pe):
                    await_load(pe, "l0_ar", "l0_b")
                    with pe.Fori(0, BATCH) as b:
                        norm_tensor(pe, sub, b, xn)
                        pe.wait_ge(xT_ready, (b + sub * BATCH) * QT + QT)
                        for i in range(QT):
                            for k in range(KC):
                                last = nc.tensor.matmul(ps[:, 2 + i, 0:EA + E0], xT[:, k, i * P:(i + 1) * P], l0_ar[:, k, :],
                                                        start=(k == 0), stop=(k == KC - 1))
                        last.then_inc(mid_done, 1)
                        pe.wait_ge(gated, b + 1)
                        for i in range(QT):
                            last = nc.tensor.transpose(ps[:, 4, i * P:(i + 1) * P], mid[:, i, :], ident[:, :])
                        last.then_inc(mid_flipped, 1)
                        pe.wait_ge(midT_ready, b + 1)
                        for i in range(QT):
                            last = nc.tensor.matmul(ps[:, 6 + i, :], midT[:, i * P:(i + 1) * P], l0_b[:, :], start=True, stop=True)
                        last.then_inc(done, 1)

        def layer1_feed_forward(sub):
            main_done = sem("f1_main_done")
            chain_sem = sem("f1_chain")
            hvar = sem("f1_hvar")
            pool_chain = sem("f1_pool_chain")
            hrstd_ready = sem("f1_hrstd_ready")
            hid_ready = sem("f1_hid_ready")
            hid_flipped = sem("f1_hid_flipped")
            hidT_ready = sem("f1_hidT_ready")
            logits_done = sem("f1_logits_done")
            gap_ready = sem("f1_gap_ready")
            gap_exped = sem("f1_gap_exped")
            turn_over = sem("f1_turn_over")
            ones_set = sem("f1_ones_set")
            counted = sem("f1_counted")
            tail_chain = sem("f1_tail_chain")
            weighted = sem("f1_weighted")
            mid_flipped = sem("f1_mid_flipped")
            midT_ready = sem("f1_midT_ready")
            done = sem("f1_done")
            EA, HG = E1 * RANK, 4 * E1

            with nc.Block() as block:
                @block.gpsimd
                def _(pool):
                    nc.gpsimd.memset(ones[:, :], 1.0).then_inc(ones_set, 1)
                    with pool.Fori(0, BATCH) as b:
                        norm_gpsimd(pool, sub, b)
                        pool.wait_ge(hvar, b + 1)
                        nc.gpsimd.tensor_tensor(hrstd[:, :, 0], hmv[:, :, 1], eps[:, :].to_broadcast([P, QT]), ALU.add).then_inc(pool_chain, 1)
                        pool.wait_ge(pool_chain, b + 1)
                        nc.gpsimd.tensor_tensor(hrstd[:, :, 0], hrstd[:, :, 0], minus_half[:, :].to_broadcast([P, QT]),
                                                ALU.pow).then_inc(hrstd_ready, 1)

                @block.vector
                def _(dve):
                    await_load(dve, "l1_gvec", "lower8")
                    chain = Chain(dve, chain_sem, 15)
                    gb1, gamma, beta, gb2 = (l1_gvec[:, HG * j:HG * j + (HG if j < 3 else E1)] for j in range(4))
                    with dve.Fori(0, BATCH) as b:
                        norm_vector(dve, sub, b, xn)
                        chain.start(b)
                        dve.wait_ge(main_done, b + 1)
                        for i in range(QT):
                            nc.vector.tensor_tensor(hid[:, i, :], ps[:, 4 + i, EA:EA + HG], gb1, ALU.add)
                        dve.drain()
                        for i in range(QT):
                            nc.vector.bn_stats(hstats[:, i, :], hid[:, i, :])
                        dve.drain()
                        for i in range(QT):
                            last = nc.vector.bn_aggr(hmv[:, i, :], hstats[:, i, :])
                        last.then_inc(hvar, 1)
                        for i in range(QT):
                            nc.vector.tensor_tensor(tile_of(b, i), ps[:, 2 + i, :], tile_of(b, i), ALU.add)
                            nc.vector.tensor_copy(tmp1[:, bass.ds(b * QT + i, 1), :].rearrange("p a d -> p (a d)"), ps[:, 4 + i, 0:EA])
                        dve.wait_ge(hrstd_ready, b + 1)
                        for i in range(QT):
                            last = nc.vector.tensor_scalar(hid[:, i, :], hid[:, i, :], hmv[:, i, 0:1], hrstd[:, i, :],
                                                           ALU.subtract, ALU.mult)
                        chain.link(last)
                        chain.link(nc.vector.tensor_tensor(hid[:, :, :], hid[:, :, :], gamma.unsqueeze(1).to_broadcast([P, QT, HG]), ALU.mult))
                        chain.link(nc.vector.tensor_tensor(hid[:, :, :], hid[:, :, :], beta.unsqueeze(1).to_broadcast([P, QT, HG]), ALU.add))
                        nc.vector.tensor_scalar(hid[:, :, :], hid[:, :, :], 0.0, None, ALU.max).then_inc(hid_ready, 1)
                        dve.wait_ge(logits_done, b + 1)
                        chain.link(nc.vector.tensor_tensor(logits[:, :, :], ps[:, 0:2, 0:E1], gb2.unsqueeze(1).to_broadcast([P, QT, E1]), ALU.add))
                        rank_experts(chain, E1, lower8)
                        pick = [chosen[:, bass.ds(b * QT, QT), c, :] for c in range(2)]
                        for c in range(2):
                            last = nc.vector.tensor_scalar(pick[c], ranks[:, :, :], float(c), None, ALU.is_equal)
                        chain.link(last)
                        for c in range(2):
                            last = nc.vector.tensor_tensor(beats[:, :, c * E1:(c + 1) * E1], pick[c], logits[:, :, :], ALU.mult)
                        chain.link(last)
                        chain.link(nc.vector.reduce_sum(gap[:, :, :], beats[:, :, 0:2 * E1].rearrange("p i (c e) -> p i c e", c=2), AX.X))
                        nc.vector.tensor_tensor(gap[:, :, 1], gap[:, :, 1], gap[:, :, 0], ALU.subtract).then_inc(gap_ready, 1)
                        dve.wait_ge(gap_exped, b + 1)
                        chain.link(nc.vector.tensor_scalar(gap[:, :, 0], gap[:, :, 1], 1.0, None, ALU.add))
                        chain.link(nc.vector.reciprocal(gap[:, :, 0], gap[:, :, 0]))
                        chain.link(nc.vector.tensor_copy(topg[:, bass.ds(b * QT, QT), 0], gap[:, :, 0]))
                        chain.link(nc.vector.tensor_tensor(topg[:, bass.ds(b * QT, QT), 1], gap[:, :, 0], gap[:, :, 1], ALU.mult))
                        chain.end()
                    tail = Chain(dve, tail_chain, 6)
                    tail.start(0)
                    dve.wait_ge(counted, 1)
                    tail.link(nc.vector.reduce_sum(counts[:, :], ps[:, 0, 0:TILES * 2 * E1].rearrange("p (t c) -> p c t", t=TILES), AX.X))
                    tail.link(nc.vector.tensor_scalar(counts[:, :], counts[:, :], float(CAPACITY) + 0.5, 1.0 / RANK, ALU.is_lt, ALU.mult))
                    tail.link(nc.vector.tensor_tensor(weighed[:, :, :, :].rearrange("p t c e -> p t (c e)"),
                                                      chosen[:, :, :, :].rearrange("p t c e -> p t (c e)"),
                                                      counts[:, :].unsqueeze(1).to_broadcast([P, TILES, 2 * E1]), ALU.mult))
                    tail.link(nc.vector.tensor_tensor(weighed[:, :, :, :].rearrange("p t c e -> p (t c) e"),
                                                      weighed[:, :, :, :].rearrange("p t c e -> p (t c) e"),
                                                      topg[:, :, :].rearrange("p t c -> p (t c)").unsqueeze(2).to_broadcast([P, TILES * 2, E1]),
                                                      ALU.mult))
                    tail.link(nc.vector.tensor_tensor(wexp[:, :, :], weighed[:, :, 0, :], weighed[:, :, 1, :], ALU.add))
                    t3 = tmp1[:, :, :].rearrange("p t (e r) -> p (t e) r", r=RANK)
                    nc.vector.tensor_tensor(t3, t3, wexp[:, :, :].rearrange("p t e -> p (t e)").unsqueeze(2)
                                            .to_broadcast([P, TILES * E1, RANK]), ALU.mult).then_inc(weighted, 1)
                    tail.k += 1
                    tail.end()
                    for T in range(TILES):
                        dve.wait_ge(done, T + 1)
                        nc.vector.tensor_tensor(x[:, T, :], ps[:, 4 + T % 4, :], x[:, T, :], ALU.add).then_inc(residual, 1)

                @block.scalar
                def _(act):
                    with act.Fori(0, BATCH) as b:
                        norm_scalar(act, sub, b, xT)
                        act.wait_ge(hid_flipped, b + 1)
                        nc.scalar.activation(hidT[:, :], ps[0:HG, 6, 0:SEQ], ACT.Copy).then_inc(hidT_ready, 1)
                        act.wait_ge(gap_ready, b + 1)
                        nc.scalar.activation(gap[:, :, 1], gap[:, :, 1], ACT.Exp).then_inc(gap_exped, 1)
                    for half in range(2):
                        act.wait_ge(mid_flipped, half + 1)
                        nc.scalar.activation(midT1[:, 4 * half:4 * half + 4, :], ps[:, 1 + half, :].rearrange("p (t c) -> p t c", t=4),
                                             ACT.Copy).then_inc(midT_ready, 1)

                @block.tensor
                def _(pe):
                    await_load(pe, "l1_w", "l1_ag", "l1_b", "l1_gw2")
                    with pe.Fori(0, BATCH) as b:
                        norm_tensor(pe, sub, b, xn)
                        pe.wait_ge(xT_ready, (b + sub * BATCH) * QT + QT)
                        for i in range(QT):
                            lhs = [xT[:, k, i * P:(i + 1) * P] for k in range(KC)]
                            for bank, w in ((4 + i, l1_ag), (2 + i, l1_w)):
                                n = w.shape[2]
                                for k in range(KC):
                                    last = nc.tensor.matmul(ps[:, bank, 0:n], lhs[k], w[:, k, :], start=(k == 0), stop=(k == KC - 1))
                        last.then_inc(main_done, 1)
                        pe.wait_ge(hid_ready, b + 1)
                        for i in range(QT):
                            last = nc.tensor.transpose(ps[0:HG, 6, i * P:(i + 1) * P], hid[:, i, :], ident[:, :])
                        last.then_inc(hid_flipped, 1)
                        pe.wait_ge(hidT_ready, b + 1)
                        for i in range(QT):
                            last = nc.tensor.matmul(ps[:, i, 0:E1], hidT[:, i * P:(i + 1) * P], l1_gw2[:, :], start=True, stop=True)
                        last.then_inc(logits_done, 1)
                    pe.wait_ge(ones_set, 1)
                    pe.wait_ge(chain_sem, BATCH * 15)
                    nc.tensor.matmul(ps[:, 0, 0:TILES * 2 * E1], ones[:, :], chosen[:, :, :, :].rearrange("p t c e -> p (t c e)"),
                                     start=True, stop=True).then_inc(counted, 1)
                    pe.wait_ge(weighted, 1)
                    for half in range(2):
                        for T in range(4 * half, 4 * half + 4):
                            last = nc.tensor.transpose(ps[:, 1 + half, (T % 4) * P:(T % 4 + 1) * P], tmp1[:, T, :], ident[:, :])
                        last.then_inc(mid_flipped, 1)
                    for T in range(TILES):
                        pe.wait_ge(midT_ready, T // 4 + 1)
                        if T >= 4:
                            pe.wait_ge(residual, (sub * TILES) + T - 3)
                        nc.tensor.matmul(ps[:, 4 + T % 4, :], midT1[:, T, :], l1_b[:, :], start=True, stop=True).then_inc(done, 1)

        def layer2_feed_forward(sub):
            low_done = sem("f2_low_done")
            lowT_ready = sem("f2_lowT_ready")
            zeroed = sem("f2_zeroed")
            up_done = sem("f2_up_done")
            tanhed = sem("f2_tanhed")
            half_done = sem("f2_half_done")
            gT_ready = sem("f2_gT_ready")
            low2_done = sem("f2_low2_done")
            low2_ready = sem("f2_low2_ready")
            done = sem("f2_done")

            def rows(c):
                return P if c < HC2 - 1 else HLAST2

            with nc.Block() as block:
                @block.gpsimd
                def _(pool):
                    nc.gpsimd.memset(lowT[:, :, :], 0.0).then_inc(zeroed, 1)
                    nc.gpsimd.memset(low2T[:, :], 0.0).then_inc(zeroed, 1)
                    with pool.Fori(0, BATCH) as b:
                        norm_gpsimd(pool, sub, b)

                @block.vector
                def _(dve):
                    with dve.Fori(0, BATCH) as b:
                        norm_vector(dve, sub, b, xn)
                        for c in range(HC2):
                            r, s, bank = rows(c), c % 2, 2 + c % 4
                            dve.wait_ge(tanhed, b * HC2 + (c + 1))
                            nc.vector.scalar_tensor_tensor(half_silu[0:r, s, :], tanh_[0:r, s, :], 1.0, ps[0:r, bank, 0:SEQ],
                                                           ALU.add, ALU.mult).then_inc(half_done, 1)
                            dve.wait_ge(half_done, b * HC2 + (c + 1))
                            nc.vector.scalar_tensor_tensor(gT[0:r, c, :], half_silu[0:r, s, :], 0.5, ps[0:r, bank, SEQ:2 * SEQ],
                                                           ALU.mult, ALU.mult).then_inc(gT_ready, 1)
                        dve.wait_ge(done, b + 1)
                        for i in range(QT):
                            nc.vector.tensor_tensor(tile_of(b, i), ps[:, i, :], tile_of(b, i), ALU.add).then_inc(residual, 1)

                @block.sync
                def _(sp):
                    load(sp, "lmask")

                @block.scalar
                def _(act):
                    await_load(act, "lmask")
                    act.wait_ge(zeroed, 2)
                    with act.Fori(0, BATCH) as b:
                        norm_scalar(act, sub, b, xT)
                        act.wait_ge(low_done, b + 1)
                        for j in range(2):
                            last = nc.scalar.activation(lowT[0:2 * RANK, j, :], ps[0:2 * RANK, 6, 0:SEQ], ACT.Copy, scale=lmask[:, j:j + 1])
                        last.then_inc(lowT_ready, 1)
                        for c in range(HC2):
                            r, s, bank = rows(c), c % 2, 2 + c % 4
                            act.wait_ge(up_done, b * HC2 + (c + 1))
                            if c >= 2:
                                act.wait_ge(half_done, b * HC2 + (c - 1))
                            nc.scalar.activation(tanh_[0:r, s, :], ps[0:r, bank, 0:SEQ], ACT.Tanh, scale=0.5).then_inc(tanhed, 1)
                        act.wait_ge(low2_done, b + 1)
                        nc.scalar.activation(low2T[0:RANK, :], ps[0:RANK, 7, 0:SEQ], ACT.Copy, scale=2.0).then_inc(low2_ready, 1)

                @block.tensor
                def _(pe):
                    await_load(pe, "l2_w13", "l2_w2", "l2_a13", "l2_b13", "l2_a2", "l2_b2")
                    pe.wait_ge(zeroed, 2)
                    with pe.Fori(0, BATCH) as b:
                        norm_tensor(pe, sub, b, xn)
                        pe.wait_ge(xT_ready, (b + sub * BATCH) * QT + QT)
                        for k in range(KC):
                            last = nc.tensor.matmul(ps[0:2 * RANK, 6, 0:SEQ], l2_a13[:, k, :], xT[:, k, :], start=(k == 0), stop=(k == KC - 1))
                        last.then_inc(low_done, 1)

                        def up(c):
                            r = rows(c)
                            if c >= 4:
                                pe.wait_ge(gT_ready, b * HC2 + (c - 3))
                            for j in range(2):
                                o = ps[0:r, 2 + c % 4, j * SEQ:(j + 1) * SEQ]
                                for k in range(KC):
                                    nc.tensor.matmul(o, l2_w13[:, k, j * HID2 + c * P:j * HID2 + c * P + r], xT[:, k, :], start=(k == 0), stop=False)
                                if c == 0 and j == 0:
                                    pe.wait_ge(lowT_ready, b + 1)
                                last = nc.tensor.matmul(o, l2_b13[:, c * P:c * P + r], lowT[:, j, :], start=False, stop=True)
                            last.then_inc(up_done, 1)

                        def down(c):
                            r = rows(c)
                            pe.wait_ge(gT_ready, b * HC2 + (c + 1))
                            for i in range(QT):
                                nc.tensor.matmul(ps[:, i, :], gT[0:r, c, i * P:(i + 1) * P], l2_w2[0:r, c, :], start=(c == 0), stop=False)
                            last = nc.tensor.matmul(ps[0:RANK, 7, 0:SEQ], l2_a2[0:r, c, :], gT[0:r, c, :], start=(c == 0), stop=(c == HC2 - 1))
                            if c == HC2 - 1:
                                last.then_inc(low2_done, 1)

                        for c in range(HC2 + 2):
                            if c < HC2:
                                up(c)
                            if c >= 2:
                                down(c - 2)
                        pe.wait_ge(low2_ready, b + 1)
                        for i in range(QT):
                            last = nc.tensor.matmul(ps[:, i, :], low2T[:, i * P:(i + 1) * P], l2_b2[:, :], start=False, stop=True)
                        last.then_inc(done, 1)

        def layer3_feed_forward(sub):
            lat_done = sem("f3_lat_done")
            latT_ready = sem("f3_latT_ready")
            expert_done = sem("f3_expert_done")
            expT_ready = sem("f3_expT_ready")
            up_done = sem("f3_up_done")
            relued = sem("f3_relued")
            hT_ready = sem("f3_hT_ready")
            shared_done = sem("f3_shared_done")
            shared_ready = sem("f3_shared_ready")
            chain_sem = sem("f3_chain")
            bank3_read = sem("f3_bank3_read")
            yvar = sem("f3_yvar")
            pool_chain = sem("f3_pool_chain")
            yrstd_ready = sem("f3_yrstd_ready")
            stored = sem("f3_stored")
            final = sem("f3_final")

            with nc.Block() as block:
                @block.sync
                def _(sp):
                    with sp.Fori(0, BATCH) as b:
                        for i in range(QT):
                            sp.wait_ge(final, b * QT + (i + 1))
                            sp.dma_start(out[bass.ds(b * QT + i, 1), :, :].rearrange("a p d -> p (a d)"), tile_of(b, i)).then_inc(stored, 16)
                    sp.wait_ge(stored, 16 * TILES)

                @block.gpsimd
                def _(pool):
                    with pool.Fori(0, BATCH) as b:
                        norm_gpsimd(pool, sub, b)
                        for c in range(IC3):
                            pool.wait_ge(relued, b * IC3 + (c + 1))
                            nc.gpsimd.tensor_tensor(hT[:, c, :], relu_[:, c % 2, :], relu_[:, c % 2, :], ALU.mult).then_inc(hT_ready, 1)
                        pool.wait_ge(yvar, b + 1)
                        nc.gpsimd.tensor_tensor(yrstd[:, :, 0], ymv[:, :, 1], eps[:, :].to_broadcast([P, QT]), ALU.add).then_inc(pool_chain, 1)
                        pool.wait_ge(pool_chain, b + 1)
                        nc.gpsimd.tensor_tensor(yrstd[:, :, 0], yrstd[:, :, 0], minus_half[:, :].to_broadcast([P, QT]),
                                                ALU.pow).then_inc(yrstd_ready, 1)

                @block.vector
                def _(dve):
                    await_load(dve, "l3_gb")
                    chain = Chain(dve, chain_sem, 4)
                    gamma, beta = (l3_gb[:, j * DIM:(j + 1) * DIM].unsqueeze(1).to_broadcast([P, QT, DIM]) for j in range(2))
                    with dve.Fori(0, BATCH) as b:
                        norm_vector(dve, sub, b, xn)
                        chain.start(b)
                        dve.wait_ge(lat_done, b + 1)
                        nc.vector.tensor_copy(logits[:, :, :], ps[:, 3, 0:QT * E3].rearrange("p (i e) -> p i e", i=QT)).then_inc(bank3_read, 1)
                        dve.drain()
                        for i in range(QT):
                            nc.vector.max(top8[:, i, :], logits[:, i, :])
                        dve.drain()
                        chain.link(nc.vector.tensor_tensor(routing[:, :], top8[:, :, 0], top8[:, :, 1], ALU.add))
                        for i in range(QT):
                            dve.wait_ge(shared_ready, b * QT + (i + 1))
                            nc.vector.scalar_tensor_tensor(shared[:, i, :], ps[:, 6 + i, :], routing[:, i:i + 1], shared[:, i, :],
                                                           ALU.mult, ALU.add)
                        dve.drain()
                        for i in range(QT):
                            nc.vector.bn_stats(ystats[:, i, :], shared[:, i, :])
                        dve.drain()
                        for i in range(QT):
                            last = nc.vector.bn_aggr(ymv[:, i, :], ystats[:, i, :])
                        last.then_inc(yvar, 1)
                        dve.wait_ge(yrstd_ready, b + 1)
                        for i in range(QT):
                            last = nc.vector.tensor_scalar(shared[:, i, :], shared[:, i, :], ymv[:, i, 0:1], yrstd[:, i, :],
                                                           ALU.subtract, ALU.mult)
                        chain.link(last)
                        chain.link(nc.vector.tensor_tensor(shared[:, :, :], shared[:, :, :], gamma, ALU.mult))
                        chain.link(nc.vector.tensor_tensor(shared[:, :, :], shared[:, :, :], beta, ALU.add))
                        chain.end()
                        for i in range(QT):
                            nc.vector.tensor_tensor(tile_of(b, i), shared[:, i, :], tile_of(b, i), ALU.add).then_inc(final, 1)

                @block.scalar
                def _(act):
                    with act.Fori(0, BATCH) as b:
                        norm_scalar(act, sub, b, xT)
                        act.wait_ge(lat_done, b + 1)
                        nc.scalar.activation(latT[:, :, :], ps[:, 2, :].rearrange("p (m t) -> p m t", m=LC3), ACT.Copy).then_inc(latT_ready, 1)
                        act.wait_ge(expert_done, b + 1)
                        nc.scalar.activation(expT[:, :, :], ps[:, 4, :].rearrange("p (m t) -> p m t", m=LC3), ACT.Copy).then_inc(expT_ready, 1)
                        for c in range(IC3):
                            act.wait_ge(up_done, b * IC3 + (c + 1))
                            if c >= 2:
                                act.wait_ge(hT_ready, b * IC3 + (c - 1))
                            nc.scalar.activation(relu_[:, c % 2, :], ps[:, 2 + c % 4, 0:SEQ], ACT.Relu).then_inc(relued, 1)
                        act.wait_ge(shared_done, b + 1)
                        for i in range(QT):
                            nc.scalar.activation(shared[:, i, :], ps[:, i, :], ACT.Copy).then_inc(shared_ready, 1)

                @block.tensor
                def _(pe):
                    await_load(pe, "l3_up", "l3_down", "l3_fc1", "l3_expert", "l3_fc2")
                    with pe.Fori(0, BATCH) as b:
                        norm_tensor(pe, sub, b, xn)
                        pe.wait_ge(xT_ready, (b + sub * BATCH) * QT + QT)
                        for m in range(LC3):
                            for k in range(KC):
                                nc.tensor.matmul(ps[:, 2, m * SEQ:(m + 1) * SEQ], l3_fc1[:, k, m * P:(m + 1) * P], xT[:, k, :],
                                                 start=(k == 0), stop=(k == KC - 1))
                        for i in range(QT):
                            for k in range(KC):
                                last = nc.tensor.matmul(ps[:, 3, i * E3:(i + 1) * E3], xT[:, k, i * P:(i + 1) * P],
                                                        l3_fc1[:, k, LAT3:LAT3 + E3], start=(k == 0), stop=(k == KC - 1))
                        last.then_inc(lat_done, 1)
                        pe.wait_ge(latT_ready, b + 1)
                        for m in range(LC3):
                            for l in range(LC3):
                                last = nc.tensor.matmul(ps[:, 4, m * SEQ:(m + 1) * SEQ], l3_expert[:, l, m * P:(m + 1) * P], latT[:, l, :],
                                                        start=(l == 0), stop=(l == LC3 - 1))
                        last.then_inc(expert_done, 1)
                        pe.wait_ge(expT_ready, b + 1)
                        for i in range(QT):
                            for l in range(LC3):
                                nc.tensor.matmul(ps[:, 6 + i, :], expT[:, l, i * P:(i + 1) * P], l3_fc2[:, l, :],
                                                 start=(l == 0), stop=(l == LC3 - 1))
                        pe.wait_ge(bank3_read, b + 1)

                        def up(c):
                            if c >= 4:
                                pe.wait_ge(relued, b * IC3 + (c - 3))
                            for k in range(KC):
                                last = nc.tensor.matmul(ps[:, 2 + c % 4, 0:SEQ], l3_up[:, k, c * P:(c + 1) * P], xT[:, k, :],
                                                        start=(k == 0), stop=(k == KC - 1))
                            last.then_inc(up_done, 1)

                        def down(c):
                            pe.wait_ge(hT_ready, b * IC3 + (c + 1))
                            for i in range(QT):
                                last = nc.tensor.matmul(ps[:, i, :], hT[:, c, i * P:(i + 1) * P], l3_down[:, c, :],
                                                        start=(c == 0), stop=(c == IC3 - 1))
                            if c == IC3 - 1:
                                last.then_inc(shared_done, 1)

                        for c in range(IC3 + 2):
                            if c < IC3:
                                up(c)
                            if c >= 2:
                                down(c - 2)

        val_set0 = sem("mid_zeroed")

        layer0_attention()
        layer0_feed_forward(1)
        attention(0, 2, l1_qkv, "l1_qkv", l1_wo, "l1_wo", (), ("l1_w", "l1_ag", "l1_b", "l1_gvec", "l1_gw2", "lower8", "l2_qkv", "l2_wo"))
        layer1_feed_forward(3)
        attention(1, 4, l2_qkv, "l2_qkv", l2_wo, "l2_wo", ("l2_w13", "l2_w2", "l2_a13", "l2_b13", "l2_a2", "l2_b2"), ("l3_qkv", "l3_bias"))
        layer2_feed_forward(5)
        attention(2, 6, l3_qkv, "l3_qkv", None, None, ("l3_up", "l3_down", "l3_fc1", "l3_expert", "l3_fc2", "l3_gb"), ())
        layer3_feed_forward(7)

def _chunks(w, k):
    return w.reshape(k, 128, w.shape[1]).transpose(1, 0, 2)


def _tables():
    import numpy as np

    def bf16(v):
        return (np.ascontiguousarray(v, np.float32).view(np.uint32) >> 16).astype(np.uint16)
    t = {}
    pos = np.arange(256, dtype=np.float32)
    inv = 1.0 / 500000.0 ** (np.arange(0, 128, 2, dtype=np.float32) / 128)
    wavelen = 2.0 * np.pi / inv
    scaled = np.where(wavelen > 1024 / 1.0, inv / 8.0, inv)
    smooth = (1024 / wavelen - 1.0) / (4.0 - 1.0)
    smoothed = (1.0 - smooth) / 8.0 * inv + smooth * inv
    medium = (wavelen <= 1024 / 1.0) & (wavelen >= 1024 / 4.0)
    inv0 = np.where(medium, smoothed, scaled).astype(np.float32)
    ang = (pos[:, None] * inv0[None, :]).astype(np.float32)
    t["l0_cos"] = np.concatenate([np.cos(ang), np.cos(ang)], 1).T.astype(np.float32)
    t["l0_sin"] = np.concatenate([-np.sin(ang), np.sin(ang)], 1).T.astype(np.float32)
    f = (1.0 / 10000.0 ** (np.arange(0, 16, 2, dtype=np.float32) / 16)).astype(np.float32)
    ang = (pos[:, None] * f[None, :]).astype(np.float32)
    cs = np.stack([np.concatenate([np.cos(ang), np.cos(ang)], 1),
                   np.concatenate([-np.sin(ang), np.sin(ang)], 1)], 1)
    t["rope"] = cs.reshape(2, 128, 2, 16).transpose(1, 0, 2, 3).astype(np.float32)
    t["ident"] = np.eye(128, dtype=np.float32)
    t["ident_bf"] = bf16(np.eye(128))
    i = np.arange(128)
    rows_q = np.where(i[None, :] > i[:, None], -1.0e30, 0.0)
    t["masks"] = bf16(np.stack([rows_q, rows_q.T], 1))
    hot = np.zeros((96, 32, 128), np.float32)
    for part in range(3):
        for h in range(32):
            hot[32 * part + h, h] = 1.0
    t["onehot"] = bf16(hot)
    t["lmask"] = np.repeat(np.eye(2, dtype=np.float32) * 2.0, 16, axis=0)
    for e in (4, 8):
        low = np.tril(np.ones((e, e), np.float32), -1).reshape(1, e * e)
        t[f"lower{e}"] = np.ascontiguousarray(np.broadcast_to(low, (128, e * e)))
    return {k: np.ascontiguousarray(v) for k, v in t.items()}


def _rows(v):
    import numpy as np
    return np.ascontiguousarray(np.broadcast_to(v.reshape(1, -1), (128, v.size)))


def _layout(a):
    import numpy as np
    o = {}
    o["x"] = a["L0_attn_x"].reshape(8, 128, 512)
    o["l0_wq"] = _chunks(a["L0_attn_Wq"].T, 4).reshape(128, 4, 8, 512).transpose(2, 0, 1, 3)
    o["l0_wk"] = _chunks(a["L0_attn_Wk"].T, 4)
    o["l0_wv"] = _chunks(a["L0_attn_Wv"].T, 4)
    o["l0_wo"] = a["L0_attn_Wo"].T.reshape(8, 4, 128, 512).transpose(0, 2, 1, 3)
    o["l0_ar"] = _chunks(np.concatenate([a["L0_ffn_A"].reshape(64, 512), a["L0_ffn_router_w"]], 0).T, 4)
    o["l0_b"] = np.concatenate([a["L0_ffn_B"].transpose(0, 2, 1).reshape(64, 512), np.zeros((64, 512), np.float32)], 0)
    def halves(w, n):
        return w.reshape(512, n, 8, 2).transpose(0, 1, 3, 2).reshape(512, n * 16)
    o["l1_qkv"] = _chunks(np.concatenate([halves(a["L1_attn_wq"], 32), halves(a["L1_attn_wk"], 8), a["L1_attn_wv"]], 1), 4)
    o["l1_wo"] = _chunks(a["L1_attn_wo"], 4)
    o["l1_w"] = _chunks(a["L1_ffn_weight"].T, 4)
    o["l1_ag"] = _chunks(np.concatenate([a["L1_ffn_lora_A"].transpose(1, 0, 2).reshape(512, 128), a["L1_ffn_gw1"].T], 1), 4)
    o["l1_b"] = a["L1_ffn_lora_B"].reshape(128, 512)
    o["l1_gvec"] = np.concatenate([_rows(a["L1_ffn_gb1"]), _rows(a["L1_ffn_ln_gamma"]), _rows(a["L1_ffn_ln_beta"]), _rows(a["L1_ffn_gb2"])], 1)
    o["l1_gw2"] = a["L1_ffn_gw2"].T
    o["l2_qkv"] = _chunks(np.concatenate([a["L2_attn_wq"].T, a["L2_attn_wk"].T, a["L2_attn_wv"].T], 1), 4)
    o["l2_wo"] = _chunks(a["L2_attn_wo"].T, 4)
    o["l2_w13"] = np.concatenate([_chunks(a["L2_ffn_w1"].T, 4), _chunks(a["L2_ffn_w3"].T, 4)], 2)
    w2 = np.zeros((11 * 128, 512), np.float32)
    w2[:1376] = a["L2_ffn_w2"].T
    o["l2_w2"] = _chunks(w2, 11)
    o["l2_a13"] = _chunks(np.concatenate([a["L2_ffn_lora_A1"], a["L2_ffn_lora_A3"]], 0).T, 4)
    none = np.zeros((64, 1376), np.float32)
    o["l2_b13"] = np.concatenate([a["L2_ffn_lora_B1"].T, a["L2_ffn_lora_B3"].T, none], 0)
    a2 = np.zeros((11 * 128, 16), np.float32)
    a2[:1376] = a["L2_ffn_lora_A2"].T
    o["l2_a2"] = _chunks(a2, 11)
    o["l2_b2"] = np.concatenate([a["L2_ffn_lora_B2"].T, np.zeros((80, 512), np.float32)], 0)
    wq3 = a["L3_attn_Wq"].reshape(2, 16, 16, 512).transpose(1, 0, 2, 3).reshape(512, 512)
    bq3 = a["L3_attn_bq"].reshape(2, 16, 16).transpose(1, 0, 2).reshape(512)
    o["l3_qkv"] = _chunks(np.concatenate([wq3.T, a["L3_attn_Wk"].T, a["L3_attn_Wv"].T], 1), 4)
    o["l3_bias"] = _rows(np.concatenate([bq3, a["L3_attn_bk"], a["L3_attn_bv"]]))
    o["l3_up"] = _chunks(a["L3_ffn_up_w"], 4)
    o["l3_down"] = _chunks(a["L3_ffn_down_w"], 8)
    o["l3_fc1"] = _chunks(np.concatenate([a["L3_ffn_fc1_w"], a["L3_ffn_gate_w"]], 1), 4)
    o["l3_expert"] = _chunks(a["L3_ffn_expert_w"], 2)
    o["l3_fc2"] = _chunks(a["L3_ffn_fc2_w"], 2)
    o["l3_gb"] = np.concatenate([_rows(a["L3_ffn_ln_gamma"]), _rows(a["L3_ffn_ln_beta"])], 1)
    return {k: np.ascontiguousarray(v) for k, v in o.items()}


def kernel(**inputs):
    import numpy as np
    import concourse.bacc as bacc
    from concourse import mybir as mb
    from concourse.bass_utils import run_bass_kernel_spmd

    nc = bacc.Bacc("TRN2", target_bir_lowering=False, num_devices=1)
    laid = _layout({k: np.asarray(v) for k, v in inputs.items()})
    laid.update(_tables())
    arrays, dram = {}, {}
    for name, v in laid.items():
        arrays[f"{name}_dram"] = v
        dram[name] = nc.dram_tensor(f"{name}_dram", v.shape, mb.dt.from_np(v.dtype), kind="ExternalInput").ap()
    out = nc.dram_tensor("out_dram", (8, 128, 512), mb.dt.float32, kind="ExternalOutput").ap()
    four_layers(nc, dram, out)
    r = run_bass_kernel_spmd(nc, [arrays], core_ids=[0])
    return r.results[0]["out_dram"].reshape(4, 256, 512)
```

```python
from contextlib import ExitStack

import concourse.bass as bass
from concourse import mybir

F32 = mybir.dt.float32
BF16 = mybir.dt.bfloat16
F32R = mybir.dt.float32r
ALU = mybir.AluOpType
ACT = mybir.ActivationFunctionType
AX = mybir.AxisListType

BATCH, SEQ, DIM = 4, 256, 512
P = 128
KC = DIM // P
QT = SEQ // P
TILES = BATCH * QT
EPS = 1e-5
MASKED = -1.0e30

H0, G0, D0 = 32, 8, 128
R0 = H0 // G0
SCALE0 = 1.0 / float(D0) ** 0.5
PROJ0 = G0 * (R0 + 1)

HEADS, HD = 32, 16
KV_HEADS = (8, 8, 16)
SCALES = (0.25, 0.25, 1.0 / 32.0 ** 0.5)
STACK = 6 * HD
UNITS = HEADS // 4
VPAD = 32

E0, RANK = 4, 16
E1 = 8
CAPACITY = int(3.0 * TILES * P / E1)
HID2 = 1376
HC2 = (HID2 + P - 1) // P
HLAST2 = HID2 - (HC2 - 1) * P
INT3, LAT3, E3 = 1024, 256, 8
IC3, LC3 = INT3 // P, LAT3 // P


class Chain:

    def __init__(self, eng, sem, per_turn, before=0):
        self.eng, self.sem, self.per, self.before, self.k = eng, sem, per_turn, before, 0

    def start(self, turn):
        self.turn, self.k = turn, 0

    def link(self, ins):
        self.k += 1
        ins.then_inc(self.sem, 1)
        self.eng.wait_ge(self.sem, self.turn * self.per + (self.before + self.k))

    def end(self):
        assert self.k == self.per, (self.k, self.per)


def four_layers(nc, dram, out):
    with ExitStack() as stack:
        def sem(name):
            return stack.enter_context(nc.semaphore(name))

        def keep(name, shape, dtype=F32):
            return stack.enter_context(nc.sbuf_tensor(name, shape, dtype))

        def words(t):
            return t[...].bitcast(mybir.dt.uint16) if t.dtype == BF16 else t[...]

        x = keep("x", [P, TILES, DIM])
        ident = keep("ident", [P, P])
        ident_bf = keep("ident_bf", [P, P], BF16)
        masks = keep("masks", [P, 2, P], BF16)
        stats = keep("stats", [P, QT, 6])
        mean_var = keep("mean_var", [P, QT, 2])
        rstd = keep("rstd", [P, QT, 1])
        minus_half = keep("minus_half", [P, 1])
        eps = keep("eps", [P, 1])

        base = (nc.sbuf_base + 63) // 64 * 64
        top = [base]
        where = {}

        def place(name, shape, dtype=F32, at=None):
            size = 1
            for s in shape[1:]:
                size *= s
            size = (size * (2 if dtype == BF16 else 4) + 63) // 64 * 64
            if at is None:
                at = top[0]
                top[0] += size
            where[name] = at
            return nc.alloc_sbuf_tensor_at(name, shape, dtype, offset=at), at + size

        ps = stack.enter_context(nc.psum_tensor("ps", [P, 8, 512], F32))
        ps_bf = ps[:, :, :].bitcast(BF16)

        consts_in = sem("consts_in")
        x_in = sem("x_in")
        normed = sem("normed")
        rstd_ready = sem("rstd_ready")
        var_ready = sem("var_ready")
        pool_norm_chain = sem("pool_norm_chain")
        flipped = sem("flipped")
        xT_ready = sem("xT_ready")
        residual = sem("residual")

        def updates(sub, b=0):
            return (G0 + sub - 1) * TILES + b * QT
        half_ready = sem("half_ready")

        def norm_stats(dve, sub, b):
            if sub == 0:
                dve.wait_ge(x_in, 16 * TILES)
            else:
                dve.wait_ge(residual, updates(sub))
            for i in range(QT):
                nc.vector.bn_stats(stats[:, i, :], x[:, bass.ds(b * QT + i, 1), :].rearrange("p a d -> p (a d)"))
            dve.drain()
            for i in range(QT):
                nc.vector.bn_aggr(mean_var[:, i, :], stats[:, i, :]).then_inc(var_ready, 1)

        def norm_apply(dve, sub, b, xn):
            turn = sub * BATCH + b
            for i in range(QT):
                tile = x[:, bass.ds(b * QT + i, 1), :].rearrange("p a d -> p (a d)")
                dve.wait_ge(rstd_ready, turn * QT + (i + 1))
                nc.vector.tensor_scalar(xn[:, i, :], tile, mean_var[:, i, 0:1], rstd[:, i, :],
                                        ALU.subtract, ALU.mult).then_inc(normed, 1)

        def norm_vector(dve, sub, b, xn):
            norm_stats(dve, sub, b)
            norm_apply(dve, sub, b, xn)

        def norm_gpsimd(pool, sub, b):
            turn = sub * BATCH + b
            for i in range(QT):
                pool.wait_ge(var_ready, turn * QT + (i + 1))
                nc.gpsimd.tensor_tensor(rstd[:, i, :], mean_var[:, i, 1:2], eps[:, :], ALU.add).then_inc(pool_norm_chain, 1)
                pool.wait_ge(pool_norm_chain, turn * QT + (i + 1))
                nc.gpsimd.tensor_tensor(rstd[:, i, :], rstd[:, i, :], minus_half[:, :], ALU.pow).then_inc(rstd_ready, 1)

        def norm_tensor(pe, sub, b, xn, bank=0, step=1):
            turn = sub * BATCH + b
            for i in range(QT):
                pe.wait_ge(normed, turn * QT + (i + 1))
                for k in range(KC):
                    last = nc.tensor.transpose(ps[:, bank + i * step, k * P:(k + 1) * P], xn[:, i, k * P:(k + 1) * P], ident[:, :])
                last.then_inc(flipped, 1)

        def norm_scalar(act, sub, b, xT, bank=0, step=1):
            turn = sub * BATCH + b
            for i in range(QT):
                act.wait_ge(flipped, turn * QT + (i + 1))
                nc.scalar.activation(xT[:, :, i * P:(i + 1) * P], ps[:, bank + i * step, :].rearrange("p (k t) -> p k t", k=KC),
                                     ACT.Copy).then_inc(xT_ready, 1)

        def subtract_high(eng, lo, value, hi):
            return eng.tensor_tensor(lo, value, hi.bitcast(F32), ALU.subtract)

        def product(o, lhs, rhs, start, stop):
            nc.tensor.matmul(o, lhs[0], rhs[0], start=start, stop=False)
            nc.tensor.matmul(o, lhs[0], rhs[1], start=False, stop=False)
            return nc.tensor.matmul(o, lhs[1], rhs[0], start=False, stop=stop)

        def split_xT(dve, sub, b, hi, lo, bank, ready, step=1):
            for i in range(QT):
                dve.wait_ge(xT_ready, (sub * BATCH + b) * QT + (i + 1))
                subtract_high(nc.vector, lo[:, :, i * P:(i + 1) * P], ps[:, bank + i * step, :].rearrange("p (k t) -> p k t", k=KC),
                              hi[:, :, i * P:(i + 1) * P]).then_inc(ready, 1)

        def layer0_attention():
            PAIRS0 = G0 // 2
            top[0] = base
            wq, _ = place("l0_wq", [P, 2, KC, R0 * D0])
            wk, _ = place("l0_wk", [P, 2, KC, D0])
            wo, _ = place("l0_wo", [P, 2, R0, DIM])
            wv, _ = place("l0_wv", [P, KC, 2 * D0])
            wq_lo, _ = place("l0_wq_lo", [P, 2, KC, R0 * D0], F32R, at=where["l0_wq"])
            wk_lo, _ = place("l0_wk_lo", [P, 2, KC, D0], F32R, at=where["l0_wk"])
            wo_lo, _ = place("l0_wo_lo", [P, 2, R0, DIM], F32R, at=where["l0_wo"])
            wv_lo, _ = place("l0_wv_lo", [P, KC, 2 * D0], F32R, at=where["l0_wv"])
            wq_hi, _ = place("l0_wq_hi", [P, 2, KC, R0 * D0], F32R)
            wk_hi, _ = place("l0_wk_hi", [P, 2, KC, D0], F32R)
            wo_hi, _ = place("l0_wo_hi", [P, 2, R0, DIM], F32R)
            wv_hi, _ = place("l0_wv_hi", [P, KC, 2 * D0], F32R)
            cos, _ = place("l0_cos", [P, SEQ])
            sin, _ = place("l0_sin", [P, SEQ])
            xT_hi, _ = place("l0_xT_hi", [P, KC, BATCH * SEQ], F32R)
            xT_lo, _ = place("l0_xT_lo", [P, KC, BATCH * SEQ], F32R)
            val, _ = place("l0_val", [P, BATCH, QT, 2 * D0])
            qT, _ = place("l0_qT", [P, R0, SEQ])
            kT, _ = place("l0_kT", [P, 2, SEQ])
            t_sin, _ = place("l0_t_sin", [P, 2, SEQ])
            oT_hi, _ = place("l0_oT_hi", [P, 2, SEQ], F32R)
            oT_lo, _ = place("l0_oT_lo", [P, 2, SEQ], F32R)
            rowmax, _ = place("l0_rowmax", [P, 2, QT])
            rowsum, _ = place("l0_rowsum", [P, 2, QT])
            prob, _ = place("l0_prob", [P, 2, 3 * P])
            probT, _ = place("l0_probT", [P, 2, 3 * P])
            xn, _ = place("l0_xn", [P, QT, DIM])

            wqk_in = [sem(f"l0_wqk_in{s}") for s in range(2)]
            wo_in = [sem(f"l0_wo_in{s}") for s in range(2)]
            wv_in = sem("l0_wv_in")
            hi_cut = sem("l0_hi_cut")
            lo_cut = sem("l0_lo_cut")
            xT_lo_ready = sem("l0_xT_lo_ready")
            v_done = sem("l0_v_done")
            v_kept = sem("l0_v_kept")
            projected = sem("l0_projected")
            rope_muled = sem("l0_rope_muled")
            roped = sem("l0_roped")
            scored = sem("l0_scored")
            max_chain = sem("l0_max_chain")
            max_ready = sem("l0_max_ready")
            exped = sem("l0_exped")
            sum_inverted = sem("l0_sum_inverted")
            scaled = sem("l0_scaled")
            prob_flipped = sem("l0_prob_flipped")
            probT_ready = sem("l0_probT_ready")
            attended = sem("l0_attended")
            oT_hi_ready = sem("l0_oT_hi_ready")
            oT_ready = sem("l0_oT_ready")
            out_used = sem("l0_out_used")

            PROJ, SCORE, FLIP, OUT, ACC = 6, 2, 4, 5, 0
            UNITS0 = 2 * BATCH
            HEADS0 = UNITS0 * R0
            ORDER = [(u, h) for u in range(UNITS0) for h in [None] + list(range(R0))]
            PROJ0 = len(ORDER)

            def place_of(n):
                return (n // R0) * (R0 + 1) + 1 + n % R0

            CUTS = (("qk", 1, 7, False), ("o", 1, 11, False), ("v", 0, 17, True), ("qk", 0, 22, True), ("o", 0, 26, True))
            PER_TURN = 4 * len(CUTS)
            BEFORE = (("v", 0), ("qk", 0), ("o", 0))

            def cut_ready(p, kind, s):
                order = [(kind_, s_) for kind_, s_ in BEFORE] + [("qk", 1), ("o", 1)]
                return p * PER_TURN + 4 * (order.index((kind, s)) + 1)

            def pieces(kind, s, k):
                if kind == "v":
                    return [(wv[:, k, :], wv_hi[:, k, :], wv_lo[:, k, :])]
                if kind == "o":
                    return [(wo[:, s, k, :], wo_hi[:, s, k, :], wo_lo[:, s, k, :])]
                return [(wq[:, s, k, :], wq_hi[:, s, k, :], wq_lo[:, s, k, :]), (wk[:, s, k, :], wk_hi[:, s, k, :], wk_lo[:, s, k, :])]

            def step_at(n, more):
                for j, (kind, s, at, following) in enumerate(CUTS):
                    if at <= n < at + 4 and (more or not following):
                        return 4 * (len(BEFORE) + j) + n - at, kind, s, n - at, following
                return None

            def each_pair(eng, turn_of):
                with eng.Fori(0, PAIRS0 - 1) as p:
                    turn_of(p, True)
                turn_of(PAIRS0 - 1, False)

            with nc.Block() as block:
                @block.sync
                def _(sp):
                    def load_group(g, s):
                        for dst, name, arrived_ in ((wk, "l0_wk", wqk_in[s]), (wq, "l0_wq", wqk_in[s]), (wo, "l0_wo", wo_in[s])):
                            sp.dma_start(dst[:, s, :, :], dram[name][bass.ds(g, 1), :, :, :].rearrange("a p k n -> p (a k) n"))\
                                .then_inc(arrived_, 16)

                    for T in range(TILES):
                        sp.dma_start(x[:, T, :], dram["x"][T, :, :]).then_inc(x_in, 16)
                        if T == 1:
                            for dst, name in ((ident, "ident"), (ident_bf, "ident_bf"), (masks, "masks"), (cos, "l0_cos"), (sin, "l0_sin")):
                                sp.dma_start(words(dst), dram[name]).then_inc(consts_in, 16)
                    sp.dma_start(wv[:, :, :], dram["l0_wv"][0, :, :, :]).then_inc(wv_in, 16)
                    for s in range(2):
                        load_group(s, s)
                    with sp.Fori(0, PAIRS0 - 1) as p:
                        sp.wait_ge(v_done, p * 4 + 4)
                        sp.dma_start(wv[:, :, :], dram["l0_wv"][bass.ds(p + 1, 1), :, :, :].rearrange("a p k n -> p (a k) n")).then_inc(wv_in, 16)
                        for s in range(2):
                            sp.wait_ge(out_used, p * HEADS0 + 16 * (s + 1))
                            load_group(2 * p + (2 + s), s)

                @block.gpsimd
                def _(pool):
                    nc.gpsimd.memset(minus_half[:, :], -0.5).then_inc(half_ready, 1)
                    nc.gpsimd.memset(eps[:, :], EPS).then_inc(half_ready, 1)
                    pool.wait_ge(half_ready, 2)
                    for b in range(BATCH):
                        norm_gpsimd(pool, 0, b)
                    with pool.Fori(0, PAIRS0) as p:
                        def add_rope(u):
                            g, h = ORDER[u]
                            pool.wait_ge(rope_muled, p * PROJ0 + (u + 1))
                            dst = kT[:, g % 2, :] if h is None else qT[:, h, :]
                            nc.gpsimd.tensor_tensor(dst, dst, t_sin[:, u % 2, :], ALU.add).then_inc(roped, 1)

                        add_rope(0)
                        add_rope(1)
                        for n in range(HEADS0):
                            if n + 1 < HEADS0:
                                if (n + 1) % R0 == 0:
                                    add_rope(place_of(n + 1) - 1)
                                add_rope(place_of(n + 1))
                            s = n % 2
                            pool.wait_ge(sum_inverted, p * HEADS0 + (n + 1))
                            nc.gpsimd.tensor_tensor(prob[:, s, 0:P], prob[:, s, 0:P],
                                                    rowsum[:, s, 0:1].to_broadcast([P, P]), ALU.mult)
                            nc.gpsimd.tensor_tensor(prob[:, s, P:3 * P], prob[:, s, P:3 * P],
                                                    rowsum[:, s, 1:2].to_broadcast([P, 2 * P]), ALU.mult).then_inc(scaled, 1)

                @block.vector
                def _(dve):
                    def cut(number, kind, s, k):
                        dve.wait_ge(hi_cut, number + 1)
                        for value, hi, lo in pieces(kind, s, k):
                            last = subtract_high(nc.vector, lo, value, hi)
                        last.then_inc(lo_cut, 1)

                    def keep_out_low(p, n):
                        dve.wait_ge(oT_hi_ready, p * HEADS0 + (n + 1))
                        subtract_high(nc.vector, oT_lo[:, n % 2, :], ps[:, OUT, 0:SEQ], oT_hi[:, n % 2, :]).then_inc(oT_ready, 1)

                    def add_unit(p, u, more):
                        dve.wait_ge(out_used, p * HEADS0 + R0 * (u + 1))
                        if u > 0:
                            dve.wait_ge(residual, p * (2 * UNITS0) + 2 * u)
                        b = u % BATCH
                        for i in range(QT):
                            tile = x[:, b * QT + i, :]
                            last = nc.vector.tensor_tensor(tile, ps[:, ACC + i, :], tile, ALU.add).then_inc(residual, 1)

                    def turn_of(p, more):
                        def mul_rope(u):
                            s = u % 2
                            pr = ps[:, PROJ + s, 0:SEQ]
                            dve.wait_ge(projected, p * PROJ0 + (u + 1))
                            if u >= 2:
                                dve.wait_ge(roped, p * PROJ0 + (u - 1))
                            g, h = ORDER[u]
                            if h is None and g >= 2:
                                dve.wait_ge(scored, p * HEADS0 + R0 * (g - 1))
                            if h is not None and g >= 1:
                                dve.wait_ge(scored, p * HEADS0 + (g * R0 + h - R0 + 1))
                            dst = kT[:, g % 2, :] if h is None else qT[:, h, :]
                            nc.vector.tensor_tensor(dst, pr, cos[:, :], ALU.mult)
                            nc.vector.tensor_tensor(t_sin[0:64, s, :], ps[64:128, PROJ + s, 0:SEQ], sin[0:64, :], ALU.mult)
                            nc.vector.tensor_tensor(t_sin[64:128, s, :], ps[0:64, PROJ + s, 0:SEQ], sin[64:128, :],
                                                    ALU.mult).then_inc(rope_muled, 1)

                        mul_rope(0)
                        mul_rope(1)
                        for n in range(HEADS0):
                            s = n % 2
                            dve.wait_ge(scored, p * HEADS0 + (n + 1))
                            nc.vector.reduce_max(rowmax[:, s, 0:1], ps[:, SCORE + s, 0:P], AX.X).then_inc(max_chain, 1)
                            nc.vector.reduce_max(rowmax[:, s, 1:2], ps[:, SCORE + s, P:3 * P], AX.X).then_inc(max_chain, 1)
                            dve.wait_ge(max_chain, p * (2 * HEADS0) + 2 * (n + 1))
                            nc.vector.tensor_scalar(rowmax[:, s, :], rowmax[:, s, :], -SCALE0, None, ALU.mult).then_inc(max_ready, 1)
                            if n + 1 < HEADS0:
                                if (n + 1) % R0 == 0:
                                    mul_rope(place_of(n + 1) - 1)
                                mul_rope(place_of(n + 1))
                            if n >= 1:
                                keep_out_low(p, n - 1)
                            if n >= 5 and (n - 1) % R0 == 0:
                                add_unit(p, (n - 2) // R0, more)
                            dve.wait_ge(exped, p * HEADS0 + (n + 1))
                            nc.vector.reciprocal(rowsum[:, s, :], rowsum[:, s, :]).then_inc(sum_inverted, 1)
                            step = step_at(n, more)
                            if step:
                                number, kind, group, k, _ = step
                                cut(p * PER_TURN + number, kind, group, k)
                        keep_out_low(p, HEADS0 - 1)
                        add_unit(p, UNITS0 - 1, more)
                        dve.wait_ge(residual, (p + 1) * (2 * UNITS0))

                    dve.wait_ge(consts_in, 16 * 5)
                    for b in range(BATCH):
                        norm_stats(dve, 0, b)
                        if b > 0:
                            split_xT(dve, 0, b - 1, xT_hi[:, :, (b - 1) * SEQ:b * SEQ], xT_lo[:, :, (b - 1) * SEQ:b * SEQ],
                                     2 * ((b - 1) % 2), xT_lo_ready)
                        norm_apply(dve, 0, b, xn)
                    split_xT(dve, 0, BATCH - 1, xT_hi[:, :, (BATCH - 1) * SEQ:], xT_lo[:, :, (BATCH - 1) * SEQ:],
                             2 * ((BATCH - 1) % 2), xT_lo_ready)
                    for j, (kind, s) in enumerate(BEFORE):
                        for k in range(4):
                            cut(4 * j + k, kind, s, k)
                    each_pair(dve, turn_of)

                @block.scalar
                def _(act):
                    def await_weights(turn, kind, s):
                        if kind == "qk":
                            act.wait_ge(wqk_in[s], turn * 32 + 32)
                        else:
                            act.wait_ge(wo_in[s] if kind == "o" else wv_in, turn * 16 + 16)

                    def cut(kind, s, k):
                        for value, hi, lo in pieces(kind, s, k):
                            last = nc.scalar.activation(hi, value, ACT.Copy)
                        last.then_inc(hi_cut, 1)

                    def turn_of(p, more):
                        for c in range(BATCH):
                            act.wait_ge(v_done, p * BATCH + (c + 1))
                            nc.scalar.activation(val[:, c, :, :].rearrange("p i d -> p (i d)"), ps[:, 2 + c, :], ACT.Copy).then_inc(v_kept, 1)

                        def keep_probT(n):
                            act.wait_ge(prob_flipped, p * HEADS0 + (n + 1))
                            if n >= 2:
                                act.wait_ge(attended, p * HEADS0 + (n - 1))
                            nc.scalar.activation(probT[:, n % 2, :], ps[:, FLIP, 0:3 * P], ACT.Copy).then_inc(probT_ready, 1)

                        def keep_out_high(n):
                            act.wait_ge(attended, p * HEADS0 + (n + 1))
                            if n >= 2:
                                act.wait_ge(out_used, p * HEADS0 + (n - 1))
                            nc.scalar.activation(oT_hi[:, n % 2, :], ps[:, OUT, 0:SEQ], ACT.Copy).then_inc(oT_hi_ready, 1)

                        for n in range(HEADS0):
                            s = n % 2
                            act.wait_ge(max_ready, p * HEADS0 + (n + 1))
                            if n >= 2:
                                act.wait_ge(prob_flipped, p * HEADS0 + (n - 1))
                            nc.scalar.activation(prob[:, s, 0:P], ps[:, SCORE + s, 0:P], ACT.Exp, bias=rowmax[:, s, 0:1],
                                                 scale=SCALE0, accum_out=rowsum[:, s, 0:1])
                            nc.scalar.activation(prob[:, s, P:3 * P], ps[:, SCORE + s, P:3 * P], ACT.Exp, bias=rowmax[:, s, 1:2],
                                                 scale=SCALE0, accum_out=rowsum[:, s, 1:2]).then_inc(exped, 1)
                            if n >= 1:
                                keep_probT(n - 1)
                                keep_out_high(n - 1)
                            step = step_at(n, more)
                            if step:
                                number, kind, group, k, following = step
                                if k == 0:
                                    await_weights(p + 1 if following else p, kind, group)
                                cut(kind, group, k)
                        keep_probT(HEADS0 - 1)
                        keep_out_high(HEADS0 - 1)

                    for b in range(BATCH):
                        norm_scalar(act, 0, b, xT_hi[:, :, b * SEQ:(b + 1) * SEQ], 2 * (b % 2))
                    for kind, s in BEFORE:
                        await_weights(0, kind, s)
                        for k in range(4):
                            cut(kind, s, k)
                    each_pair(act, turn_of)

                @block.tensor
                def _(pe):
                    def turn_of(p, more):
                        pe.wait_ge(lo_cut, cut_ready(p, "v", 0))
                        for c in range(BATCH):
                            pe.wait_ge(xT_lo_ready, QT * (c + 1))
                            for i in range(QT):
                                at = slice(c * SEQ + i * P, c * SEQ + (i + 1) * P)
                                for k in range(KC):
                                    last = product(ps[:, 2 + c, i * 2 * D0:(i + 1) * 2 * D0], (xT_hi[:, k, at], xT_lo[:, k, at]),
                                                   (wv_hi[:, k, :], wv_lo[:, k, :]), k == 0, k == KC - 1)
                            last.then_inc(v_done, 1)

                        def project(u):
                            unit, h = ORDER[u]
                            s, b = unit // BATCH, unit % BATCH
                            if u >= 2:
                                pe.wait_ge(rope_muled, p * PROJ0 + (u - 1))
                            if h is None and b == 0:
                                pe.wait_ge(lo_cut, cut_ready(p, "qk", s))
                            tokens = slice(b * SEQ, (b + 1) * SEQ)
                            for k in range(KC):
                                w = [t[:, s, k, :] for t in (wk_hi, wk_lo)] if h is None else \
                                    [t[:, s, k, h * D0:(h + 1) * D0] for t in (wq_hi, wq_lo)]
                                last = product(ps[:, PROJ + u % 2, 0:SEQ], w, (xT_hi[:, k, tokens], xT_lo[:, k, tokens]), k == 0, k == KC - 1)
                            last.then_inc(projected, 1)

                        def score(n):
                            g, s = n // R0, n % 2
                            pe.wait_ge(roped, p * PROJ0 + (place_of(n) + 1))
                            if n >= 2:
                                pe.wait_ge(exped, p * HEADS0 + (n - 1))
                            q, k_, bank = qT[:, n % R0, :], kT[:, g % 2, :], ps[:, SCORE + s, :]
                            nc.tensor.matmul(bank[:, 0:P], q[:, 0:P], k_[:, 0:P], start=True, stop=False)
                            nc.tensor.matmul(bank[:, 0:P], ident_bf[:, :], masks[:, 0, :], start=False, stop=True)
                            nc.tensor.matmul(bank[:, P:3 * P], q[:, P:SEQ], k_, start=True, stop=False)
                            nc.tensor.matmul(bank[:, 2 * P:3 * P], ident_bf[:, :], masks[:, 0, :], start=False,
                                             stop=True).then_inc(scored, 1)

                        def flip(n):
                            pe.wait_ge(scaled, p * HEADS0 + (n + 1))
                            if n >= 1:
                                pe.wait_ge(probT_ready, p * HEADS0 + n)
                            for c in range(3):
                                last = nc.tensor.transpose(ps[:, FLIP, c * P:(c + 1) * P], prob[:, n % 2, c * P:(c + 1) * P], ident[:, :])
                            last.then_inc(prob_flipped, 1)

                        def attend(n):
                            unit, slot = n // R0, n % 2
                            s, b = unit // BATCH, unit % BATCH
                            pe.wait_ge(probT_ready, p * HEADS0 + (n + 1))
                            if n >= 1:
                                pe.wait_ge(oT_ready, p * HEADS0 + n)
                            nc.tensor.matmul(ps[:, OUT, 0:2 * P], val[:, b, 0, s * D0:(s + 1) * D0], probT[:, slot, 0:2 * P],
                                             start=True, stop=False)
                            nc.tensor.matmul(ps[:, OUT, P:2 * P], val[:, b, 1, s * D0:(s + 1) * D0], probT[:, slot, 2 * P:3 * P],
                                             start=False, stop=True).then_inc(attended, 1)

                        def project_out(n):
                            unit, h = n // R0, n % R0
                            s = unit // BATCH
                            pe.wait_ge(oT_ready, p * HEADS0 + (n + 1))
                            if n % (R0 * BATCH) == 0:
                                pe.wait_ge(lo_cut, cut_ready(p, "o", s))
                            if h == 0 and unit > 0:
                                pe.wait_ge(residual, p * (2 * UNITS0) + 2 * unit)
                            for i in range(QT):
                                at = slice(i * P, (i + 1) * P)
                                last = product(ps[:, ACC + i, :], (oT_hi[:, n % 2, at], oT_lo[:, n % 2, at]),
                                               (wo_hi[:, s, h, :], wo_lo[:, s, h, :]), h == 0, h == R0 - 1)
                            last.then_inc(out_used, 1)

                        project(0)
                        project(1)
                        for n in range(HEADS0 + 2):
                            if n < HEADS0:
                                if n == 0:
                                    pe.wait_ge(v_kept, p * BATCH + BATCH)
                                score(n)
                            if n + 1 < HEADS0:
                                if (n + 1) % R0 == 0:
                                    project(place_of(n + 1) - 1)
                                project(place_of(n + 1))
                            if 1 <= n <= HEADS0:
                                flip(n - 1)
                            if n >= 2:
                                project_out(n - 2)
                            if 1 <= n <= HEADS0:
                                attend(n - 1)

                    pe.wait_ge(consts_in, 16 * 5)
                    for b in range(BATCH):
                        if b >= 2:
                            pe.wait_ge(xT_lo_ready, QT * (b - 1))
                        norm_tensor(pe, 0, b, xn, 2 * (b % 2))
                    each_pair(pe, turn_of)

        top[0] = base
        l0_ar, _ = place("l0_ar", [P, KC, E0 * RANK + E0])
        l0_b, _ = place("l0_b", [P, DIM])
        l1_qkv, _ = place("l1_qkv", [P, KC, DIM + 2 * KV_HEADS[0] * HD])
        l1_wo, _ = place("l1_wo", [P, KC, DIM])
        l1_w, _ = place("l1_w", [P, KC, DIM])
        l1_ag, _ = place("l1_ag", [P, KC, E1 * RANK + 4 * E1])
        l1_b, _ = place("l1_b", [P, DIM])
        l1_gvec, _ = place("l1_gvec", [P, 3 * 4 * E1 + E1])
        l1_gw2, _ = place("l1_gw2", [4 * E1, E1])
        top[0] = base
        l2_w13, _ = place("l2_w13", [P, KC, 2 * HID2])
        l2_w2, _ = place("l2_w2", [P, HC2, DIM])
        l2_a13, _ = place("l2_a13", [P, KC, 96])
        l2_b13, _ = place("l2_b13", [96, HID2])
        l2_a2, _ = place("l2_a2", [P, HC2, RANK])
        l2_b2, _ = place("l2_b2", [96, DIM])
        after = top[0]
        top[0] = base
        l3_up, _ = place("l3_up", [P, KC, INT3])
        l3_down, _ = place("l3_down", [P, IC3, DIM])
        l3_fc1, _ = place("l3_fc1", [P, KC, LAT3 + E3])
        l3_expert, _ = place("l3_expert", [P, LC3, LAT3])
        l3_fc2, _ = place("l3_fc2", [P, LC3, DIM])
        l3_gb, behind3 = place("l3_gb", [P, 2 * DIM])
        top[0] = after
        l2_qkv, _ = place("l2_qkv", [P, KC, DIM + 2 * KV_HEADS[1] * HD])
        l2_wo, _ = place("l2_wo", [P, KC, DIM])
        rope, _ = place("rope", [P, QT, 2, HD])
        lower4, _ = place("lower4", [P, E0 * E0])
        lower8, _ = place("lower8", [P, E1 * E1])
        work = top[0]
        l3_qkv, top[0] = place("l3_qkv", [P, KC, DIM + 2 * KV_HEADS[2] * HD], at=after)
        l3_bias, top[0] = place("l3_bias", [P, DIM + 2 * KV_HEADS[2] * HD], at=top[0])
        assert top[0] <= after + 20 * 1024

        tensors = dict(l0_ar=l0_ar, l0_b=l0_b, lower4=lower4, l1_qkv=l1_qkv, rope=rope, l1_wo=l1_wo,
                       l1_w=l1_w, l1_ag=l1_ag, l1_b=l1_b, l1_gvec=l1_gvec, l1_gw2=l1_gw2,
                       lower8=lower8, l2_qkv=l2_qkv, l2_wo=l2_wo, l3_qkv=l3_qkv, l3_bias=l3_bias,
                       l2_w13=l2_w13, l2_w2=l2_w2, l2_a13=l2_a13, l2_b13=l2_b13, l2_a2=l2_a2, l2_b2=l2_b2,
                       l3_up=l3_up, l3_down=l3_down, l3_fc1=l3_fc1, l3_expert=l3_expert, l3_fc2=l3_fc2, l3_gb=l3_gb)
        arrived, arriving = {}, {}

        def load(sp, group, *names):
            for name in names:
                sp.dma_start(words(tensors[name]), dram[name]).then_inc(arrived[group], 16)

        def group_of(group, *names):
            arrived[group], arriving[group] = sem(f"{group}_in"), names

        for group, names in (("f0", ("l0_ar", "l0_b", "lower4")),
                             ("a1", ("l1_qkv", "rope", "l1_wo")),
                             ("f1", ("l1_w", "l1_ag", "l1_b", "l1_gvec", "l1_gw2", "lower8")),
                             ("a2", ("l2_qkv", "l2_wo")),
                             ("f2", ("l2_w13", "l2_w2", "l2_a13", "l2_b13", "l2_a2", "l2_b2")),
                             ("f2_mask", ("lmask",)),
                             ("a3", ("l3_qkv",)),
                             ("a3_bias", ("l3_bias",)),
                             ("f3", ("l3_up", "l3_down", "l3_fc1", "l3_expert", "l3_fc2", "l3_gb"))):
            group_of(group, *names)

        def load_groups(sp, *groups):
            for group in groups:
                load(sp, group, *arriving[group])

        def await_group(eng, group):
            eng.wait_ge(arrived[group], 16 * len(arriving[group]))

        top[0] = work
        xn, _ = place("xn", [P, QT, DIM])
        xT, _ = place("xT", [P, KC, SEQ])
        attn, _ = place("attn", [P, QT, DIM], at=work)
        aT, _ = place("aT", [P, KC, SEQ], at=work + QT * DIM * 4)
        oT, _ = place("oT", [P, UNITS, SEQ])
        SHIFT = STACK
        qsT, _ = place("qsT", [P, HEADS, SEQ], BF16)
        ksT, _ = place("ksT", [P, 16, SEQ], BF16)
        val, _ = place("val", [P, QT, 16, VPAD])
        vf, _ = place("vf", [P, QT, 256])
        negmaxT, _ = place("negmaxT", [96, SEQ], BF16)
        negmax, _ = place("negmax", [P, QT, 3, HEADS], BF16)
        rowmax, _ = place("rowmax", [P, QT, HEADS])
        maxrest, _ = place("maxrest", [P, QT, HEADS])
        rowrcp, _ = place("rowrcp", [P, QT, HEADS])
        qs, _ = place("qs", [P, QT, HEADS, STACK], BF16)
        ks, _ = place("ks", [P, QT, 16, STACK], BF16)
        probT, _ = place("probT", [P, 4, 3 * SEQ])
        qf, _ = place("qf", [P, QT, DIM])
        kf, _ = place("kf", [P, QT, 256])
        rot, _ = place("rot", [P, DIM + 256])
        rest, _ = place("rest", [P, DIM + 256])

        PAIRS = HEADS // 2
        qkv_done = sem("qkv_done")
        v_staged = sem("v_staged")
        rope_muled = sem("rope_muled")
        qk_float = sem("qk_float")
        part_cut = sem("part_cut")
        rest_ready = sem("rest_ready")
        stack_flipped = sem("stack_flipped")
        stackT_vector = sem("stackT_vector")
        stackT_scalar = sem("stackT_scalar")
        val_ready = sem("val_ready")
        scored = sem("scored")
        maxed = sem("maxed")
        max_chain = sem("max_chain")
        negmax_ready = sem("negmax_ready")
        negmax_flipped = sem("negmax_flipped")
        negmaxT_ready = sem("negmaxT_ready")
        shift_in = sem("shift_in")
        key_scored = sem("key_scored")
        exped = sem("exped")
        attended = sem("attended")
        oT_ready = sem("oT_ready")
        o_flipped = sem("o_flipped")
        rcp_chain = sem("rcp_chain")
        attn_ready = sem("attn_ready")
        attn_flipped = sem("attn_flipped")
        aT_ready = sem("aT_ready")
        out_done = sem("out_done")
        val_set = sem("val_set")

        def attention(a, sub, wqkv, wo, weights, bias, early_loads):
            kv = KV_HEADS[a]
            rep = HEADS // kv
            kvd = kv * HD
            rotary = wo is not None
            t0 = a * BATCH
            SU = kv // 8 + 4
            su0 = t0 * 5
            SORDER = [(i, kind, c) for i in range(QT) for kind, c in
                      [("k", c) for c in range(kv // 8)] + [("q", c) for c in range(4)]]

            with nc.Block() as block:
                @block.sync
                def _(sp):
                    load_groups(sp, *early_loads)
                    with sp.Fori(0, BATCH) as b:
                        turn = b + t0
                        sp.wait_ge(negmaxT_ready, turn * QT + QT)
                        sp.dma_start(qsT[SHIFT:SHIFT + 3, :, :], negmaxT[:, :]).then_inc(shift_in, 16)

                @block.gpsimd
                def _(pool):
                    nc.gpsimd.memset(val[:, :, :, HD:VPAD], 0.0).then_inc(val_set, 1)
                    pool.wait_ge(val_set, 3 * a + 1)
                    nc.gpsimd.memset(val[:, :, :, HD:HD + 1], 1.0).then_inc(val_set, 1)
                    pool.wait_ge(val_set, 3 * a + 2)
                    nc.gpsimd.memset(ksT[SHIFT:SHIFT + 3, :, :], 1.0).then_inc(val_set, 1)
                    pool.wait_ge(val_set, 3 * a + 3)

                    def front(b):
                        norm_gpsimd(pool, sub, b)
                        turn = b + t0
                        for i in range(QT):
                            if rotary:
                                pool.wait_ge(rope_muled, turn * QT + (i + 1))
                                nc.gpsimd.tensor_tensor(qf[:, i, :], qf[:, i, :], rot[:, 0:DIM], ALU.add)
                                nc.gpsimd.tensor_tensor(kf[:, i, 0:kvd], kf[:, i, 0:kvd], rot[:, DIM:DIM + kvd],
                                                        ALU.add).then_inc(qk_float, 1)
                            pool.wait_ge(part_cut, turn * 6 + (3 * i + 1))
                            restq = rest[:, 0:DIM].rearrange("p (h d) -> p h d", d=HD)
                            restk = rest[:, DIM:DIM + kvd].rearrange("p (h d) -> p h d", d=HD)
                            nc.gpsimd.tensor_tensor(restq, qf[:, i, :].rearrange("p (h d) -> p h d", d=HD),
                                                    qs[:, i, :, 0:HD], ALU.subtract)
                            nc.gpsimd.tensor_tensor(restk, kf[:, i, 0:kvd].rearrange("p (h d) -> p h d", d=HD),
                                                    ks[:, i, 0:kv, HD:2 * HD], ALU.subtract).then_inc(rest_ready, 1)
                            pool.wait_ge(part_cut, turn * 6 + (3 * i + 2))
                            nc.gpsimd.tensor_tensor(restq, restq, qs[:, i, :, 3 * HD:4 * HD], ALU.subtract)
                            nc.gpsimd.tensor_tensor(restk, restk, ks[:, i, 0:kv, 2 * HD:3 * HD],
                                                    ALU.subtract).then_inc(rest_ready, 1)

                    front(0)
                    with pool.Fori(1, BATCH) as b:
                        front(b)

                @block.vector
                def _(dve):
                    def front_rope(b, i):
                        turn = b + t0
                        dve.wait_ge(qkv_done, turn * QT + (i + 1))
                        pq, pk = ps[:, 6, :], ps[:, 7, 0:kvd]
                        if rotary:
                            if i == 1:
                                dve.wait_ge(qk_float, turn * QT + 1)
                            cos = rope[:, i, 0:1, :]
                            for src, dst, tmp, n in ((pq, qf[:, i, :], rot[:, 0:DIM], HEADS),
                                                     (pk, kf[:, i, 0:kvd], rot[:, DIM:DIM + kvd], kv)):
                                s3 = src.rearrange("p (h d) -> p h d", d=HD)
                                t3 = tmp.rearrange("p (h d) -> p h d", d=HD)
                                nc.vector.tensor_tensor(dst.rearrange("p (h d) -> p h d", d=HD), s3,
                                                        cos.to_broadcast([P, n, HD]), ALU.mult)
                                nc.vector.tensor_tensor(t3[:, :, 0:8], s3[:, :, 8:16],
                                                        rope[:, i, 1:2, 0:8].to_broadcast([P, n, 8]), ALU.mult)
                                last = nc.vector.tensor_tensor(t3[:, :, 8:16], s3[:, :, 0:8],
                                                               rope[:, i, 1:2, 8:16].to_broadcast([P, n, 8]), ALU.mult)
                            last.then_inc(rope_muled, 1)
                        else:
                            nc.vector.tensor_tensor(qf[:, i, :], pq, l3_bias[:, 0:DIM], ALU.add)
                            nc.vector.tensor_tensor(vf[:, i, 0:kvd], ps[:, 7, kvd:2 * kvd], l3_bias[:, DIM + kvd:DIM + 2 * kvd],
                                                    ALU.add).then_inc(v_staged, 1)
                            nc.vector.tensor_tensor(kf[:, i, 0:kvd], pk, l3_bias[:, DIM:DIM + kvd], ALU.add).then_inc(qk_float, 1)

                    def front_stack(b, us):
                        for u in us:
                            i, kind, c = SORDER[u]
                            dst = (ksT if kind == "k" else qsT)[0:STACK, 8 * c:8 * c + 8, i * P:(i + 1) * P]
                            dve.wait_ge(stack_flipped, b * (2 * SU) + (2 * su0 + u + 1))
                            nc.vector.tensor_copy(dst, ps_bf[0:STACK, u % 4, :].rearrange("p (h t) -> p h t", t=P))\
                                .then_inc(stackT_vector, 1)

                    def row_maxima(b, i):
                        turn = b + t0
                        for hg in range(UNITS):
                            v = i * UNITS + hg
                            dve.wait_ge(scored, turn * (2 * UNITS) + (v + 1))
                            s = ps[:, 2 * (v % 2):2 * (v % 2) + 2, :].rearrange("p a (h t) -> p a h t", h=2)
                            out_ = rowmax[:, i, 4 * hg:4 * hg + 4].rearrange("p (a h) -> p a h", h=2)
                            nc.vector.reduce_max(out_, s[:, :, :, 0:(i + 1) * P], AX.X).then_inc(maxed, 1)
                        dve.wait_ge(maxed, turn * (2 * UNITS) + (i + 1) * UNITS)
                        nc.vector.tensor_scalar(negmax[:, i, 0, :], rowmax[:, i, :], -1.0, None, ALU.mult).then_inc(max_chain, 1)
                        dve.wait_ge(max_chain, turn * (3 * QT) + (3 * i + 1))
                        nc.vector.scalar_tensor_tensor(maxrest[:, i, :], rowmax[:, i, :], -1.0, negmax[:, i, 0, :],
                                                       ALU.mult, ALU.subtract).then_inc(max_chain, 1)
                        dve.wait_ge(max_chain, turn * (3 * QT) + (3 * i + 2))
                        nc.vector.tensor_copy(negmax[:, i, 1, :], maxrest[:, i, :]).then_inc(max_chain, 1)
                        dve.wait_ge(max_chain, turn * (3 * QT) + (3 * i + 3))
                        nc.vector.tensor_tensor(negmax[:, i, 2, :], maxrest[:, i, :], negmax[:, i, 1, :],
                                                ALU.subtract).then_inc(negmax_ready, 1)

                    def keep_oT(b, e):
                        dve.wait_ge(attended, (b + t0) * UNITS + (e + 1))
                        nc.vector.tensor_copy(oT[:, e, :], ps[:, 4 + e % 2, 0:SEQ]).then_inc(oT_ready, 1)

                    def divide(b, c):
                        turn = b + t0
                        half, i = c // 2, c % 2
                        o = ps[:, (6, 7, 4, 5)[c], :].rearrange("p (h d) -> p h d", d=VPAD)
                        rcp = rowrcp[:, i, 16 * half:16 * half + 16]
                        dve.wait_ge(o_flipped, turn * 4 + (c + 1))
                        nc.vector.reciprocal(rcp, o[:, :, HD]).then_inc(rcp_chain, 1)
                        dve.wait_ge(rcp_chain, turn * 4 + (c + 1))
                        nc.vector.tensor_tensor(attn[:, i, 256 * half:256 * half + 256].rearrange("p (h d) -> p h d", d=HD),
                                                o[:, :, 0:HD], rcp.unsqueeze(2).to_broadcast([P, 16, HD]), ALU.mult)\
                            .then_inc(attn_ready, 1)

                    def add_output(b, i):
                        turn = b + t0
                        tile = x[:, bass.ds(b * QT + i, 1), :].rearrange("p a d -> p (a d)")
                        if rotary:
                            dve.wait_ge(out_done, turn * QT + (i + 1))
                            nc.vector.tensor_tensor(tile, ps[:, 4 + i, :], tile, ALU.add).then_inc(residual, 1)
                        else:
                            dve.wait_ge(attn_ready, turn * 4 + 4)
                            view = tile.rearrange("p (g k d) -> p k g d", g=rep, d=HD)
                            nc.vector.tensor_tensor(view, view, attn[:, i, :].rearrange("p (k g d) -> p k g d", g=rep, d=HD),
                                                    ALU.add).then_inc(residual, 1)

                    def back(b, more):
                        if more:
                            norm_stats(dve, sub, b + 1)
                        row_maxima(b, 0)
                        if more:
                            norm_apply(dve, sub, b + 1, xn)
                        row_maxima(b, 1)
                        if more:
                            front_rope(b + 1, 0)
                        for e in range(UNITS):
                            keep_oT(b, e)
                            if e == 1 and more:
                                front_rope(b + 1, 1)
                            if e == 5:
                                divide(b, 0)
                                divide(b, 1)
                        if more:
                            front_stack(b + 1, range(0, 4, 2))
                        divide(b, 2)
                        divide(b, 3)
                        if more:
                            front_stack(b + 1, range(4, 2 * SU, 2))
                        for i in range(QT):
                            add_output(b, i)

                    await_group(dve, "a1" if rotary else bias)
                    norm_stats(dve, sub, 0)
                    norm_apply(dve, sub, 0, xn)
                    front_rope(0, 0)
                    front_rope(0, 1)
                    front_stack(0, range(0, 2 * SU, 2))
                    with dve.Fori(0, BATCH - 1) as b:
                        back(b, True)
                    back(BATCH - 1, False)

                @block.scalar
                def _(act):
                    def stage_values(b, i):
                        if rotary:
                            act.wait_ge(rope_muled, (b + t0) * QT + (i + 1))
                            nc.scalar.activation(vf[:, i, 0:kvd], ps[:, 7, kvd:2 * kvd], ACT.Copy).then_inc(v_staged, 1)

                    def cut(b, i, part):
                        turn = b + t0
                        src_q, src_k = (qf[:, i, :], kf[:, i, 0:kvd]) if part == 0 else (rest[:, 0:DIM], rest[:, DIM:DIM + kvd])
                        q3 = src_q.rearrange("p (h r d) -> p h r d", r=1, d=HD)
                        k3 = src_k.rearrange("p (h r d) -> p h r d", r=1, d=HD)
                        q4 = qs[:, i, :, :].rearrange("p h (r d) -> p h r d", d=HD)
                        k4 = ks[:, i, 0:kv, :].rearrange("p h (r d) -> p h r d", d=HD)
                        rows_q = (slice(0, 3), slice(3, 5), slice(5, 6))[part]
                        rows_k = (slice(1, 6, 2), slice(2, 5, 2), slice(0, 1))[part]
                        n = 3 - part
                        if part == 0:
                            act.wait_ge(qk_float, turn * QT + (i + 1))
                        else:
                            act.wait_ge(rest_ready, turn * 4 + (2 * i + part))
                        nc.scalar.activation(q4[:, :, rows_q, :], q3.to_broadcast([P, HEADS, n, HD]), ACT.Copy)
                        nc.scalar.activation(k4[:, :, rows_k, :], k3.to_broadcast([P, kv, n, HD]), ACT.Copy).then_inc(part_cut, 1)

                    def front_stack(b, us):
                        for u in us:
                            i, kind, c = SORDER[u]
                            dst = (ksT if kind == "k" else qsT)[0:STACK, 8 * c:8 * c + 8, i * P:(i + 1) * P]
                            act.wait_ge(stack_flipped, b * (2 * SU) + (2 * su0 + u + 1))
                            nc.scalar.activation(dst, ps_bf[0:STACK, u % 4, :].rearrange("p (h t) -> p h t", t=P), ACT.Copy)\
                                .then_inc(stackT_scalar, 1)

                    def keep_values(b, last_turn):
                        if last_turn is not None:
                            act.wait_ge(attended, (last_turn + t0) * UNITS + UNITS)
                        act.wait_ge(v_staged, (b + t0) * QT + QT)
                        nc.scalar.activation(val[:, :, 0:kv, 0:HD], vf[:, :, 0:kvd].rearrange("p i (h d) -> p i h d", d=HD),
                                             ACT.Copy).then_inc(val_ready, 1)

                    def exps(b, e):
                        turn = b + t0
                        act.wait_ge(key_scored, turn * PAIRS + (e + 1))
                        if e >= 4:
                            act.wait_ge(attended, turn * UNITS + ((e - 4) // 2 + 1))
                        bank = 2 * (e % 2)
                        nc.scalar.activation(probT[:, e % 4, :], ps[:, bank:bank + 2, :].rearrange("p a t -> p (a t)")[:, 0:3 * SEQ],
                                             ACT.Exp, scale=SCALES[a]).then_inc(exped, 1)

                    def back(b, more):
                        turn = b + t0
                        if more:
                            norm_scalar(act, sub, b + 1, xT, 6)
                        for i in range(QT):
                            act.wait_ge(negmax_flipped, turn * QT + (i + 1))
                            nc.scalar.activation(negmaxT[:, i * P:(i + 1) * P], ps_bf[0:96, 4 + i, 0:P], ACT.Copy)\
                                .then_inc(negmaxT_ready, 1)
                        if more:
                            stage_values(b + 1, 0)
                        for e in range(PAIRS):
                            exps(b, e)
                            if more:
                                if e in (1, 3, 5):
                                    cut(b + 1, 0, e // 2)
                                if e == 6:
                                    stage_values(b + 1, 1)
                                if e in (7, 9, 11):
                                    cut(b + 1, 1, (e - 7) // 2)
                        if more:
                            keep_values(b + 1, b)
                            front_stack(b + 1, range(1, 2 * SU, 2))
                        if rotary:
                            for i in range(QT):
                                act.wait_ge(attn_flipped, turn * QT + (i + 1))
                                nc.scalar.activation(aT[:, :, i * P:(i + 1) * P], ps[:, 6 + i, :].rearrange("p (k t) -> p k t", k=KC),
                                                     ACT.Copy).then_inc(aT_ready, 1)

                    norm_scalar(act, sub, 0, xT, 6)
                    for i in range(QT):
                        stage_values(0, i)
                        for part in range(3):
                            cut(0, i, part)
                    keep_values(0, None)
                    front_stack(0, range(1, 2 * SU, 2))
                    with act.Fori(0, BATCH - 1) as b:
                        back(b, True)
                    back(BATCH - 1, False)

                @block.tensor
                def _(pe):
                    def project_q(b, i):
                        if i == 0:
                            pe.wait_ge(xT_ready, (b + sub * BATCH) * QT + QT)
                        else:
                            pe.wait_ge(v_staged, (b + t0) * QT + 1)
                            pe.wait_ge(qk_float, (b + t0) * QT + 1)
                        for k in range(KC):
                            nc.tensor.matmul(ps[:, 6, :], xT[:, k, i * P:(i + 1) * P], wqkv[:, k, 0:DIM], start=(k == 0), stop=(k == KC - 1))

                    def project_kv(b, i):
                        for k in range(KC):
                            last = nc.tensor.matmul(ps[:, 7, 0:2 * kvd], xT[:, k, i * P:(i + 1) * P], wqkv[:, k, DIM:DIM + 2 * kvd],
                                                    start=(k == 0), stop=(k == KC - 1))
                        last.then_inc(qkv_done, 1)

                    def flip_stack(b, us):
                        for u in us:
                            i, kind, c = SORDER[u]
                            if u % SU == 0:
                                pe.wait_ge(part_cut, (b + t0) * 6 + 3 * (i + 1))
                            if u >= 4:
                                kept = stackT_scalar if u % 2 else stackT_vector
                                pe.wait_ge(kept, b * SU + (su0 + (u - 4) // 2 + 1))
                            src = ks if kind == "k" else qs
                            for h in range(8):
                                last = nc.tensor.transpose(ps_bf[0:STACK, u % 4, h * P:(h + 1) * P],
                                                           src[:, i, 8 * c + h, :], ident_bf[:, :])
                            last.then_inc(stack_flipped, 1)

                    def score(b, i, hg):
                        turn, keys, v = b + t0, (i + 1) * P, i * UNITS + hg
                        if v >= 2:
                            pe.wait_ge(maxed, turn * (2 * UNITS) + (v - 1))
                        for half in range(2):
                            bank = ps[:, 2 * (v % 2) + half, :].rearrange("p (h t) -> p h t", h=2)
                            nc.tensor.matmul(bank[:, :, i * P:keys], ident_bf[:, :], masks[:, 0:1, :].to_broadcast([P, 2, P]),
                                             start=True, stop=False, skip_group_check=True)
                            for j in range(2):
                                h = 4 * hg + 2 * half + j
                                last = nc.tensor.matmul(bank[:, j, 0:keys], qsT[0:STACK, h, i * P:(i + 1) * P],
                                                        ksT[0:STACK, h // rep, 0:keys], start=False, stop=(j == 1),
                                                        skip_group_check=True)
                        last.then_inc(scored, 1)

                    def flip_maxima(b, i):
                        pe.wait_ge(negmax_ready, (b + t0) * QT + (i + 1))
                        nc.tensor.transpose(ps_bf[0:96, 4 + i, 0:P], negmax[:, i, :, :].rearrange("p c h -> p (c h)"),
                                            ident_bf[:, :]).then_inc(negmax_flipped, 1)

                    def key_score(b, e):
                        turn = b + t0
                        if e >= 2:
                            pe.wait_ge(exped, turn * PAIRS + (e - 1))
                        bank = 2 * (e % 2)
                        for j, n in ((0, SEQ), (1, P)):
                            o = ps[:, bank + j, 0:2 * n].rearrange("p (h t) -> p h t", h=2)
                            nc.tensor.matmul(o[:, :, 0:P], ident_bf[:, :], masks[:, 1:2, :].to_broadcast([P, 2, P]),
                                             start=True, stop=False, skip_group_check=True)
                            for c in range(2):
                                h = 2 * e + c
                                last = nc.tensor.matmul(o[:, c, :], ksT[0:SHIFT + 3, h // rep, j * P:(j + 1) * P],
                                                        qsT[0:SHIFT + 3, h, SEQ - n:SEQ], start=False, stop=(c == 1),
                                                        skip_group_check=True)
                        last.then_inc(key_scored, 1)

                    def attend(b, e):
                        turn = b + t0
                        pe.wait_ge(exped, turn * PAIRS + (2 * e + 2))
                        if e >= 2:
                            pe.wait_ge(oT_ready, turn * UNITS + (e - 1))
                        for kt in range(QT):
                            for j in range(4):
                                slot, c = (2 * e + j // 2) % 4, j % 2
                                pr = probT[:, slot, c * SEQ:(c + 1) * SEQ] if kt == 0 else probT[:, slot, 2 * SEQ + c * P:2 * SEQ + (c + 1) * P]
                                last = nc.tensor.matmul(ps[32 * j:32 * j + 32, 4 + e % 2, kt * P:SEQ], val[:, kt, (4 * e + j) // rep, :],
                                                        pr, start=(kt == 0), stop=(kt == 1))
                        last.then_inc(attended, 1)

                    def flip_output(b, c):
                        half, i = c // 2, c % 2
                        pe.wait_ge(oT_ready, (b + t0) * UNITS + 4 * (half + 1))
                        for e in range(4 * half, 4 * half + 4):
                            last = nc.tensor.transpose(ps[:, (6, 7, 4, 5)[c], (e % 4) * P:(e % 4 + 1) * P], oT[:, e, i * P:(i + 1) * P],
                                                       ident[:, :])
                        last.then_inc(o_flipped, 1)

                    def back(b, more):
                        turn = b + t0
                        for hg in range(UNITS):
                            score(b, 0, hg)
                        if more:
                            norm_tensor(pe, sub, b + 1, xn, 6)
                        for hg in range(UNITS):
                            score(b, 1, hg)
                            if hg == 3:
                                flip_maxima(b, 0)
                        if more:
                            project_q(b + 1, 0)
                        flip_maxima(b, 1)
                        if more:
                            project_kv(b + 1, 0)
                        pe.wait_ge(shift_in, turn * 16 + 16)
                        pe.wait_ge(maxed, turn * (2 * UNITS) + 2 * UNITS)
                        pe.wait_ge(val_ready, turn + 1)
                        for e in range(PAIRS):
                            key_score(b, e)
                            if e >= 3 and e % 2 == 1:
                                attend(b, (e - 3) // 2)
                            if more and e == 5:
                                project_q(b + 1, 1)
                                project_kv(b + 1, 1)
                            if e == 12:
                                if more:
                                    pe.wait_ge(v_staged, (b + 1 + t0) * QT + QT)
                                    pe.wait_ge(qk_float, (b + 1 + t0) * QT + QT)
                                flip_output(b, 0)
                                flip_output(b, 1)
                        attend(b, UNITS - 1)
                        if more:
                            pe.wait_ge(exped, turn * PAIRS + PAIRS)
                            flip_stack(b + 1, range(0, 4))
                        flip_output(b, 2)
                        flip_output(b, 3)
                        if more:
                            flip_stack(b + 1, range(4, 2 * SU))
                        if rotary:
                            for i in range(QT):
                                pe.wait_ge(attn_ready, turn * 4 + (3 + i))
                                for k in range(KC):
                                    last = nc.tensor.transpose(ps[:, 6 + i, k * P:(k + 1) * P], attn[:, i, k * P:(k + 1) * P], ident[:, :])
                                last.then_inc(attn_flipped, 1)
                            for i in range(QT):
                                pe.wait_ge(aT_ready, turn * QT + (i + 1))
                                for k in range(KC):
                                    last = nc.tensor.matmul(ps[:, 4 + i, :], aT[:, k, i * P:(i + 1) * P], wo[:, k, :],
                                                            start=(k == 0), stop=(k == KC - 1))
                                last.then_inc(out_done, 1)
                        if more:
                            pe.wait_ge(stackT_vector, (b + 1) * SU + (su0 + SU))
                            pe.wait_ge(stackT_scalar, (b + 1) * SU + (su0 + SU))

                    await_group(pe, weights)
                    pe.wait_ge(val_set, 3 * a + 3)
                    norm_tensor(pe, sub, 0, xn, 6)
                    for i in range(QT):
                        project_q(0, i)
                        project_kv(0, i)
                    flip_stack(0, range(2 * SU))
                    pe.wait_ge(stackT_vector, su0 + SU)
                    pe.wait_ge(stackT_scalar, su0 + SU)
                    with pe.Fori(0, BATCH - 1) as b:
                        back(b, True)
                    back(BATCH - 1, False)

        top[0] = work + QT * DIM * 4 + KC * SEQ * 4
        logits, _ = place("logits", [P, QT, E1])
        beats, _ = place("beats", [P, QT, E1 * E1])
        ties, _ = place("ties", [P, QT, E1 * E1])
        ranks, _ = place("ranks", [P, QT, E1])
        gates, _ = place("gates", [P, QT, E1])
        top_logit, _ = place("top_logit", [P, QT])
        gate_sum, _ = place("gate_sum", [P, QT])
        mid, _ = place("mid", [P, QT, P])
        midT, _ = place("midT", [P, SEQ])
        here = top[0]
        tmp1, _ = place("tmp1", [P, TILES, E1 * RANK])
        midT1, _ = place("midT1", [P, TILES, P])
        chosen, _ = place("chosen", [P, TILES, 2, E1])
        topg, _ = place("topg", [P, TILES, 2])
        weighed, _ = place("weighed", [P, TILES, 2, E1])
        wexp, _ = place("wexp", [P, TILES, E1])
        counts, _ = place("counts", [P, 2 * E1])
        ones, _ = place("ones", [P, P])
        hid, _ = place("hid", [P, QT, 4 * E1])
        hidT, _ = place("hidT", [4 * E1, SEQ])
        hstats, _ = place("hstats", [P, QT, 6])
        hmv, _ = place("hmv", [P, QT, 2])
        hrstd, _ = place("hrstd", [P, QT, 1])
        gap, _ = place("gap", [P, QT, 2])
        parts = after + (DIM + 2 * KV_HEADS[2] * HD) * KC * 4
        top[0] = parts
        w13_hi, _ = place("w13_hi", [P, KC, 2 * HID2], F32R)
        w2_hi, _ = place("w2_hi", [P, HC2, DIM], F32R)
        a13_hi, _ = place("a13_hi", [P, KC, 96], F32R)
        a2_hi, _ = place("a2_hi", [P, HC2, RANK], F32R)
        b13_parts, _ = place("b13_parts", [96, HID2], F32R)
        w13_lo, w2_lo, a13_lo, a2_lo = (place(f"{n}_lo", shape, F32R, at=at)[0] for n, shape, at in (
            ("w13", [P, KC, 2 * HID2], where["l2_w13"]), ("w2", [P, HC2, DIM], where["l2_w2"]),
            ("a13", [P, KC, 96], where["l2_a13"]), ("a2", [P, HC2, RANK], where["l2_a2"])))
        xn2, _ = place("xn2", [P, QT, DIM])
        xT2_hi, _ = place("xT2_hi", [P, KC, SEQ], F32R)
        xT2_lo, _ = place("xT2_lo", [P, KC, SEQ], F32R)
        lowT, _ = place("lowT", [96, 2, SEQ], F32R)
        low2T, _ = place("low2T", [96, SEQ])
        lmask, _ = place("lmask", [96, 2])
        tanh_, _ = place("tanh_", [P, 2, SEQ])
        gate_, _ = place("gate_", [P, 2, SEQ])
        g_hi, _ = place("g_hi", [P, 4, SEQ], F32R)
        g_lo, _ = place("g_lo", [P, 4, SEQ], F32R)
        top[0] = behind3
        up_hi, _ = place("up_hi", [P, KC, INT3], F32R)
        down_hi, _ = place("down_hi", [P, IC3, DIM], F32R)
        fc1_hi, _ = place("fc1_hi", [P, KC, LAT3 + E3], F32R)
        expert_hi, _ = place("expert_hi", [P, LC3, LAT3], F32R)
        fc2_hi, _ = place("fc2_hi", [P, LC3, DIM], F32R)
        up_lo, down_lo, fc1_lo, expert_lo, fc2_lo = (place(f"{n}_lo", shape, F32R, at=at)[0] for n, shape, at in (
            ("up", [P, KC, INT3], where["l3_up"]), ("down", [P, IC3, DIM], where["l3_down"]),
            ("fc1", [P, KC, LAT3 + E3], where["l3_fc1"]), ("expert", [P, LC3, LAT3], where["l3_expert"]),
            ("fc2", [P, LC3, DIM], where["l3_fc2"])))
        xn3, _ = place("xn3", [P, QT, DIM])
        xT3_hi, _ = place("xT3_hi", [P, KC, SEQ], F32R)
        xT3_lo, _ = place("xT3_lo", [P, KC, SEQ], F32R)
        lat_hi, _ = place("lat_hi", [P, LC3, SEQ], F32R)
        lat_lo, _ = place("lat_lo", [P, LC3, SEQ], F32R)
        exp_hi, _ = place("exp_hi", [P, LC3, SEQ], F32R)
        exp_lo, _ = place("exp_lo", [P, LC3, SEQ], F32R)
        logitsT, _ = place("logitsT", [E3, SEQ])
        logits3, _ = place("logits3", [P, QT, E3])
        top8, _ = place("top8", [P, QT, E3])
        routing, _ = place("routing", [P, QT])
        relu_, _ = place("relu_", [P, 2, SEQ])
        square, _ = place("square", [P, 2, SEQ])
        h_hi, _ = place("h_hi", [P, 4, SEQ], F32R)
        h_lo, _ = place("h_lo", [P, 4, SEQ], F32R)
        shared, _ = place("shared", [P, QT, DIM])
        ystats, _ = place("ystats", [P, QT, 6])
        ymv, _ = place("ymv", [P, QT, 2])
        yrstd, _ = place("yrstd", [P, QT, 1])
        tensors["lmask"] = lmask
        lo_ready = sem("xT_lo_ready")

        def each_turn(eng, turn_of):
            turn_of(0, True, True)
            with eng.Fori(1, BATCH - 1) as b:
                turn_of(b, False, True)
            turn_of(BATCH - 1, False, False)

        def tile_of(b, i):
            return x[:, bass.ds(b * QT + i, 1), :].rearrange("p a d -> p (a d)")

        def rank_experts(chain, E, lower):
            lg = logits[:, :, 0:E]
            f = lg.unsqueeze(2).to_broadcast([P, QT, E, E])
            e = lg.unsqueeze(3).to_broadcast([P, QT, E, E])
            bt = beats[:, :, 0:E * E].rearrange("p i (e f) -> p i e f", f=E)
            ti = ties[:, :, 0:E * E].rearrange("p i (e f) -> p i e f", f=E)
            for i in range(QT):
                nc.vector.tensor_tensor(bt[:, i], f[:, i], e[:, i], ALU.is_gt)
                last = nc.vector.tensor_tensor(ti[:, i], f[:, i], e[:, i], ALU.is_equal)
            chain.link(last)
            low = lower[:, :].unsqueeze(1).to_broadcast([P, QT, E * E])
            chain.link(nc.vector.tensor_tensor(ties[:, :, 0:E * E], ties[:, :, 0:E * E], low, ALU.mult))
            chain.link(nc.vector.tensor_tensor(beats[:, :, 0:E * E], beats[:, :, 0:E * E], ties[:, :, 0:E * E], ALU.add))
            chain.link(nc.vector.reduce_sum(ranks[:, :, 0:E], bt, AX.X))

        def layer0_feed_forward(sub):
            mid_done = sem("f0_mid_done")
            chain_sem = sem("f0_chain")
            shifted = sem("f0_shifted")
            exped0 = sem("f0_exped")
            gated = sem("f0_gated")
            mid_flipped = sem("f0_mid_flipped")
            midT_ready = sem("f0_midT_ready")
            done = sem("f0_done")
            EA = E0 * RANK

            with nc.Block() as block:
                @block.sync
                def _(sp):
                    load_groups(sp, "f0", "a1")

                @block.gpsimd
                def _(pool):
                    nc.gpsimd.memset(mid[:, :, :], 0.0).then_inc(val_set0, 1)
                    with pool.Fori(0, BATCH) as b:
                        norm_gpsimd(pool, sub, b)

                @block.vector
                def _(dve):
                    await_group(dve, "f0")
                    dve.wait_ge(val_set0, 1)
                    chain = Chain(dve, chain_sem, 11)
                    with dve.Fori(0, BATCH) as b:
                        norm_vector(dve, sub, b, xn)
                        chain.start(b)
                        dve.wait_ge(mid_done, b + 1)
                        lg, gt = logits[:, :, 0:E0], gates[:, :, 0:E0]
                        chain.link(nc.vector.tensor_copy(lg, ps[:, 2:4, EA:EA + E0]))
                        rank_experts(chain, E0, lower4)
                        chain.link(nc.vector.tensor_scalar(ranks[:, :, 0:E0], ranks[:, :, 0:E0], 1.5, None, ALU.is_lt))
                        chain.link(nc.vector.reduce_max(top_logit[:, :], lg, AX.X))
                        nc.vector.tensor_tensor(gt, lg, top_logit[:, :].unsqueeze(2).to_broadcast([P, QT, E0]),
                                                ALU.subtract).then_inc(shifted, 1)
                        dve.wait_ge(exped0, b + 1)
                        chain.link(nc.vector.tensor_tensor(gt, gt, ranks[:, :, 0:E0], ALU.mult))
                        chain.link(nc.vector.reduce_sum(gate_sum[:, :], gt, AX.X))
                        chain.link(nc.vector.reciprocal(gate_sum[:, :], gate_sum[:, :]))
                        chain.link(nc.vector.scalar_tensor_tensor(gt, gt, 4.0, gate_sum[:, :].unsqueeze(2).to_broadcast([P, QT, E0]),
                                                                  ALU.mult, ALU.mult))
                        for i in range(QT):
                            last = nc.vector.tensor_tensor(mid[:, i, 0:EA].rearrange("p (e r) -> p e r", r=RANK),
                                                           ps[:, 2 + i, 0:EA].rearrange("p (e r) -> p e r", r=RANK),
                                                           gt[:, i, :].unsqueeze(2).to_broadcast([P, E0, RANK]), ALU.mult)
                        last.then_inc(gated, 1)
                        chain.end()
                        dve.wait_ge(done, b + 1)
                        for i in range(QT):
                            nc.vector.tensor_tensor(tile_of(b, i), ps[:, 6 + i, :], tile_of(b, i), ALU.add).then_inc(residual, 1)

                @block.scalar
                def _(act):
                    with act.Fori(0, BATCH) as b:
                        norm_scalar(act, sub, b, xT)
                        act.wait_ge(shifted, b + 1)
                        nc.scalar.activation(gates[:, :, 0:E0], gates[:, :, 0:E0], ACT.Exp).then_inc(exped0, 1)
                        act.wait_ge(mid_flipped, b + 1)
                        nc.scalar.activation(midT[:, :], ps[:, 4, 0:SEQ], ACT.Copy).then_inc(midT_ready, 1)

                @block.tensor
                def _(pe):
                    await_group(pe, "f0")
                    with pe.Fori(0, BATCH) as b:
                        norm_tensor(pe, sub, b, xn)
                        pe.wait_ge(xT_ready, (b + sub * BATCH) * QT + QT)
                        for i in range(QT):
                            for k in range(KC):
                                last = nc.tensor.matmul(ps[:, 2 + i, 0:EA + E0], xT[:, k, i * P:(i + 1) * P], l0_ar[:, k, :],
                                                        start=(k == 0), stop=(k == KC - 1))
                        last.then_inc(mid_done, 1)
                        pe.wait_ge(gated, b + 1)
                        for i in range(QT):
                            last = nc.tensor.transpose(ps[:, 4, i * P:(i + 1) * P], mid[:, i, :], ident[:, :])
                        last.then_inc(mid_flipped, 1)
                        pe.wait_ge(midT_ready, b + 1)
                        for i in range(QT):
                            last = nc.tensor.matmul(ps[:, 6 + i, :], midT[:, i * P:(i + 1) * P], l0_b[:, :], start=True, stop=True)
                        last.then_inc(done, 1)

        def layer1_feed_forward(sub):
            main_done = sem("f1_main_done")
            chain_sem = sem("f1_chain")
            hvar = sem("f1_hvar")
            pool_chain = sem("f1_pool_chain")
            hrstd_ready = sem("f1_hrstd_ready")
            hid_ready = sem("f1_hid_ready")
            hid_flipped = sem("f1_hid_flipped")
            hidT_ready = sem("f1_hidT_ready")
            logits_done = sem("f1_logits_done")
            gap_ready = sem("f1_gap_ready")
            gap_exped = sem("f1_gap_exped")
            turn_over = sem("f1_turn_over")
            ones_set = sem("f1_ones_set")
            counted = sem("f1_counted")
            tail_chain = sem("f1_tail_chain")
            weighted = sem("f1_weighted")
            mid_flipped = sem("f1_mid_flipped")
            midT_ready = sem("f1_midT_ready")
            done = sem("f1_done")
            EA, HG = E1 * RANK, 4 * E1

            with nc.Block() as block:
                @block.gpsimd
                def _(pool):
                    nc.gpsimd.memset(ones[:, :], 1.0).then_inc(ones_set, 1)
                    with pool.Fori(0, BATCH) as b:
                        norm_gpsimd(pool, sub, b)
                        pool.wait_ge(hvar, b + 1)
                        nc.gpsimd.tensor_tensor(hrstd[:, :, 0], hmv[:, :, 1], eps[:, :].to_broadcast([P, QT]), ALU.add).then_inc(pool_chain, 1)
                        pool.wait_ge(pool_chain, b + 1)
                        nc.gpsimd.tensor_tensor(hrstd[:, :, 0], hrstd[:, :, 0], minus_half[:, :].to_broadcast([P, QT]),
                                                ALU.pow).then_inc(hrstd_ready, 1)

                @block.vector
                def _(dve):
                    await_group(dve, "f1")
                    chain = Chain(dve, chain_sem, 15)
                    gb1, gamma, beta, gb2 = (l1_gvec[:, HG * j:HG * j + (HG if j < 3 else E1)] for j in range(4))
                    with dve.Fori(0, BATCH) as b:
                        norm_vector(dve, sub, b, xn)
                        chain.start(b)
                        dve.wait_ge(main_done, b + 1)
                        for i in range(QT):
                            nc.vector.tensor_tensor(hid[:, i, :], ps[:, 4 + i, EA:EA + HG], gb1, ALU.add)
                        dve.drain()
                        for i in range(QT):
                            nc.vector.bn_stats(hstats[:, i, :], hid[:, i, :])
                        dve.drain()
                        for i in range(QT):
                            last = nc.vector.bn_aggr(hmv[:, i, :], hstats[:, i, :])
                        last.then_inc(hvar, 1)
                        for i in range(QT):
                            nc.vector.tensor_tensor(tile_of(b, i), ps[:, 2 + i, :], tile_of(b, i), ALU.add)
                            nc.vector.tensor_copy(tmp1[:, bass.ds(b * QT + i, 1), :].rearrange("p a d -> p (a d)"), ps[:, 4 + i, 0:EA])
                        dve.wait_ge(hrstd_ready, b + 1)
                        for i in range(QT):
                            last = nc.vector.tensor_scalar(hid[:, i, :], hid[:, i, :], hmv[:, i, 0:1], hrstd[:, i, :],
                                                           ALU.subtract, ALU.mult)
                        chain.link(last)
                        chain.link(nc.vector.tensor_tensor(hid[:, :, :], hid[:, :, :], gamma.unsqueeze(1).to_broadcast([P, QT, HG]), ALU.mult))
                        chain.link(nc.vector.tensor_tensor(hid[:, :, :], hid[:, :, :], beta.unsqueeze(1).to_broadcast([P, QT, HG]), ALU.add))
                        nc.vector.tensor_scalar(hid[:, :, :], hid[:, :, :], 0.0, None, ALU.max).then_inc(hid_ready, 1)
                        dve.wait_ge(logits_done, b + 1)
                        chain.link(nc.vector.tensor_tensor(logits[:, :, :], ps[:, 0:2, 0:E1], gb2.unsqueeze(1).to_broadcast([P, QT, E1]), ALU.add))
                        rank_experts(chain, E1, lower8)
                        pick = [chosen[:, bass.ds(b * QT, QT), c, :] for c in range(2)]
                        for c in range(2):
                            last = nc.vector.tensor_scalar(pick[c], ranks[:, :, :], float(c), None, ALU.is_equal)
                        chain.link(last)
                        for c in range(2):
                            last = nc.vector.tensor_tensor(beats[:, :, c * E1:(c + 1) * E1], pick[c], logits[:, :, :], ALU.mult)
                        chain.link(last)
                        chain.link(nc.vector.reduce_sum(gap[:, :, :], beats[:, :, 0:2 * E1].rearrange("p i (c e) -> p i c e", c=2), AX.X))
                        nc.vector.tensor_tensor(gap[:, :, 1], gap[:, :, 1], gap[:, :, 0], ALU.subtract).then_inc(gap_ready, 1)
                        dve.wait_ge(gap_exped, b + 1)
                        chain.link(nc.vector.tensor_scalar(gap[:, :, 0], gap[:, :, 1], 1.0, None, ALU.add))
                        chain.link(nc.vector.reciprocal(gap[:, :, 0], gap[:, :, 0]))
                        chain.link(nc.vector.tensor_copy(topg[:, bass.ds(b * QT, QT), 0], gap[:, :, 0]))
                        chain.link(nc.vector.tensor_tensor(topg[:, bass.ds(b * QT, QT), 1], gap[:, :, 0], gap[:, :, 1], ALU.mult))
                        chain.end()
                    tail = Chain(dve, tail_chain, 6)
                    tail.start(0)
                    dve.wait_ge(counted, 1)
                    tail.link(nc.vector.reduce_sum(counts[:, :], ps[:, 0, 0:TILES * 2 * E1].rearrange("p (t c) -> p c t", t=TILES), AX.X))
                    tail.link(nc.vector.tensor_scalar(counts[:, :], counts[:, :], float(CAPACITY) + 0.5, 1.0 / RANK, ALU.is_lt, ALU.mult))
                    tail.link(nc.vector.tensor_tensor(weighed[:, :, :, :].rearrange("p t c e -> p t (c e)"),
                                                      chosen[:, :, :, :].rearrange("p t c e -> p t (c e)"),
                                                      counts[:, :].unsqueeze(1).to_broadcast([P, TILES, 2 * E1]), ALU.mult))
                    tail.link(nc.vector.tensor_tensor(weighed[:, :, :, :].rearrange("p t c e -> p (t c) e"),
                                                      weighed[:, :, :, :].rearrange("p t c e -> p (t c) e"),
                                                      topg[:, :, :].rearrange("p t c -> p (t c)").unsqueeze(2).to_broadcast([P, TILES * 2, E1]),
                                                      ALU.mult))
                    tail.link(nc.vector.tensor_tensor(wexp[:, :, :], weighed[:, :, 0, :], weighed[:, :, 1, :], ALU.add))
                    t3 = tmp1[:, :, :].rearrange("p t (e r) -> p (t e) r", r=RANK)
                    nc.vector.tensor_tensor(t3, t3, wexp[:, :, :].rearrange("p t e -> p (t e)").unsqueeze(2)
                                            .to_broadcast([P, TILES * E1, RANK]), ALU.mult).then_inc(weighted, 1)
                    tail.k += 1
                    tail.end()
                    for T in range(TILES):
                        dve.wait_ge(done, T + 1)
                        nc.vector.tensor_tensor(x[:, T, :], ps[:, 4 + T % 4, :], x[:, T, :], ALU.add).then_inc(residual, 1)

                @block.scalar
                def _(act):
                    with act.Fori(0, BATCH) as b:
                        norm_scalar(act, sub, b, xT)
                        act.wait_ge(hid_flipped, b + 1)
                        nc.scalar.activation(hidT[:, :], ps[0:HG, 6, 0:SEQ], ACT.Copy).then_inc(hidT_ready, 1)
                        act.wait_ge(gap_ready, b + 1)
                        nc.scalar.activation(gap[:, :, 1], gap[:, :, 1], ACT.Exp).then_inc(gap_exped, 1)
                    for half in range(2):
                        act.wait_ge(mid_flipped, half + 1)
                        nc.scalar.activation(midT1[:, 4 * half:4 * half + 4, :], ps[:, 1 + half, :].rearrange("p (t c) -> p t c", t=4),
                                             ACT.Copy).then_inc(midT_ready, 1)

                @block.tensor
                def _(pe):
                    await_group(pe, "f1")
                    with pe.Fori(0, BATCH) as b:
                        norm_tensor(pe, sub, b, xn)
                        pe.wait_ge(xT_ready, (b + sub * BATCH) * QT + QT)
                        for i in range(QT):
                            lhs = [xT[:, k, i * P:(i + 1) * P] for k in range(KC)]
                            for bank, w in ((4 + i, l1_ag), (2 + i, l1_w)):
                                n = w.shape[2]
                                for k in range(KC):
                                    last = nc.tensor.matmul(ps[:, bank, 0:n], lhs[k], w[:, k, :], start=(k == 0), stop=(k == KC - 1))
                        last.then_inc(main_done, 1)
                        pe.wait_ge(hid_ready, b + 1)
                        for i in range(QT):
                            last = nc.tensor.transpose(ps[0:HG, 6, i * P:(i + 1) * P], hid[:, i, :], ident[:, :])
                        last.then_inc(hid_flipped, 1)
                        pe.wait_ge(hidT_ready, b + 1)
                        for i in range(QT):
                            last = nc.tensor.matmul(ps[:, i, 0:E1], hidT[:, i * P:(i + 1) * P], l1_gw2[:, :], start=True, stop=True)
                        last.then_inc(logits_done, 1)
                    pe.wait_ge(ones_set, 1)
                    pe.wait_ge(chain_sem, BATCH * 15)
                    nc.tensor.matmul(ps[:, 0, 0:TILES * 2 * E1], ones[:, :], chosen[:, :, :, :].rearrange("p t c e -> p (t c e)"),
                                     start=True, stop=True).then_inc(counted, 1)
                    pe.wait_ge(weighted, 1)
                    for half in range(2):
                        for T in range(4 * half, 4 * half + 4):
                            last = nc.tensor.transpose(ps[:, 1 + half, (T % 4) * P:(T % 4 + 1) * P], tmp1[:, T, :], ident[:, :])
                        last.then_inc(mid_flipped, 1)
                    for T in range(TILES):
                        pe.wait_ge(midT_ready, T // 4 + 1)
                        if T >= 4:
                            pe.wait_ge(residual, updates(sub) + T - 3)
                        nc.tensor.matmul(ps[:, 4 + T % 4, :], midT1[:, T, :], l1_b[:, :], start=True, stop=True).then_inc(done, 1)

        def layer2_feed_forward(sub):
            low_done = sem("f2_low_done")
            low_hi_ready = sem("f2_low_hi_ready")
            lowT_ready = sem("f2_lowT_ready")
            zeroed = sem("f2_zeroed")
            hi_cut = sem("f2_hi_cut")
            lo_cut = sem("f2_lo_cut")
            up_done = sem("f2_up_done")
            tanhed = sem("f2_tanhed")
            half_done = sem("f2_half_done")
            g_ready = sem("f2_g_ready")
            g_hi_ready = sem("f2_g_hi_ready")
            g_lo_ready = sem("f2_g_lo_ready")
            down_done = sem("f2_down_done")
            low2_ready = sem("f2_low2_ready")
            done = sem("f2_done")
            AHEAD = 3
            XBANK = 5

            def rows(c):
                return P if c < HC2 - 1 else HLAST2

            def chunk_of(w, c):
                return w[:, :, :].rearrange("p k (j h) -> p k j h", j=2)[:, :, :, c * P:c * P + rows(c)]

            with nc.Block() as block:
                @block.sync
                def _(sp):
                    load_groups(sp, "f2_mask", "a3")

                @block.gpsimd
                def _(pool):
                    nc.gpsimd.memset(low2T[:, :], 0.0).then_inc(zeroed, 1)
                    norm_gpsimd(pool, sub, 0)

                    def turn_of(b, first, more):
                        for c in range(HC2):
                            r = rows(c)
                            pool.wait_ge(g_hi_ready, b * HC2 + (c + 1))
                            subtract_high(nc.gpsimd, g_lo[0:r, c % 4, :], gate_[0:r, c % 2, :], g_hi[0:r, c % 4, :]).then_inc(g_lo_ready, 1)
                            if more and c == 4:
                                norm_gpsimd(pool, sub, b + 1)

                    each_turn(pool, turn_of)

                @block.vector
                def _(dve):
                    def cut_chunk(c):
                        r = rows(c)
                        dve.wait_ge(hi_cut, c + 2)
                        for k in range(KC):
                            subtract_high(nc.vector, chunk_of(w13_lo, c)[:, k], chunk_of(l2_w13, c)[:, k], chunk_of(w13_hi, c)[:, k])
                        subtract_high(nc.vector, a2_lo[0:r, c, :], l2_a2[0:r, c, :], a2_hi[0:r, c, :])
                        subtract_high(nc.vector, w2_lo[0:r, c, :], l2_w2[0:r, c, :], w2_hi[0:r, c, :]).then_inc(lo_cut, 1)

                    def turn_of(b, first, more):
                        dve.wait_ge(low_hi_ready, b + 1)
                        for j in range(2):
                            last = nc.vector.scalar_tensor_tensor(lowT[32:64, j, :], ps[32:64, 6, 0:SEQ], lmask[32:64, j:j + 1],
                                                                  lowT[32:64, j, :].bitcast(F32), ALU.mult, ALU.subtract)
                        last.then_inc(lowT_ready, 1)
                        for c in range(HC2):
                            r, s, bank = rows(c), c % 2, 2 + c % 4
                            if first and c + AHEAD < HC2:
                                cut_chunk(c + AHEAD)
                            dve.wait_ge(tanhed, b * HC2 + (c + 1))
                            nc.vector.scalar_tensor_tensor(tanh_[0:r, s, :], tanh_[0:r, s, :], 1.0, ps[0:r, bank, 0:SEQ],
                                                           ALU.add, ALU.mult).then_inc(half_done, 1)
                            dve.wait_ge(half_done, b * HC2 + (c + 1))
                            if not (first and c < 2):
                                dve.wait_ge(g_lo_ready, b * HC2 + (c - 1))
                            nc.vector.scalar_tensor_tensor(gate_[0:r, s, :], tanh_[0:r, s, :], 0.5, ps[0:r, bank, SEQ:2 * SEQ],
                                                           ALU.mult, ALU.mult).then_inc(g_ready, 1)
                            if more and c == 4:
                                norm_stats(dve, sub, b + 1)
                            if more and c == 6:
                                norm_apply(dve, sub, b + 1, xn2)
                        if more:
                            split_xT(dve, sub, b + 1, xT2_hi, xT2_lo, XBANK, lo_ready)
                        dve.wait_ge(done, b + 1)
                        for i in range(QT):
                            nc.vector.tensor_tensor(tile_of(b, i), ps[:, i, :], tile_of(b, i), ALU.add).then_inc(residual, 1)

                    await_group(dve, "f2")
                    await_group(dve, "f2_mask")
                    norm_stats(dve, sub, 0)
                    norm_apply(dve, sub, 0, xn2)
                    dve.wait_ge(hi_cut, 1)
                    subtract_high(nc.vector, a13_lo[:, :, :], l2_a13[:, :, :], a13_hi[:, :, :])
                    subtract_high(nc.vector, b13_parts[64:96, :], l2_b13[64:96, :], b13_parts[64:96, :]).then_inc(lo_cut, 1)
                    split_xT(dve, sub, 0, xT2_hi, xT2_lo, XBANK, lo_ready)
                    for c in range(AHEAD):
                        cut_chunk(c)
                    each_turn(dve, turn_of)

                @block.scalar
                def _(act):
                    def cut_chunk(c):
                        r = rows(c)
                        for k in range(KC):
                            nc.scalar.activation(chunk_of(w13_hi, c)[:, k], chunk_of(l2_w13, c)[:, k], ACT.Copy)
                        nc.scalar.activation(a2_hi[0:r, c, :], l2_a2[0:r, c, :], ACT.Copy)
                        nc.scalar.activation(w2_hi[0:r, c, :], l2_w2[0:r, c, :], ACT.Copy).then_inc(hi_cut, 1)

                    def high_gate(b, c):
                        r = rows(c)
                        act.wait_ge(g_ready, b * HC2 + (c + 1))
                        if c >= 4:
                            act.wait_ge(down_done, b * HC2 + (c - 3))
                        else:
                            act.wait_ge(residual, updates(sub, b))
                        nc.scalar.activation(g_hi[0:r, c % 4, :], gate_[0:r, c % 2, :], ACT.Copy).then_inc(g_hi_ready, 1)

                    def turn_of(b, first, more):
                        act.wait_ge(low_done, b + 1)
                        for j in range(2):
                            last = nc.scalar.activation(lowT[:, j, :], ps[0:96, 6, 0:SEQ], ACT.Copy, scale=lmask[:, j:j + 1])
                        last.then_inc(low_hi_ready, 1)
                        for c in range(HC2):
                            r, s, bank = rows(c), c % 2, 2 + c % 4
                            if first and c + AHEAD < HC2:
                                cut_chunk(c + AHEAD)
                            act.wait_ge(up_done, b * HC2 + (c + 1))
                            if not (first and c < 2):
                                act.wait_ge(g_ready, b * HC2 + (c - 1))
                            nc.scalar.activation(tanh_[0:r, s, :], ps[0:r, bank, 0:SEQ], ACT.Tanh, scale=0.5).then_inc(tanhed, 1)
                            if c >= 1:
                                high_gate(b, c - 1)
                        if more:
                            norm_scalar(act, sub, b + 1, xT2_hi, XBANK)
                        high_gate(b, HC2 - 1)
                        act.wait_ge(down_done, b * HC2 + HC2)
                        nc.scalar.activation(low2T[0:RANK, :], ps[0:RANK, 7, 0:SEQ], ACT.Copy, scale=2.0).then_inc(low2_ready, 1)

                    await_group(act, "f2")
                    await_group(act, "f2_mask")
                    act.wait_ge(zeroed, 1)
                    nc.scalar.activation(a13_hi[:, :, :], l2_a13[:, :, :], ACT.Copy)
                    nc.scalar.activation(b13_parts[:, :], l2_b13[:, :], ACT.Copy).then_inc(hi_cut, 1)
                    norm_scalar(act, sub, 0, xT2_hi, XBANK)
                    for c in range(AHEAD):
                        cut_chunk(c)
                    each_turn(act, turn_of)

                @block.tensor
                def _(pe):
                    def xT_parts(k):
                        return xT2_hi[:, k, :], xT2_lo[:, k, :]

                    def turn_of(b, first, more):
                        pe.wait_ge(lo_ready, b * QT + QT)
                        if first:
                            pe.wait_ge(lo_cut, 1)
                        for k in range(KC):
                            last = product(ps[0:96, 6, 0:SEQ], (a13_hi[:, k, :], a13_lo[:, k, :]), xT_parts(k), k == 0, k == KC - 1)
                        last.then_inc(low_done, 1)

                        def up(c):
                            r = rows(c)
                            if first:
                                pe.wait_ge(lo_cut, c + 2)
                            if c >= 4:
                                pe.wait_ge(g_ready, b * HC2 + (c - 3))
                            for j in range(2):
                                o = ps[0:r, 2 + c % 4, j * SEQ:(j + 1) * SEQ]
                                for k in range(KC):
                                    at = slice(j * HID2 + c * P, j * HID2 + c * P + r)
                                    product(o, (w13_hi[:, k, at], w13_lo[:, k, at]), xT_parts(k), k == 0, False)
                                if c == 0 and j == 0:
                                    pe.wait_ge(lowT_ready, b + 1)
                                last = nc.tensor.matmul(o, b13_parts[:, c * P:c * P + r], lowT[:, j, :], start=False, stop=True)
                            last.then_inc(up_done, 1)

                        def down(c):
                            r, s = rows(c), c % 4
                            pe.wait_ge(g_lo_ready, b * HC2 + (c + 1))
                            if c == 0:
                                pe.wait_ge(residual, updates(sub, b))
                            for i in range(QT):
                                at = slice(i * P, (i + 1) * P)
                                product(ps[:, i, :], (g_hi[0:r, s, at], g_lo[0:r, s, at]), (w2_hi[0:r, c, :], w2_lo[0:r, c, :]), c == 0, False)
                            last = product(ps[0:RANK, 7, 0:SEQ], (a2_hi[0:r, c, :], a2_lo[0:r, c, :]), (g_hi[0:r, s, :], g_lo[0:r, s, :]),
                                           c == 0, c == HC2 - 1)
                            last.then_inc(down_done, 1)

                        for c in range(HC2 + 2):
                            if c < HC2:
                                up(c)
                            if c == HC2 and more:
                                norm_tensor(pe, sub, b + 1, xn2, XBANK)
                            if c >= 2:
                                down(c - 2)
                        pe.wait_ge(low2_ready, b + 1)
                        for i in range(QT):
                            last = nc.tensor.matmul(ps[:, i, :], low2T[:, i * P:(i + 1) * P], l2_b2[:, :], start=False, stop=True)
                        last.then_inc(done, 1)

                    await_group(pe, "f2")
                    pe.wait_ge(zeroed, 1)
                    norm_tensor(pe, sub, 0, xn2, XBANK)
                    each_turn(pe, turn_of)

        def layer3_feed_forward(sub):
            hi_cut = sem("f3_hi_cut")
            lo_cut = sem("f3_lo_cut")
            lat_done = sem("f3_lat_done")
            lat_hi_ready = sem("f3_lat_hi_ready")
            lat_lo_ready = sem("f3_lat_lo_ready")
            logitsT_ready = sem("f3_logitsT_ready")
            logits_done = sem("f3_logits_done")
            expert_done = sem("f3_expert_done")
            exp_hi_ready = sem("f3_exp_hi_ready")
            exp_lo_ready = sem("f3_exp_lo_ready")
            up_done = sem("f3_up_done")
            relued = sem("f3_relued")
            squared = sem("f3_squared")
            h_hi_ready = sem("f3_h_hi_ready")
            h_lo_ready = sem("f3_h_lo_ready")
            down_done = sem("f3_down_done")
            shared_kept = sem("f3_shared_kept")
            summed = sem("f3_summed")
            chain_sem = sem("f3_chain")
            logits_kept = sem("f3_logits_kept")
            routing_ready = sem("f3_routing_ready")
            yvar = sem("f3_yvar")
            pool_chain = sem("f3_pool_chain")
            yrstd_ready = sem("f3_yrstd_ready")
            stored = sem("f3_stored")
            final = sem("f3_final")
            XBANK = 5, -3
            AHEAD = 2

            def bank_of(c):
                return 2 + (c + 3) % 4

            with nc.Block() as block:
                @block.sync
                def _(sp):
                    with sp.Fori(0, BATCH) as b:
                        for i in range(QT):
                            sp.wait_ge(final, b * QT + (i + 1))
                            sp.dma_start(out[bass.ds(b * QT + i, 1), :, :].rearrange("a p d -> p (a d)"), tile_of(b, i)).then_inc(stored, 16)
                    sp.wait_ge(stored, 16 * TILES)

                @block.gpsimd
                def _(pool):
                    norm_gpsimd(pool, sub, 0)

                    def turn_of(b, first, more):
                        for c in range(IC3):
                            pool.wait_ge(relued, b * IC3 + (c + 1))
                            if not (first and c < 2):
                                pool.wait_ge(h_lo_ready, b * IC3 + (c - 1))
                            nc.gpsimd.tensor_tensor(square[:, c % 2, :], relu_[:, c % 2, :], relu_[:, c % 2, :], ALU.mult).then_inc(squared, 1)
                            if more and c == 4:
                                norm_gpsimd(pool, sub, b + 1)
                        pool.wait_ge(yvar, b + 1)
                        nc.gpsimd.tensor_tensor(yrstd[:, :, 0], ymv[:, :, 1], eps[:, :].to_broadcast([P, QT]), ALU.add).then_inc(pool_chain, 1)
                        pool.wait_ge(pool_chain, b + 1)
                        nc.gpsimd.tensor_tensor(yrstd[:, :, 0], yrstd[:, :, 0], minus_half[:, :].to_broadcast([P, QT]),
                                                ALU.pow).then_inc(yrstd_ready, 1)

                    each_turn(pool, turn_of)

                @block.vector
                def _(dve):
                    gamma, beta = (l3_gb[:, j * DIM:(j + 1) * DIM].unsqueeze(1).to_broadcast([P, QT, DIM]) for j in range(2))

                    def cut_chunk(c):
                        dve.wait_ge(hi_cut, c + 2)
                        at = slice(c * P, (c + 1) * P)
                        subtract_high(nc.vector, up_lo[:, :, at], l3_up[:, :, at], up_hi[:, :, at])
                        subtract_high(nc.vector, down_lo[:, c, :], l3_down[:, c, :], down_hi[:, c, :]).then_inc(lo_cut, 1)

                    def scale_out(b, step):
                        turn = b * 3
                        if step == 0:
                            dve.wait_ge(yrstd_ready, b + 1)
                            for i in range(QT):
                                last = nc.vector.tensor_scalar(shared[:, i, :], shared[:, i, :], ymv[:, i, 0:1], yrstd[:, i, :],
                                                               ALU.subtract, ALU.mult)
                            last.then_inc(chain_sem, 1)
                        elif step == 1:
                            dve.wait_ge(chain_sem, turn + 1)
                            nc.vector.tensor_tensor(shared[:, :, :], shared[:, :, :], gamma, ALU.mult).then_inc(chain_sem, 1)
                        elif step == 2:
                            dve.wait_ge(chain_sem, turn + 2)
                            nc.vector.tensor_tensor(shared[:, :, :], shared[:, :, :], beta, ALU.add).then_inc(chain_sem, 1)
                        elif step == 3:
                            dve.wait_ge(chain_sem, turn + 3)
                            for i in range(QT):
                                nc.vector.tensor_tensor(tile_of(b, i), shared[:, i, :], tile_of(b, i), ALU.add).then_inc(final, 1)

                    def turn_of(b, first, more):
                        dve.wait_ge(lat_hi_ready, b + 1)
                        subtract_high(nc.vector, lat_lo[:, :, :], ps[:, 2, :].rearrange("p (m t) -> p m t", m=LC3), lat_hi[:, :, :])\
                            .then_inc(lat_lo_ready, 1)
                        dve.wait_ge(exp_hi_ready, b + 1)
                        subtract_high(nc.vector, exp_lo[:, :, :], ps[:, 4, :].rearrange("p (m t) -> p m t", m=LC3), exp_hi[:, :, :])\
                            .then_inc(exp_lo_ready, 1)
                        dve.wait_ge(logits_done, b + 1)
                        nc.vector.tensor_copy(logits3[:, :, :], ps[:, 3, 0:QT * E3].rearrange("p (i e) -> p i e", i=QT)).then_inc(logits_kept, 1)
                        dve.drain()
                        for i in range(QT):
                            nc.vector.max(top8[:, i, :], logits3[:, i, :])
                        dve.drain()
                        nc.vector.tensor_tensor(routing[:, :], top8[:, :, 0], top8[:, :, 1], ALU.add).then_inc(routing_ready, 1)
                        for c in range(IC3):
                            if first and c + AHEAD < IC3:
                                cut_chunk(c + AHEAD)
                            dve.wait_ge(h_hi_ready, b * IC3 + (c + 1))
                            subtract_high(nc.vector, h_lo[:, c % 4, :], square[:, c % 2, :], h_hi[:, c % 4, :]).then_inc(h_lo_ready, 1)
                            if not first:
                                scale_out(b - 1, c)
                            if more and c == 4:
                                norm_stats(dve, sub, b + 1)
                            if more and c == 6:
                                norm_apply(dve, sub, b + 1, xn3)
                        if more:
                            split_xT(dve, sub, b + 1, xT3_hi, xT3_lo, XBANK[0], lo_ready, XBANK[1])
                        dve.wait_ge(routing_ready, b + 1)
                        for i in range(QT):
                            dve.wait_ge(shared_kept, b * QT + (i + 1))
                            nc.vector.scalar_tensor_tensor(shared[:, i, :], ps[:, 6 + i, :], routing[:, i:i + 1], shared[:, i, :],
                                                           ALU.mult, ALU.add).then_inc(summed, 1)
                        dve.drain()
                        for i in range(QT):
                            nc.vector.bn_stats(ystats[:, i, :], shared[:, i, :])
                        dve.drain()
                        for i in range(QT):
                            last = nc.vector.bn_aggr(ymv[:, i, :], ystats[:, i, :])
                        last.then_inc(yvar, 1)

                    await_group(dve, "f3")
                    norm_stats(dve, sub, 0)
                    norm_apply(dve, sub, 0, xn3)
                    dve.wait_ge(hi_cut, 1)
                    subtract_high(nc.vector, fc1_lo[:, :, :], l3_fc1[:, :, :], fc1_hi[:, :, :])
                    split_xT(dve, sub, 0, xT3_hi, xT3_lo, XBANK[0], lo_ready, XBANK[1])
                    subtract_high(nc.vector, expert_lo[:, :, :], l3_expert[:, :, :], expert_hi[:, :, :])
                    subtract_high(nc.vector, fc2_lo[:, :, :], l3_fc2[:, :, :], fc2_hi[:, :, :]).then_inc(lo_cut, 1)
                    for c in range(AHEAD):
                        cut_chunk(c)
                    each_turn(dve, turn_of)
                    for step in range(4):
                        scale_out(BATCH - 1, step)

                @block.scalar
                def _(act):
                    def cut_chunk(c):
                        at = slice(c * P, (c + 1) * P)
                        nc.scalar.activation(up_hi[:, :, at], l3_up[:, :, at], ACT.Copy)
                        nc.scalar.activation(down_hi[:, c, :], l3_down[:, c, :], ACT.Copy).then_inc(hi_cut, 1)

                    def high_square(b, first, c):
                        act.wait_ge(squared, b * IC3 + (c + 1))
                        if not (first and c < 4):
                            act.wait_ge(down_done, b * IC3 + (c - 3))
                        nc.scalar.activation(h_hi[:, c % 4, :], square[:, c % 2, :], ACT.Copy).then_inc(h_hi_ready, 1)

                    def turn_of(b, first, more):
                        act.wait_ge(lat_done, b + 1)
                        nc.scalar.activation(lat_hi[:, :, :], ps[:, 2, :].rearrange("p (m t) -> p m t", m=LC3), ACT.Copy).then_inc(lat_hi_ready, 1)
                        nc.scalar.activation(logitsT[:, :], ps[0:E3, 3, 0:SEQ], ACT.Copy).then_inc(logitsT_ready, 1)
                        act.wait_ge(expert_done, b + 1)
                        nc.scalar.activation(exp_hi[:, :, :], ps[:, 4, :].rearrange("p (m t) -> p m t", m=LC3), ACT.Copy).then_inc(exp_hi_ready, 1)
                        for c in range(IC3):
                            if first and c + AHEAD < IC3:
                                cut_chunk(c + AHEAD)
                            act.wait_ge(up_done, b * IC3 + (c + 1))
                            if not (first and c < 2):
                                act.wait_ge(squared, b * IC3 + (c - 1))
                            nc.scalar.activation(relu_[:, c % 2, :], ps[:, bank_of(c), 0:SEQ], ACT.Relu).then_inc(relued, 1)
                            if c >= 1:
                                high_square(b, first, c - 1)
                        if more:
                            norm_scalar(act, sub, b + 1, xT3_hi, *XBANK)
                        high_square(b, first, IC3 - 1)
                        act.wait_ge(down_done, b * IC3 + IC3)
                        if not first:
                            act.wait_ge(final, b * QT)
                        for i in range(QT):
                            nc.scalar.activation(shared[:, i, :], ps[:, i, :], ACT.Copy).then_inc(shared_kept, 1)

                    await_group(act, "f3")
                    nc.scalar.activation(fc1_hi[:, :, :], l3_fc1[:, :, :], ACT.Copy)
                    nc.scalar.activation(expert_hi[:, :, :], l3_expert[:, :, :], ACT.Copy)
                    nc.scalar.activation(fc2_hi[:, :, :], l3_fc2[:, :, :], ACT.Copy).then_inc(hi_cut, 1)
                    norm_scalar(act, sub, 0, xT3_hi, *XBANK)
                    for c in range(AHEAD):
                        cut_chunk(c)
                    each_turn(act, turn_of)

                @block.tensor
                def _(pe):
                    def xT_parts(k):
                        return xT3_hi[:, k, :], xT3_lo[:, k, :]

                    def turn_of(b, first, more):
                        pe.wait_ge(lo_ready, (BATCH + b) * QT + QT)
                        if first:
                            pe.wait_ge(lo_cut, 1)
                        for m in range(LC3):
                            for k in range(KC):
                                at = slice(m * P, (m + 1) * P)
                                product(ps[:, 2, m * SEQ:(m + 1) * SEQ], (fc1_hi[:, k, at], fc1_lo[:, k, at]), xT_parts(k), k == 0, k == KC - 1)
                        for k in range(KC):
                            at = slice(LAT3, LAT3 + E3)
                            last = product(ps[0:E3, 3, 0:SEQ], (fc1_hi[:, k, at], fc1_lo[:, k, at]), xT_parts(k), k == 0, k == KC - 1)
                        last.then_inc(lat_done, 1)

                        def up(c):
                            if first:
                                pe.wait_ge(lo_cut, c + 2)
                            if c >= 4:
                                pe.wait_ge(relued, b * IC3 + (c - 3))
                            for k in range(KC):
                                at = slice(c * P, (c + 1) * P)
                                last = product(ps[:, bank_of(c), 0:SEQ], (up_hi[:, k, at], up_lo[:, k, at]), xT_parts(k), k == 0, k == KC - 1)
                            last.then_inc(up_done, 1)

                        def down(c):
                            pe.wait_ge(h_lo_ready, b * IC3 + (c + 1))
                            for i in range(QT):
                                at = slice(i * P, (i + 1) * P)
                                last = product(ps[:, i, :], (h_hi[:, c % 4, at], h_lo[:, c % 4, at]), (down_hi[:, c, :], down_lo[:, c, :]),
                                               c == 0, c == IC3 - 1)
                            last.then_inc(down_done, 1)

                        def expert():
                            pe.wait_ge(lat_lo_ready, b + 1)
                            for m in range(LC3):
                                for l in range(LC3):
                                    at = slice(m * P, (m + 1) * P)
                                    last = product(ps[:, 4, m * SEQ:(m + 1) * SEQ], (expert_hi[:, l, at], expert_lo[:, l, at]),
                                                   (lat_hi[:, l, :], lat_lo[:, l, :]), l == 0, l == LC3 - 1)
                            last.then_inc(expert_done, 1)

                        def flip_logits():
                            pe.wait_ge(logitsT_ready, b + 1)
                            for i in range(QT):
                                last = nc.tensor.matmul(ps[:, 3, i * E3:(i + 1) * E3], logitsT[:, i * P:(i + 1) * P], ident[0:E3, 0:E3],
                                                        start=True, stop=True)
                            last.then_inc(logits_done, 1)

                        def routed():
                            pe.wait_ge(exp_lo_ready, b + 1)
                            if not first:
                                pe.wait_ge(summed, b * QT)
                            for i in range(QT):
                                for l in range(LC3):
                                    at = slice(i * P, (i + 1) * P)
                                    product(ps[:, 6 + i, :], (exp_hi[:, l, at], exp_lo[:, l, at]), (fc2_hi[:, l, :], fc2_lo[:, l, :]),
                                            l == 0, l == LC3 - 1)

                        up(0)
                        expert()
                        flip_logits()
                        up(1)
                        routed()
                        pe.wait_ge(logits_kept, b + 1)
                        for c in range(2, IC3 + 2):
                            if c < IC3:
                                up(c)
                            if c == IC3 and more:
                                norm_tensor(pe, sub, b + 1, xn3, *XBANK)
                            down(c - 2)

                    norm_tensor(pe, sub, 0, xn3, *XBANK)
                    each_turn(pe, turn_of)

        val_set0 = sem("mid_zeroed")

        layer0_attention()
        layer0_feed_forward(1)
        attention(0, 2, l1_qkv, l1_wo, "a1", None, ("f1", "a2"))
        layer1_feed_forward(3)
        attention(1, 4, l2_qkv, l2_wo, "a2", None, ("f2",))
        layer2_feed_forward(5)
        attention(2, 6, l3_qkv, None, "a3", "a3_bias", ("a3_bias", "f3"))
        layer3_feed_forward(7)

def _chunks(w, k):
    return w.reshape(k, 128, w.shape[1]).transpose(1, 0, 2)


def _tables():
    import numpy as np

    def bf16(v):
        return (np.ascontiguousarray(v, np.float32).view(np.uint32) >> 16).astype(np.uint16)
    t = {}
    pos = np.arange(256, dtype=np.float32)
    inv = 1.0 / 500000.0 ** (np.arange(0, 128, 2, dtype=np.float32) / 128)
    wavelen = 2.0 * np.pi / inv
    scaled = np.where(wavelen > 1024 / 1.0, inv / 8.0, inv)
    smooth = (1024 / wavelen - 1.0) / (4.0 - 1.0)
    smoothed = (1.0 - smooth) / 8.0 * inv + smooth * inv
    medium = (wavelen <= 1024 / 1.0) & (wavelen >= 1024 / 4.0)
    inv0 = np.where(medium, smoothed, scaled).astype(np.float32)
    ang = (pos[:, None] * inv0[None, :]).astype(np.float32)
    t["l0_cos"] = np.concatenate([np.cos(ang), np.cos(ang)], 1).T.astype(np.float32)
    t["l0_sin"] = np.concatenate([-np.sin(ang), np.sin(ang)], 1).T.astype(np.float32)
    f = (1.0 / 10000.0 ** (np.arange(0, 16, 2, dtype=np.float32) / 16)).astype(np.float32)
    ang = (pos[:, None] * f[None, :]).astype(np.float32)
    cs = np.stack([np.concatenate([np.cos(ang), np.cos(ang)], 1),
                   np.concatenate([-np.sin(ang), np.sin(ang)], 1)], 1)
    t["rope"] = cs.reshape(2, 128, 2, 16).transpose(1, 0, 2, 3).astype(np.float32)
    t["ident"] = np.eye(128, dtype=np.float32)
    t["ident_bf"] = bf16(np.eye(128))
    i = np.arange(128)
    rows_q = np.where(i[None, :] > i[:, None], -1.0e30, 0.0)
    t["masks"] = bf16(np.stack([rows_q, rows_q.T], 1))
    t["lmask"] = np.tile(np.repeat(np.eye(2, dtype=np.float32) * 2.0, 16, axis=0), (3, 1))
    for e in (4, 8):
        low = np.tril(np.ones((e, e), np.float32), -1).reshape(1, e * e)
        t[f"lower{e}"] = np.ascontiguousarray(np.broadcast_to(low, (128, e * e)))
    return {k: np.ascontiguousarray(v) for k, v in t.items()}


def _rows(v):
    import numpy as np
    return np.ascontiguousarray(np.broadcast_to(v.reshape(1, -1), (128, v.size)))


def _layout(a):
    import numpy as np
    o = {}
    o["x"] = a["L0_attn_x"].reshape(8, 128, 512)
    o["l0_wq"] = _chunks(a["L0_attn_Wq"].T, 4).reshape(128, 4, 8, 512).transpose(2, 0, 1, 3)
    o["l0_wk"] = _chunks(a["L0_attn_Wk"].T, 4).reshape(128, 4, 8, 128).transpose(2, 0, 1, 3)
    o["l0_wv"] = _chunks(a["L0_attn_Wv"].T, 4).reshape(128, 4, 4, 256).transpose(2, 0, 1, 3)
    o["l0_wo"] = a["L0_attn_Wo"].T.reshape(8, 4, 128, 512).transpose(0, 2, 1, 3)
    o["l0_ar"] = _chunks(np.concatenate([a["L0_ffn_A"].reshape(64, 512), a["L0_ffn_router_w"]], 0).T, 4)
    o["l0_b"] = np.concatenate([a["L0_ffn_B"].transpose(0, 2, 1).reshape(64, 512), np.zeros((64, 512), np.float32)], 0)
    def halves(w, n):
        return w.reshape(512, n, 8, 2).transpose(0, 1, 3, 2).reshape(512, n * 16)
    o["l1_qkv"] = _chunks(np.concatenate([halves(a["L1_attn_wq"], 32), halves(a["L1_attn_wk"], 8), a["L1_attn_wv"]], 1), 4)
    o["l1_wo"] = _chunks(a["L1_attn_wo"], 4)
    o["l1_w"] = _chunks(a["L1_ffn_weight"].T, 4)
    o["l1_ag"] = _chunks(np.concatenate([a["L1_ffn_lora_A"].transpose(1, 0, 2).reshape(512, 128), a["L1_ffn_gw1"].T], 1), 4)
    o["l1_b"] = a["L1_ffn_lora_B"].reshape(128, 512)
    o["l1_gvec"] = np.concatenate([_rows(a["L1_ffn_gb1"]), _rows(a["L1_ffn_ln_gamma"]), _rows(a["L1_ffn_ln_beta"]), _rows(a["L1_ffn_gb2"])], 1)
    o["l1_gw2"] = a["L1_ffn_gw2"].T
    o["l2_qkv"] = _chunks(np.concatenate([a["L2_attn_wq"].T, a["L2_attn_wk"].T, a["L2_attn_wv"].T], 1), 4)
    o["l2_wo"] = _chunks(a["L2_attn_wo"].T, 4)
    o["l2_w13"] = np.concatenate([_chunks(a["L2_ffn_w1"].T, 4), _chunks(a["L2_ffn_w3"].T, 4)], 2)
    w2 = np.zeros((11 * 128, 512), np.float32)
    w2[:1376] = a["L2_ffn_w2"].T
    o["l2_w2"] = _chunks(w2, 11)
    o["l2_a13"] = _chunks(np.concatenate([a["L2_ffn_lora_A1"], a["L2_ffn_lora_A3"]] * 3, 0).T, 4)
    o["l2_b13"] = np.concatenate([a["L2_ffn_lora_B1"].T, a["L2_ffn_lora_B3"].T] * 3, 0)
    a2 = np.zeros((11 * 128, 16), np.float32)
    a2[:1376] = a["L2_ffn_lora_A2"].T
    o["l2_a2"] = _chunks(a2, 11)
    o["l2_b2"] = np.concatenate([a["L2_ffn_lora_B2"].T, np.zeros((80, 512), np.float32)], 0)
    wq3 = a["L3_attn_Wq"].reshape(2, 16, 16, 512).transpose(1, 0, 2, 3).reshape(512, 512)
    bq3 = a["L3_attn_bq"].reshape(2, 16, 16).transpose(1, 0, 2).reshape(512)
    o["l3_qkv"] = _chunks(np.concatenate([wq3.T, a["L3_attn_Wk"].T, a["L3_attn_Wv"].T], 1), 4)
    o["l3_bias"] = _rows(np.concatenate([bq3, a["L3_attn_bk"], a["L3_attn_bv"]]))
    o["l3_up"] = _chunks(a["L3_ffn_up_w"], 4)
    o["l3_down"] = _chunks(a["L3_ffn_down_w"], 8)
    o["l3_fc1"] = _chunks(np.concatenate([a["L3_ffn_fc1_w"], a["L3_ffn_gate_w"]], 1), 4)
    o["l3_expert"] = _chunks(a["L3_ffn_expert_w"], 2)
    o["l3_fc2"] = _chunks(a["L3_ffn_fc2_w"], 2)
    o["l3_gb"] = np.concatenate([_rows(a["L3_ffn_ln_gamma"]), _rows(a["L3_ffn_ln_beta"])], 1)
    return {k: np.ascontiguousarray(v) for k, v in o.items()}


def kernel(**inputs):
    import numpy as np
    import concourse.bacc as bacc
    from concourse import mybir as mb
    from concourse.bass_utils import run_bass_kernel_spmd

    nc = bacc.Bacc("TRN2", target_bir_lowering=False, num_devices=1)
    laid = _layout({k: np.asarray(v) for k, v in inputs.items()})
    laid.update(_tables())
    arrays, dram = {}, {}
    for name, v in laid.items():
        arrays[f"{name}_dram"] = v
        dram[name] = nc.dram_tensor(f"{name}_dram", v.shape, mb.dt.from_np(v.dtype), kind="ExternalInput").ap()
    out = nc.dram_tensor("out_dram", (8, 128, 512), mb.dt.float32, kind="ExternalOutput").ap()
    four_layers(nc, dram, out)
    r = run_bass_kernel_spmd(nc, [arrays], core_ids=[0])
    return r.results[0]["out_dram"].reshape(4, 256, 512)
```

```python
from contextlib import ExitStack

import concourse.bass as bass
from concourse import mybir

F32 = mybir.dt.float32
BF16 = mybir.dt.bfloat16
F32R = mybir.dt.float32r
ALU = mybir.AluOpType
ACT = mybir.ActivationFunctionType
AX = mybir.AxisListType

BATCH, SEQ, DIM = 4, 256, 512
P = 128
KC = DIM // P
QT = SEQ // P
TILES = BATCH * QT
EPS = 1e-5
MASKED = -1.0e30

H0, G0, D0 = 32, 8, 128
R0 = H0 // G0
SCALE0 = 1.0 / float(D0) ** 0.5
PROJ0 = G0 * (R0 + 1)

HEADS, HD = 32, 16
KV_HEADS = (8, 8, 16)
SCALES = (0.25, 0.25, 1.0 / 32.0 ** 0.5)
STACK = 6 * HD
UNITS = HEADS // 4
VPAD = 32

E0, RANK = 4, 16
E1 = 8
CAPACITY = int(3.0 * TILES * P / E1)
HID2 = 1376
HC2 = (HID2 + P - 1) // P
HLAST2 = HID2 - (HC2 - 1) * P
INT3, LAT3, E3 = 1024, 256, 8
IC3, LC3 = INT3 // P, LAT3 // P


class Chain:

    def __init__(self, eng, sem, per_turn, before=0):
        self.eng, self.sem, self.per, self.before, self.k = eng, sem, per_turn, before, 0

    def start(self, turn):
        self.turn, self.k = turn, 0

    def link(self, ins):
        self.k += 1
        ins.then_inc(self.sem, 1)
        self.eng.wait_ge(self.sem, self.turn * self.per + (self.before + self.k))

    def end(self):
        assert self.k == self.per, (self.k, self.per)


def four_layers(nc, dram, out):
    with ExitStack() as stack:
        def sem(name):
            return stack.enter_context(nc.semaphore(name))

        def keep(name, shape, dtype=F32):
            return stack.enter_context(nc.sbuf_tensor(name, shape, dtype))

        def words(t):
            return t[...].bitcast(mybir.dt.uint16) if t.dtype == BF16 else t[...]

        x = keep("x", [P, TILES, DIM])
        ident = keep("ident", [P, P])
        ident_bf = keep("ident_bf", [P, P], BF16)
        masks = keep("masks", [P, 2, P], BF16)
        stats = keep("stats", [P, QT, 6])
        mean_var = keep("mean_var", [P, QT, 2])
        rstd = keep("rstd", [P, QT, 1])
        minus_half = keep("minus_half", [P, 1])
        eps = keep("eps", [P, 1])

        base = (nc.sbuf_base + 63) // 64 * 64
        top = [base]
        where = {}

        def place(name, shape, dtype=F32, at=None):
            size = 1
            for s in shape[1:]:
                size *= s
            size = (size * (2 if dtype == BF16 else 4) + 63) // 64 * 64
            if at is None:
                at = top[0]
                top[0] += size
            where[name] = at
            return nc.alloc_sbuf_tensor_at(name, shape, dtype, offset=at), at + size

        ps = stack.enter_context(nc.psum_tensor("ps", [P, 8, 512], F32))
        ps_bf = ps[:, :, :].bitcast(BF16)

        consts_in = sem("consts_in")
        x_in = [sem(f"x_in{b}") for b in range(BATCH)]
        normed = sem("normed")
        rstd_ready = sem("rstd_ready")
        var_ready = sem("var_ready")
        pool_norm_chain = sem("pool_norm_chain")
        flipped = sem("flipped")
        xT_ready = sem("xT_ready")
        residual = sem("residual")

        def updates(sub, b=0):
            return (G0 + sub - 1) * TILES + b * QT
        half_ready = sem("half_ready")

        def norm_stats(dve, sub, b, after=None):
            if sub == 0:
                dve.wait_ge(x_in[b], 16 * QT)
            else:
                dve.wait_ge(residual, after or updates(sub))
            for i in range(QT):
                nc.vector.bn_stats(stats[:, i, :], x[:, bass.ds(b * QT + i, 1), :].rearrange("p a d -> p (a d)"))
            dve.drain()
            for i in range(QT):
                nc.vector.bn_aggr(mean_var[:, i, :], stats[:, i, :]).then_inc(var_ready, 1)

        def norm_apply(dve, sub, b, xn):
            turn = sub * BATCH + b
            for i in range(QT):
                tile = x[:, bass.ds(b * QT + i, 1), :].rearrange("p a d -> p (a d)")
                dve.wait_ge(rstd_ready, turn * QT + (i + 1))
                nc.vector.tensor_scalar(xn[:, i, :], tile, mean_var[:, i, 0:1], rstd[:, i, :],
                                        ALU.subtract, ALU.mult).then_inc(normed, 1)

        def norm_vector(dve, sub, b, xn):
            norm_stats(dve, sub, b)
            norm_apply(dve, sub, b, xn)

        def norm_gpsimd(pool, sub, b):
            turn = sub * BATCH + b
            for i in range(QT):
                pool.wait_ge(var_ready, turn * QT + (i + 1))
                nc.gpsimd.tensor_tensor(rstd[:, i, :], mean_var[:, i, 1:2], eps[:, :], ALU.add).then_inc(pool_norm_chain, 1)
                pool.wait_ge(pool_norm_chain, turn * QT + (i + 1))
                nc.gpsimd.tensor_tensor(rstd[:, i, :], rstd[:, i, :], minus_half[:, :], ALU.pow).then_inc(rstd_ready, 1)

        def norm_tensor(pe, sub, b, xn, bank=0, step=1):
            turn = sub * BATCH + b
            for i in range(QT):
                pe.wait_ge(normed, turn * QT + (i + 1))
                for k in range(KC):
                    last = nc.tensor.transpose(ps[:, bank + i * step, k * P:(k + 1) * P], xn[:, i, k * P:(k + 1) * P], ident[:, :])
                last.then_inc(flipped, 1)

        def norm_scalar(act, sub, b, xT, bank=0, step=1):
            turn = sub * BATCH + b
            for i in range(QT):
                act.wait_ge(flipped, turn * QT + (i + 1))
                nc.scalar.activation(xT[:, :, i * P:(i + 1) * P], ps[:, bank + i * step, :].rearrange("p (k t) -> p k t", k=KC),
                                     ACT.Copy).then_inc(xT_ready, 1)

        def subtract_high(eng, lo, value, hi):
            return eng.tensor_tensor(lo, value, hi.bitcast(F32), ALU.subtract)

        def product(o, lhs, rhs, start, stop):
            nc.tensor.matmul(o, lhs[0], rhs[0], start=start, stop=False)
            nc.tensor.matmul(o, lhs[0], rhs[1], start=False, stop=False)
            return nc.tensor.matmul(o, lhs[1], rhs[0], start=False, stop=stop)

        def split_xT(dve, sub, b, hi, lo, bank, ready, step=1):
            for i in range(QT):
                dve.wait_ge(xT_ready, (sub * BATCH + b) * QT + (i + 1))
                subtract_high(nc.vector, lo[:, :, i * P:(i + 1) * P], ps[:, bank + i * step, :].rearrange("p (k t) -> p k t", k=KC),
                              hi[:, :, i * P:(i + 1) * P]).then_inc(ready, 1)

        LAYER0_END = base + 180 * 1024

        def layer0_attention():
            PAIRS0 = G0 // 2
            top[0] = base
            wq, _ = place("l0_wq", [P, 2, KC, R0 * D0])
            wk, _ = place("l0_wk", [P, 2, KC, D0])
            wo, _ = place("l0_wo", [P, 2, R0, DIM])
            wv, _ = place("l0_wv", [P, KC, 2 * D0])
            wq_lo, _ = place("l0_wq_lo", [P, 2, KC, R0 * D0], F32R, at=where["l0_wq"])
            wk_lo, _ = place("l0_wk_lo", [P, 2, KC, D0], F32R, at=where["l0_wk"])
            wo_lo, _ = place("l0_wo_lo", [P, 2, R0, DIM], F32R, at=where["l0_wo"])
            wv_lo, _ = place("l0_wv_lo", [P, KC, 2 * D0], F32R, at=where["l0_wv"])
            wq_hi, _ = place("l0_wq_hi", [P, 2, KC, R0 * D0], F32R)
            wk_hi, _ = place("l0_wk_hi", [P, 2, KC, D0], F32R)
            wo_hi, _ = place("l0_wo_hi", [P, 2, R0, DIM], F32R)
            wv_hi, _ = place("l0_wv_hi", [P, KC, 2 * D0], F32R)
            cos, _ = place("l0_cos", [P, SEQ])
            sin, _ = place("l0_sin", [P, SEQ])
            xT_hi, _ = place("l0_xT_hi", [P, KC, BATCH * SEQ], F32R)
            xT_lo, _ = place("l0_xT_lo", [P, KC, BATCH * SEQ], F32R)
            val, _ = place("l0_val", [P, BATCH, QT, 2 * D0])
            qT, _ = place("l0_qT", [P, R0, SEQ])
            kT, _ = place("l0_kT", [P, 2, SEQ])
            t_sin, _ = place("l0_t_sin", [P, 2, SEQ])
            oT_hi, _ = place("l0_oT_hi", [P, 2, SEQ], F32R)
            oT_lo, _ = place("l0_oT_lo", [P, 2, SEQ], F32R)
            rowmax, _ = place("l0_rowmax", [P, 2, QT])
            rowsum, _ = place("l0_rowsum", [P, 2, QT])
            prob, _ = place("l0_prob", [P, 2, 3 * P])
            probT, _ = place("l0_probT", [P, 2, 3 * P])
            xn, end = place("l0_xn", [P, QT, DIM])
            assert end <= LAYER0_END

            wqk_in = [sem(f"l0_wqk_in{s}") for s in range(2)]
            wo_in = [sem(f"l0_wo_in{s}") for s in range(2)]
            wv_in = sem("l0_wv_in")
            hi_cut = sem("l0_hi_cut")
            lo_cut = sem("l0_lo_cut")
            xT_lo_ready = sem("l0_xT_lo_ready")
            v_done = sem("l0_v_done")
            v_kept = sem("l0_v_kept")
            projected = sem("l0_projected")
            rope_muled = sem("l0_rope_muled")
            roped = sem("l0_roped")
            scored = sem("l0_scored")
            max_chain = sem("l0_max_chain")
            max_ready = sem("l0_max_ready")
            exped = sem("l0_exped")
            sum_inverted = sem("l0_sum_inverted")
            scaled = sem("l0_scaled")
            prob_flipped = sem("l0_prob_flipped")
            probT_ready = sem("l0_probT_ready")
            attended = sem("l0_attended")
            oT_hi_ready = sem("l0_oT_hi_ready")
            oT_ready = sem("l0_oT_ready")
            out_used = sem("l0_out_used")

            PROJ, SCORE, FLIP, OUT, ACC = 6, 2, 4, 5, 0
            UNITS0 = 2 * BATCH
            HEADS0 = UNITS0 * R0
            ORDER = [(u, h) for u in range(UNITS0) for h in [None] + list(range(R0))]
            PROJ0 = len(ORDER)
            LAG = 2

            def place_of(n):
                return (n // R0) * (R0 + 1) + 1 + n % R0

            CUTS = (("qk", 1, 7, False), ("o", 1, 11, False), ("v", 0, 17, True), ("qk", 0, 22, True), ("o", 0, 26, True))
            PER_TURN = 4 * len(CUTS)
            BEFORE = (("v", 0), ("qk", 0), ("o", 0))

            def cut_ready(p, kind, s):
                order = [(kind_, s_) for kind_, s_ in BEFORE] + [("qk", 1), ("o", 1)]
                return p * PER_TURN + 4 * (order.index((kind, s)) + 1)

            def pieces(kind, s, k):
                if kind == "v":
                    return [(wv[:, k, :], wv_hi[:, k, :], wv_lo[:, k, :])]
                if kind == "o":
                    return [(wo[:, s, k, :], wo_hi[:, s, k, :], wo_lo[:, s, k, :])]
                return [(wq[:, s, k, :], wq_hi[:, s, k, :], wq_lo[:, s, k, :]), (wk[:, s, k, :], wk_hi[:, s, k, :], wk_lo[:, s, k, :])]

            def step_at(n, more):
                for j, (kind, s, at, following) in enumerate(CUTS):
                    if at <= n < at + 4 and (more or not following):
                        return 4 * (len(BEFORE) + j) + n - at, kind, s, n - at, following
                return None

            def each_pair(eng, turn_of):
                with eng.Fori(0, PAIRS0 - 1) as p:
                    turn_of(p, True)
                turn_of(PAIRS0 - 1, False)

            with nc.Block() as block:
                @block.sync
                def _(sp):
                    def load_group(g, s):
                        for dst, name, arrived_ in ((wk, "l0_wk", wqk_in[s]), (wq, "l0_wq", wqk_in[s]), (wo, "l0_wo", wo_in[s])):
                            sp.dma_start(dst[:, s, :, :], dram[name][bass.ds(g, 1), :, :, :].rearrange("a p k n -> p (a k) n"))\
                                .then_inc(arrived_, 16)

                    for T in range(TILES):
                        sp.dma_start(x[:, T, :], dram["x"][T, :, :]).then_inc(x_in[T // QT], 16)
                        if T == 1:
                            for dst, name in ((ident, "ident"), (ident_bf, "ident_bf"), (masks, "masks"), (cos, "l0_cos"), (sin, "l0_sin")):
                                sp.dma_start(words(dst), dram[name]).then_inc(consts_in, 16)
                        if T == 3:
                            sp.dma_start(wv[:, :, :], dram["l0_wv"][0, :, :, :]).then_inc(wv_in, 16)
                            load_group(0, 0)
                    load_group(1, 1)
                    load_groups(sp, "f0")
                    with sp.Fori(0, PAIRS0 - 1) as p:
                        sp.wait_ge(v_done, p * 4 + 4)
                        sp.dma_start(wv[:, :, :], dram["l0_wv"][bass.ds(p + 1, 1), :, :, :].rearrange("a p k n -> p (a k) n")).then_inc(wv_in, 16)
                        for s in range(2):
                            sp.wait_ge(out_used, p * HEADS0 + 16 * (s + 1))
                            load_group(2 * p + (2 + s), s)

                @block.gpsimd
                def _(pool):
                    nc.gpsimd.memset(minus_half[:, :], -0.5).then_inc(half_ready, 1)
                    nc.gpsimd.memset(eps[:, :], EPS).then_inc(half_ready, 1)
                    pool.wait_ge(half_ready, 2)
                    for b in range(BATCH):
                        norm_gpsimd(pool, 0, b)
                    def add_rope(p, u):
                        g, h = ORDER[u]
                        pool.wait_ge(rope_muled, p * PROJ0 + (u + 1))
                        dst = kT[:, g % 2, :] if h is None else qT[:, h, :]
                        nc.gpsimd.tensor_tensor(dst, dst, t_sin[:, u % 2, :], ALU.add).then_inc(roped, 1)

                    def turn_of(p, more):
                        for n in range(HEADS0):
                            if n + 1 < HEADS0:
                                if (n + 1) % R0 == 0:
                                    add_rope(p, place_of(n + 1) - 1)
                                add_rope(p, place_of(n + 1))
                            s = n % 2
                            pool.wait_ge(sum_inverted, p * HEADS0 + (n + 1))
                            nc.gpsimd.tensor_tensor(prob[:, s, 0:P], prob[:, s, 0:P],
                                                    rowsum[:, s, 0:1].to_broadcast([P, P]), ALU.mult)
                            nc.gpsimd.tensor_tensor(prob[:, s, P:3 * P], prob[:, s, P:3 * P],
                                                    rowsum[:, s, 1:2].to_broadcast([P, 2 * P]), ALU.mult).then_inc(scaled, 1)
                        if more:
                            add_rope(p + 1, 0)
                            add_rope(p + 1, 1)

                    add_rope(0, 0)
                    add_rope(0, 1)
                    each_pair(pool, turn_of)

                @block.vector
                def _(dve):
                    def cut(number, kind, s, k):
                        dve.wait_ge(hi_cut, number + 1)
                        for value, hi, lo in pieces(kind, s, k):
                            last = subtract_high(nc.vector, lo, value, hi)
                        last.then_inc(lo_cut, 1)

                    def keep_out_low(p, n):
                        dve.wait_ge(oT_hi_ready, p * HEADS0 + (n + 1))
                        subtract_high(nc.vector, oT_lo[:, n % 2, :], ps[:, OUT, 0:SEQ], oT_hi[:, n % 2, :]).then_inc(oT_ready, 1)

                    def add_unit(p, u):
                        dve.wait_ge(out_used, p * HEADS0 + R0 * (u + 1))
                        if u > 0:
                            dve.wait_ge(residual, p * (2 * UNITS0) + 2 * u)
                        b = u % BATCH
                        for i in range(QT):
                            tile = x[:, b * QT + i, :]
                            nc.vector.tensor_tensor(tile, ps[:, ACC + i, :], tile, ALU.add).then_inc(residual, 1)

                    def mul_rope(p, u):
                        s = u % 2
                        pr = ps[:, PROJ + s, 0:SEQ]
                        dve.wait_ge(projected, p * PROJ0 + (u + 1))
                        if u >= 2:
                            dve.wait_ge(roped, p * PROJ0 + (u - 1))
                        g, h = ORDER[u]
                        if h is None and g >= 2:
                            dve.wait_ge(scored, p * HEADS0 + R0 * (g - 1))
                        if h is not None and g >= 1:
                            dve.wait_ge(scored, p * HEADS0 + (g * R0 + h - R0 + 1))
                        dst = kT[:, g % 2, :] if h is None else qT[:, h, :]
                        nc.vector.tensor_tensor(dst, pr, cos[:, :], ALU.mult)
                        nc.vector.tensor_tensor(t_sin[0:64, s, :], ps[64:128, PROJ + s, 0:SEQ], sin[0:64, :], ALU.mult)
                        nc.vector.tensor_tensor(t_sin[64:128, s, :], ps[0:64, PROJ + s, 0:SEQ], sin[64:128, :],
                                                ALU.mult).then_inc(rope_muled, 1)

                    def turn_of(p, more):
                        for n in range(HEADS0):
                            s = n % 2
                            dve.wait_ge(scored, p * HEADS0 + (n + 1))
                            nc.vector.reduce_max(rowmax[:, s, 0:1], ps[:, SCORE + s, 0:P], AX.X).then_inc(max_chain, 1)
                            nc.vector.reduce_max(rowmax[:, s, 1:2], ps[:, SCORE + s, P:3 * P], AX.X).then_inc(max_chain, 1)
                            dve.wait_ge(max_chain, p * (2 * HEADS0) + 2 * (n + 1))
                            nc.vector.tensor_scalar(rowmax[:, s, :], rowmax[:, s, :], -SCALE0, None, ALU.mult).then_inc(max_ready, 1)
                            if n + 1 < HEADS0:
                                if (n + 1) % R0 == 0:
                                    mul_rope(p, place_of(n + 1) - 1)
                                mul_rope(p, place_of(n + 1))
                            dve.wait_ge(exped, p * HEADS0 + (n + 1))
                            nc.vector.reciprocal(rowsum[:, s, :], rowsum[:, s, :]).then_inc(sum_inverted, 1)
                            step = step_at(n, more)
                            if step:
                                number, kind, group, k, _ = step
                                cut(p * PER_TURN + number, kind, group, k)
                            if n >= LAG:
                                keep_out_low(p, n - LAG)
                            if n > R0 + 1 and (n - LAG) % R0 == 0:
                                add_unit(p, (n - LAG - 1) // R0)
                        for j in range(LAG):
                            keep_out_low(p, HEADS0 - LAG + j)
                            if more:
                                mul_rope(p + 1, j)
                        add_unit(p, UNITS0 - 1)
                        dve.wait_ge(residual, (p + 1) * (2 * UNITS0))

                    dve.wait_ge(consts_in, 16 * 5)
                    def split(b):
                        at = slice(b * SEQ, (b + 1) * SEQ)
                        split_xT(dve, 0, b, xT_hi[:, :, at], xT_lo[:, :, at], 4 * (b % 2), xT_lo_ready)

                    def cut_before(first, last):
                        for j in range(first, last):
                            for k in range(4):
                                cut(4 * j + k, *BEFORE[j], k)

                    for b in range(BATCH):
                        norm_stats(dve, 0, b)
                        if b > 0:
                            split(b - 1)
                        norm_apply(dve, 0, b, xn)
                        if b == 1:
                            cut_before(0, 2)
                    split(BATCH - 1)
                    cut_before(2, 3)
                    mul_rope(0, 0)
                    mul_rope(0, 1)
                    each_pair(dve, turn_of)

                @block.scalar
                def _(act):
                    def await_weights(turn, kind, s):
                        if kind == "qk":
                            act.wait_ge(wqk_in[s], turn * 32 + 32)
                        else:
                            act.wait_ge(wo_in[s] if kind == "o" else wv_in, turn * 16 + 16)

                    def cut(kind, s, k):
                        for value, hi, lo in pieces(kind, s, k):
                            last = nc.scalar.activation(hi, value, ACT.Copy)
                        last.then_inc(hi_cut, 1)

                    def turn_of(p, more):
                        def keep_values(c):
                            act.wait_ge(v_done, p * BATCH + (c + 1))
                            nc.scalar.activation(val[:, c, :, :].rearrange("p i d -> p (i d)"), ps[:, 2 + c, :], ACT.Copy).then_inc(v_kept, 1)

                        def keep_probT(n):
                            act.wait_ge(prob_flipped, p * HEADS0 + (n + 1))
                            if n >= 2:
                                act.wait_ge(attended, p * HEADS0 + (n - 1))
                            nc.scalar.activation(probT[:, n % 2, :], ps[:, FLIP, 0:3 * P], ACT.Copy).then_inc(probT_ready, 1)

                        def keep_out_high(n):
                            act.wait_ge(attended, p * HEADS0 + (n + 1))
                            if n >= 2:
                                act.wait_ge(out_used, p * HEADS0 + (n - 1))
                            nc.scalar.activation(oT_hi[:, n % 2, :], ps[:, OUT, 0:SEQ], ACT.Copy).then_inc(oT_hi_ready, 1)

                        keep_values(0)
                        keep_values(1)
                        for n in range(HEADS0):
                            s = n % 2
                            if n >= LAG:
                                keep_probT(n - LAG)
                            act.wait_ge(max_ready, p * HEADS0 + (n + 1))
                            nc.scalar.activation(prob[:, s, 0:P], ps[:, SCORE + s, 0:P], ACT.Exp, bias=rowmax[:, s, 0:1],
                                                 scale=SCALE0, accum_out=rowsum[:, s, 0:1])
                            nc.scalar.activation(prob[:, s, P:3 * P], ps[:, SCORE + s, P:3 * P], ACT.Exp, bias=rowmax[:, s, 1:2],
                                                 scale=SCALE0, accum_out=rowsum[:, s, 1:2]).then_inc(exped, 1)
                            if n < 2:
                                keep_values(2 + n)
                            step = step_at(n, more)
                            if step:
                                number, kind, group, k, following = step
                                if k == 0:
                                    await_weights(p + 1 if following else p, kind, group)
                                cut(kind, group, k)
                            if n >= LAG:
                                keep_out_high(n - LAG)
                        for n in range(HEADS0 - LAG, HEADS0):
                            keep_probT(n)
                            keep_out_high(n)

                    for b in range(BATCH):
                        norm_scalar(act, 0, b, xT_hi[:, :, b * SEQ:(b + 1) * SEQ], 4 * (b % 2))
                        for kind, s in {1: BEFORE[:2], 3: BEFORE[2:]}.get(b, ()):
                            await_weights(0, kind, s)
                            for k in range(4):
                                cut(kind, s, k)
                    each_pair(act, turn_of)

                @block.tensor
                def _(pe):
                    def project(p, u, first=False):
                        unit, h = ORDER[u]
                        s, b = unit // BATCH, unit % BATCH
                        if not (first and u < 2):
                            pe.wait_ge(rope_muled, p * PROJ0 + (u - 1))
                        if h is None and b == 0:
                            pe.wait_ge(lo_cut, cut_ready(p, "qk", s))
                        pe.wait_ge(xT_lo_ready, QT * (b + 1))
                        tokens = slice(b * SEQ, (b + 1) * SEQ)
                        for k in range(KC):
                            w = [t[:, s, k, :] for t in (wk_hi, wk_lo)] if h is None else \
                                [t[:, s, k, h * D0:(h + 1) * D0] for t in (wq_hi, wq_lo)]
                            last = product(ps[:, PROJ + u % 2, 0:SEQ], w, (xT_hi[:, k, tokens], xT_lo[:, k, tokens]), k == 0, k == KC - 1)
                        last.then_inc(projected, 1)

                    def turn_of(p, more):
                        def project_values(c):
                            if c == 0:
                                pe.wait_ge(lo_cut, cut_ready(p, "v", 0))
                            pe.wait_ge(xT_lo_ready, QT * (c + 1 if c < 2 else BATCH))
                            for i in range(QT):
                                at = slice(c * SEQ + i * P, c * SEQ + (i + 1) * P)
                                for k in range(KC):
                                    last = product(ps[:, 2 + c, i * 2 * D0:(i + 1) * 2 * D0], (xT_hi[:, k, at], xT_lo[:, k, at]),
                                                   (wv_hi[:, k, :], wv_lo[:, k, :]), k == 0, k == KC - 1)
                            last.then_inc(v_done, 1)

                        def score(n):
                            g, s = n // R0, n % 2
                            pe.wait_ge(roped, p * PROJ0 + (place_of(n) + 1))
                            if n >= 2:
                                pe.wait_ge(exped, p * HEADS0 + (n - 1))
                            q, k_, bank = qT[:, n % R0, :], kT[:, g % 2, :], ps[:, SCORE + s, :]
                            nc.tensor.matmul(bank[:, 0:P], q[:, 0:P], k_[:, 0:P], start=True, stop=False)
                            nc.tensor.matmul(bank[:, 0:P], ident_bf[:, :], masks[:, 0, :], start=False, stop=True)
                            nc.tensor.matmul(bank[:, P:3 * P], q[:, P:SEQ], k_, start=True, stop=False)
                            nc.tensor.matmul(bank[:, 2 * P:3 * P], ident_bf[:, :], masks[:, 0, :], start=False,
                                             stop=True).then_inc(scored, 1)

                        def flip(n):
                            pe.wait_ge(scaled, p * HEADS0 + (n + 1))
                            if n >= 1:
                                pe.wait_ge(probT_ready, p * HEADS0 + n)
                            for c in range(3):
                                last = nc.tensor.transpose(ps[:, FLIP, c * P:(c + 1) * P], prob[:, n % 2, c * P:(c + 1) * P], ident[:, :])
                            last.then_inc(prob_flipped, 1)

                        def attend(n):
                            unit, slot = n // R0, n % 2
                            s, b = unit // BATCH, unit % BATCH
                            pe.wait_ge(probT_ready, p * HEADS0 + (n + 1))
                            if n >= 1:
                                pe.wait_ge(oT_ready, p * HEADS0 + n)
                            nc.tensor.matmul(ps[:, OUT, 0:2 * P], val[:, b, 0, s * D0:(s + 1) * D0], probT[:, slot, 0:2 * P],
                                             start=True, stop=False)
                            nc.tensor.matmul(ps[:, OUT, P:2 * P], val[:, b, 1, s * D0:(s + 1) * D0], probT[:, slot, 2 * P:3 * P],
                                             start=False, stop=True).then_inc(attended, 1)

                        def project_out(n):
                            unit, h = n // R0, n % R0
                            s = unit // BATCH
                            pe.wait_ge(oT_ready, p * HEADS0 + (n + 1))
                            if n % (R0 * BATCH) == 0:
                                pe.wait_ge(lo_cut, cut_ready(p, "o", s))
                            if h == 0 and unit > 0:
                                pe.wait_ge(residual, p * (2 * UNITS0) + 2 * unit)
                            for i in range(QT):
                                at = slice(i * P, (i + 1) * P)
                                last = product(ps[:, ACC + i, :], (oT_hi[:, n % 2, at], oT_lo[:, n % 2, at]),
                                               (wo_hi[:, s, h, :], wo_lo[:, s, h, :]), h == 0, h == R0 - 1)
                            last.then_inc(out_used, 1)

                        project_values(0)
                        project_values(1)
                        for n in range(HEADS0 + LAG + 1):
                            if n < HEADS0:
                                if n < 2:
                                    pe.wait_ge(v_kept, p * BATCH + (n + 1))
                                score(n)
                            if n + 1 < HEADS0:
                                if (n + 1) % R0 == 0:
                                    project(p, place_of(n + 1) - 1)
                                project(p, place_of(n + 1))
                            if n < 2:
                                project_values(2 + n)
                            if n == LAG:
                                pe.wait_ge(v_kept, p * BATCH + BATCH)
                            if LAG <= n < HEADS0 + LAG:
                                flip(n - LAG)
                            if n > LAG:
                                project_out(n - LAG - 1)
                            if LAG <= n < HEADS0 + LAG:
                                attend(n - LAG)
                            if more and n >= HEADS0 + LAG - 2 and n < HEADS0 + LAG:
                                project(p + 1, n - (HEADS0 + LAG - 2))

                    pe.wait_ge(consts_in, 16 * 5)
                    for b in range(BATCH):
                        if b >= 2:
                            pe.wait_ge(xT_lo_ready, QT * (b - 1))
                        norm_tensor(pe, 0, b, xn, 4 * (b % 2))
                        if b == 1:
                            project(0, 0, True)
                            project(0, 1, True)
                    each_pair(pe, turn_of)

        top[0] = LAYER0_END
        l0_ar, _ = place("l0_ar", [P, KC, E0 * RANK + E0])
        l0_b, _ = place("l0_b", [P, DIM])
        lower4, _ = place("lower4", [P, E0 * E0])
        top[0] = base
        l1_qkv, _ = place("l1_qkv", [P, KC, DIM + 2 * KV_HEADS[0] * HD])
        l1_wo, _ = place("l1_wo", [P, KC, DIM])
        l1_w, _ = place("l1_w", [P, KC, DIM])
        l1_ag, _ = place("l1_ag", [P, KC, E1 * RANK + 4 * E1])
        l1_b, _ = place("l1_b", [P, DIM])
        l1_gvec, _ = place("l1_gvec", [P, 3 * 4 * E1 + E1])
        l1_gw2, _ = place("l1_gw2", [4 * E1, E1])
        top[0] = base
        l2_w13, _ = place("l2_w13", [P, KC, 2 * HID2])
        l2_w2, _ = place("l2_w2", [P, HC2, DIM])
        l2_a13, _ = place("l2_a13", [P, KC, 96])
        l2_b13, _ = place("l2_b13", [96, HID2])
        l2_a2, _ = place("l2_a2", [P, HC2, RANK])
        l2_b2, _ = place("l2_b2", [96, DIM])
        after = top[0]
        top[0] = base
        l3_up, _ = place("l3_up", [P, KC, INT3])
        l3_down, _ = place("l3_down", [P, IC3, DIM])
        l3_fc1, _ = place("l3_fc1", [P, KC, LAT3 + E3])
        l3_expert, _ = place("l3_expert", [P, LC3, LAT3])
        l3_fc2, _ = place("l3_fc2", [P, LC3, DIM])
        l3_gb, behind3 = place("l3_gb", [P, 2 * DIM])
        top[0] = after
        l2_qkv, _ = place("l2_qkv", [P, KC, DIM + 2 * KV_HEADS[1] * HD])
        l2_wo, _ = place("l2_wo", [P, KC, DIM])
        rope, _ = place("rope", [P, QT, 2, HD])
        lower8, _ = place("lower8", [P, E1 * E1])
        work = top[0]
        l3_qkv, top[0] = place("l3_qkv", [P, KC, DIM + 2 * KV_HEADS[2] * HD], at=after)
        l3_bias, top[0] = place("l3_bias", [P, DIM + 2 * KV_HEADS[2] * HD], at=top[0])
        assert top[0] <= after + 20 * 1024

        tensors = dict(l0_ar=l0_ar, l0_b=l0_b, lower4=lower4, l1_qkv=l1_qkv, rope=rope, l1_wo=l1_wo,
                       l1_w=l1_w, l1_ag=l1_ag, l1_b=l1_b, l1_gvec=l1_gvec, l1_gw2=l1_gw2,
                       lower8=lower8, l2_qkv=l2_qkv, l2_wo=l2_wo, l3_qkv=l3_qkv, l3_bias=l3_bias,
                       l2_w13=l2_w13, l2_w2=l2_w2, l2_a13=l2_a13, l2_b13=l2_b13, l2_a2=l2_a2, l2_b2=l2_b2,
                       l3_up=l3_up, l3_down=l3_down, l3_fc1=l3_fc1, l3_expert=l3_expert, l3_fc2=l3_fc2, l3_gb=l3_gb)
        arrived, arriving = {}, {}

        def load(sp, group, *names):
            for name in names:
                sp.dma_start(words(tensors[name]), dram[name]).then_inc(arrived[group], 16)

        def group_of(group, *names):
            arrived[group], arriving[group] = sem(f"{group}_in"), names

        for group, names in (("f0", ("l0_ar", "l0_b", "lower4")),
                             ("a1", ("l1_qkv", "rope", "l1_wo")),
                             ("f1", ("l1_w", "l1_ag", "l1_b", "l1_gvec", "l1_gw2", "lower8")),
                             ("a2", ("l2_qkv", "l2_wo")),
                             ("f2", ("l2_w13", "l2_w2", "l2_a13", "l2_b13", "l2_a2", "l2_b2")),
                             ("f2_mask", ("lmask",)),
                             ("a3", ("l3_qkv",)),
                             ("a3_bias", ("l3_bias",)),
                             ("f3", ("l3_up", "l3_down", "l3_fc1", "l3_expert", "l3_fc2", "l3_gb"))):
            group_of(group, *names)

        def load_groups(sp, *groups):
            for group in groups:
                load(sp, group, *arriving[group])

        def await_group(eng, group):
            eng.wait_ge(arrived[group], 16 * len(arriving[group]))

        top[0] = work
        xn, _ = place("xn", [P, QT, DIM])
        xT, _ = place("xT", [P, KC, SEQ])
        attn, _ = place("attn", [P, QT, DIM], at=where["xn"])
        aT, _ = place("aT", [P, KC, SEQ])
        oT, _ = place("oT", [P, UNITS, SEQ])
        SHIFT = STACK
        qsT, _ = place("qsT", [P, HEADS, SEQ], BF16)
        ksT, _ = place("ksT", [P, 16, SEQ], BF16)
        val, _ = place("val", [P, QT, 16, VPAD])
        vf, _ = place("vf", [P, QT, 256])
        negmaxT, _ = place("negmaxT", [96, SEQ], BF16)
        negmax, _ = place("negmax", [P, QT, 3, HEADS], BF16)
        rowmax, _ = place("rowmax", [P, QT, HEADS])
        maxrest, _ = place("maxrest", [P, QT, HEADS])
        rowrcp, _ = place("rowrcp", [P, QT, HEADS])
        qs, _ = place("qs", [P, QT, HEADS, STACK], BF16)
        ks, _ = place("ks", [P, QT, 16, STACK], BF16)
        probT, _ = place("probT", [P, 4, 3 * SEQ])
        qf, _ = place("qf", [P, QT, DIM])
        kf, _ = place("kf", [P, QT, 256])
        rot, _ = place("rot", [P, DIM + 256])
        rest, _ = place("rest", [P, DIM + 256])

        PAIRS = HEADS // 2
        qkv_done = sem("qkv_done")
        v_staged = sem("v_staged")
        rope_muled = sem("rope_muled")
        qk_float = sem("qk_float")
        part_cut = sem("part_cut")
        rest_ready = sem("rest_ready")
        stack_flipped = sem("stack_flipped")
        stackT_vector = sem("stackT_vector")
        stackT_scalar = sem("stackT_scalar")
        val_ready = sem("val_ready")
        scored = sem("scored")
        maxed = sem("maxed")
        max_chain = sem("max_chain")
        negmax_ready = sem("negmax_ready")
        negmax_flipped = sem("negmax_flipped")
        negmaxT_ready = sem("negmaxT_ready")
        shift_in = sem("shift_in")
        key_scored = sem("key_scored")
        exped = sem("exped")
        attended = sem("attended")
        oT_ready = sem("oT_ready")
        o_flipped = sem("o_flipped")
        rcp_chain = sem("rcp_chain")
        attn_ready = sem("attn_ready")
        attn_flipped = sem("attn_flipped")
        aT_ready = sem("aT_ready")
        out_done = sem("out_done")
        val_set = sem("val_set")

        def attention(a, sub, wqkv, wo, weights, bias, early_loads, normed_before=False, norm_after=False):
            kv = KV_HEADS[a]
            rep = HEADS // kv
            kvd = kv * HD
            rotary = wo is not None
            t0 = a * BATCH
            SU = kv // 8 + 4
            su0 = t0 * 5
            SORDER = [(i, kind, c) for i in range(QT) for kind, c in
                      [("k", c) for c in range(kv // 8)] + [("q", c) for c in range(4)]]

            with nc.Block() as block:
                @block.sync
                def _(sp):
                    load_groups(sp, *early_loads)
                    with sp.Fori(0, BATCH) as b:
                        turn = b + t0
                        sp.wait_ge(negmaxT_ready, turn * QT + QT)
                        sp.dma_start(qsT[SHIFT:SHIFT + 3, :, :], negmaxT[:, :]).then_inc(shift_in, 16)

                @block.gpsimd
                def _(pool):
                    if not normed_before:
                        norm_gpsimd(pool, sub, 0)
                    nc.gpsimd.memset(val[:, :, :, HD:VPAD], 0.0).then_inc(val_set, 1)
                    pool.wait_ge(val_set, 3 * a + 1)
                    nc.gpsimd.memset(val[:, :, :, HD:HD + 1], 1.0).then_inc(val_set, 1)
                    pool.wait_ge(val_set, 3 * a + 2)
                    nc.gpsimd.memset(ksT[SHIFT:SHIFT + 3, :, :], 1.0).then_inc(val_set, 1)
                    pool.wait_ge(val_set, 3 * a + 3)

                    def front(b):
                        turn = b + t0
                        for i in range(QT):
                            if rotary:
                                pool.wait_ge(rope_muled, turn * QT + (i + 1))
                                nc.gpsimd.tensor_tensor(qf[:, i, :], qf[:, i, :], rot[:, 0:DIM], ALU.add)
                                nc.gpsimd.tensor_tensor(kf[:, i, 0:kvd], kf[:, i, 0:kvd], rot[:, DIM:DIM + kvd],
                                                        ALU.add).then_inc(qk_float, 1)
                            pool.wait_ge(part_cut, turn * 6 + (3 * i + 1))
                            restq = rest[:, 0:DIM].rearrange("p (h d) -> p h d", d=HD)
                            restk = rest[:, DIM:DIM + kvd].rearrange("p (h d) -> p h d", d=HD)
                            nc.gpsimd.tensor_tensor(restq, qf[:, i, :].rearrange("p (h d) -> p h d", d=HD),
                                                    qs[:, i, :, 0:HD], ALU.subtract)
                            nc.gpsimd.tensor_tensor(restk, kf[:, i, 0:kvd].rearrange("p (h d) -> p h d", d=HD),
                                                    ks[:, i, 0:kv, HD:2 * HD], ALU.subtract).then_inc(rest_ready, 1)
                            pool.wait_ge(part_cut, turn * 6 + (3 * i + 2))
                            nc.gpsimd.tensor_tensor(restq, restq, qs[:, i, :, 3 * HD:4 * HD], ALU.subtract)
                            nc.gpsimd.tensor_tensor(restk, restk, ks[:, i, 0:kv, 2 * HD:3 * HD],
                                                    ALU.subtract).then_inc(rest_ready, 1)

                    front(0)
                    with pool.Fori(1, BATCH) as b:
                        norm_gpsimd(pool, sub, b)
                        front(b)
                    if norm_after:
                        norm_gpsimd(pool, sub + 1, 0)

                @block.vector
                def _(dve):
                    def front_rope(b, i):
                        turn = b + t0
                        dve.wait_ge(qkv_done, turn * QT + (i + 1))
                        pq, pk = ps[:, 6, :], ps[:, 7, 0:kvd]
                        if rotary:
                            if i == 1:
                                dve.wait_ge(qk_float, turn * QT + 1)
                            cos = rope[:, i, 0:1, :]
                            for src, dst, tmp, n in ((pq, qf[:, i, :], rot[:, 0:DIM], HEADS),
                                                     (pk, kf[:, i, 0:kvd], rot[:, DIM:DIM + kvd], kv)):
                                s3 = src.rearrange("p (h d) -> p h d", d=HD)
                                t3 = tmp.rearrange("p (h d) -> p h d", d=HD)
                                nc.vector.tensor_tensor(dst.rearrange("p (h d) -> p h d", d=HD), s3,
                                                        cos.to_broadcast([P, n, HD]), ALU.mult)
                                nc.vector.tensor_tensor(t3[:, :, 0:8], s3[:, :, 8:16],
                                                        rope[:, i, 1:2, 0:8].to_broadcast([P, n, 8]), ALU.mult)
                                last = nc.vector.tensor_tensor(t3[:, :, 8:16], s3[:, :, 0:8],
                                                               rope[:, i, 1:2, 8:16].to_broadcast([P, n, 8]), ALU.mult)
                            last.then_inc(rope_muled, 1)
                        else:
                            nc.vector.tensor_tensor(qf[:, i, :], pq, l3_bias[:, 0:DIM], ALU.add)
                            nc.vector.tensor_tensor(vf[:, i, 0:kvd], ps[:, 7, kvd:2 * kvd], l3_bias[:, DIM + kvd:DIM + 2 * kvd],
                                                    ALU.add).then_inc(v_staged, 1)
                            nc.vector.tensor_tensor(kf[:, i, 0:kvd], pk, l3_bias[:, DIM:DIM + kvd], ALU.add).then_inc(qk_float, 1)

                    def front_stack(b, us):
                        for u in us:
                            i, kind, c = SORDER[u]
                            dst = (ksT if kind == "k" else qsT)[0:STACK, 8 * c:8 * c + 8, i * P:(i + 1) * P]
                            dve.wait_ge(stack_flipped, b * (2 * SU) + (2 * su0 + u + 1))
                            nc.vector.tensor_copy(dst, ps_bf[0:STACK, u % 4, :].rearrange("p (h t) -> p h t", t=P))\
                                .then_inc(stackT_vector, 1)

                    def row_maxima(b, i, before=False):
                        turn = b + t0
                        for hg in range(UNITS):
                            if before and hg == 5:
                                add_output(b - 1, 1)
                            v = i * UNITS + hg
                            dve.wait_ge(scored, turn * (2 * UNITS) + (v + 1))
                            s = ps[:, 2 * (v % 2):2 * (v % 2) + 2, :].rearrange("p a (h t) -> p a h t", h=2)
                            out_ = rowmax[:, i, 4 * hg:4 * hg + 4].rearrange("p (a h) -> p a h", h=2)
                            nc.vector.reduce_max(out_, s[:, :, :, 0:(i + 1) * P], AX.X).then_inc(maxed, 1)
                        dve.wait_ge(maxed, turn * (2 * UNITS) + (i + 1) * UNITS)
                        nc.vector.tensor_scalar(negmax[:, i, 0, :], rowmax[:, i, :], -1.0, None, ALU.mult).then_inc(max_chain, 1)
                        dve.wait_ge(max_chain, turn * (3 * QT) + (3 * i + 1))
                        nc.vector.scalar_tensor_tensor(maxrest[:, i, :], rowmax[:, i, :], -1.0, negmax[:, i, 0, :],
                                                       ALU.mult, ALU.subtract).then_inc(max_chain, 1)
                        dve.wait_ge(max_chain, turn * (3 * QT) + (3 * i + 2))
                        nc.vector.tensor_copy(negmax[:, i, 1, :], maxrest[:, i, :]).then_inc(max_chain, 1)
                        dve.wait_ge(max_chain, turn * (3 * QT) + (3 * i + 3))
                        nc.vector.tensor_tensor(negmax[:, i, 2, :], maxrest[:, i, :], negmax[:, i, 1, :],
                                                ALU.subtract).then_inc(negmax_ready, 1)

                    def keep_oT(b, e):
                        dve.wait_ge(attended, (b + t0) * UNITS + (e + 1))
                        nc.vector.tensor_copy(oT[:, e, :], ps[:, 4 + e % 2, 0:SEQ]).then_inc(oT_ready, 1)

                    def divide(b, c):
                        turn = b + t0
                        half, i = c // 2, c % 2
                        o = ps[:, (6, 7, 4, 5)[c], :].rearrange("p (h d) -> p h d", d=VPAD)
                        rcp = rowrcp[:, i, 16 * half:16 * half + 16]
                        dve.wait_ge(o_flipped, turn * 4 + (c + 1))
                        nc.vector.reciprocal(rcp, o[:, :, HD]).then_inc(rcp_chain, 1)
                        dve.wait_ge(rcp_chain, turn * 4 + (c + 1))
                        nc.vector.tensor_tensor(attn[:, i, 256 * half:256 * half + 256].rearrange("p (h d) -> p h d", d=HD),
                                                o[:, :, 0:HD], rcp.unsqueeze(2).to_broadcast([P, 16, HD]), ALU.mult)\
                            .then_inc(attn_ready, 1)

                    def add_output(b, i):
                        turn = b + t0
                        tile = x[:, bass.ds(b * QT + i, 1), :].rearrange("p a d -> p (a d)")
                        if rotary:
                            dve.wait_ge(out_done, turn * QT + (i + 1))
                            nc.vector.tensor_tensor(tile, ps[:, 4 + i, :], tile, ALU.add).then_inc(residual, 1)
                        else:
                            dve.wait_ge(attn_ready, turn * 4 + 4)
                            view = tile.rearrange("p (g k d) -> p k g d", g=rep, d=HD)
                            nc.vector.tensor_tensor(view, view, attn[:, i, :].rearrange("p (k g d) -> p k g d", g=rep, d=HD),
                                                    ALU.add).then_inc(residual, 1)

                    def back(b, more, norm_next, before):
                        row_maxima(b, 0)
                        if before:
                            add_output(b - 1, 0)
                        row_maxima(b, 1, before)
                        if more:
                            front_rope(b + 1, 0)
                        for e in range(UNITS):
                            keep_oT(b, e)
                            if e == 1 and more:
                                front_rope(b + 1, 1)
                            if e == 5:
                                divide(b, 0)
                                divide(b, 1)
                        if more:
                            front_stack(b + 1, range(0, 4, 2))
                        divide(b, 2)
                        divide(b, 3)
                        if more:
                            front_stack(b + 1, range(4, 2 * SU, 2))
                        if not rotary:
                            for i in range(QT):
                                add_output(b, i)
                        if norm_next:
                            norm_stats(dve, sub, b + 2)
                            if rotary:
                                dve.wait_ge(attn_flipped, (b + t0) * QT + QT)
                            norm_apply(dve, sub, b + 2, xn)

                    if not normed_before:
                        norm_vector(dve, sub, 0, xn)
                    await_group(dve, "a1" if rotary else bias)
                    front_rope(0, 0)
                    front_rope(0, 1)
                    front_stack(0, range(0, 2 * SU, 2))
                    norm_stats(dve, sub, 1)
                    norm_apply(dve, sub, 1, xn)
                    back(0, True, True, False)
                    with dve.Fori(1, BATCH - 2) as b:
                        back(b, True, True, rotary)
                    back(BATCH - 2, True, False, rotary)
                    back(BATCH - 1, False, False, rotary)
                    if norm_after:
                        norm_stats(dve, sub + 1, 0, updates(sub, 1))
                        dve.wait_ge(attn_flipped, (t0 + BATCH) * QT)
                        norm_apply(dve, sub + 1, 0, xn)
                    if rotary:
                        for i in range(QT):
                            add_output(BATCH - 1, i)

                @block.scalar
                def _(act):
                    def stage_values(b, i):
                        if rotary:
                            act.wait_ge(rope_muled, (b + t0) * QT + (i + 1))
                            nc.scalar.activation(vf[:, i, 0:kvd], ps[:, 7, kvd:2 * kvd], ACT.Copy).then_inc(v_staged, 1)

                    def cut(b, i, part, pieces=(0, 1)):
                        turn = b + t0
                        src_q, src_k = (qf[:, i, :], kf[:, i, 0:kvd]) if part == 0 else (rest[:, 0:DIM], rest[:, DIM:DIM + kvd])
                        q3 = src_q.rearrange("p (h r d) -> p h r d", r=1, d=HD)
                        k3 = src_k.rearrange("p (h r d) -> p h r d", r=1, d=HD)
                        q4 = qs[:, i, :, :].rearrange("p h (r d) -> p h r d", d=HD)
                        k4 = ks[:, i, 0:kv, :].rearrange("p h (r d) -> p h r d", d=HD)
                        rows_q = (slice(0, 3), slice(3, 5), slice(5, 6))[part]
                        rows_k = (slice(1, 6, 2), slice(2, 5, 2), slice(0, 1))[part]
                        n = 3 - part
                        if 0 in pieces:
                            if part == 0:
                                act.wait_ge(qk_float, turn * QT + (i + 1))
                            else:
                                act.wait_ge(rest_ready, turn * 4 + (2 * i + part))
                        half = HEADS // 2
                        for piece in pieces:
                            heads = slice(piece * half, (piece + 1) * half)
                            nc.scalar.activation(q4[:, heads, rows_q, :], q3[:, heads].to_broadcast([P, half, n, HD]), ACT.Copy)
                        if 1 in pieces:
                            nc.scalar.activation(k4[:, :, rows_k, :], k3.to_broadcast([P, kv, n, HD]), ACT.Copy).then_inc(part_cut, 1)

                    def front_stack(b, us):
                        for u in us:
                            i, kind, c = SORDER[u]
                            dst = (ksT if kind == "k" else qsT)[0:STACK, 8 * c:8 * c + 8, i * P:(i + 1) * P]
                            act.wait_ge(stack_flipped, b * (2 * SU) + (2 * su0 + u + 1))
                            nc.scalar.activation(dst, ps_bf[0:STACK, u % 4, :].rearrange("p (h t) -> p h t", t=P), ACT.Copy)\
                                .then_inc(stackT_scalar, 1)

                    def keep_values(b, last_turn):
                        if last_turn is not None:
                            act.wait_ge(attended, (last_turn + t0) * UNITS + UNITS)
                        act.wait_ge(v_staged, (b + t0) * QT + QT)
                        nc.scalar.activation(val[:, :, 0:kv, 0:HD], vf[:, :, 0:kvd].rearrange("p i (h d) -> p i h d", d=HD),
                                             ACT.Copy).then_inc(val_ready, 1)

                    def exps(b, e):
                        turn = b + t0
                        act.wait_ge(key_scored, turn * PAIRS + (e + 1))
                        if e >= 4:
                            act.wait_ge(attended, turn * UNITS + ((e - 4) // 2 + 1))
                        bank = 2 * (e % 2)
                        nc.scalar.activation(probT[:, e % 4, :], ps[:, bank:bank + 2, :].rearrange("p a t -> p (a t)")[:, 0:3 * SEQ],
                                             ACT.Exp, scale=SCALES[a]).then_inc(exped, 1)

                    CUT_AT = {2: (0, 0, (0,)), 3: (0, 0, (1,)), 5: (0, 1), 7: (0, 2),
                              8: (1, 0, (0,)), 9: (1, 0, (1,)), 11: (1, 1), 13: (1, 2)}
                    STAGE_AT = 6

                    def back(b, more):
                        turn = b + t0
                        if more:
                            norm_scalar(act, sub, b + 1, xT, 6)
                        for i in range(QT):
                            act.wait_ge(negmax_flipped, turn * QT + (i + 1))
                            nc.scalar.activation(negmaxT[:, i * P:(i + 1) * P], ps_bf[0:96, 4 + i, 0:P], ACT.Copy)\
                                .then_inc(negmaxT_ready, 1)
                        if more:
                            stage_values(b + 1, 0)
                        for e in range(PAIRS):
                            exps(b, e)
                            if more:
                                if e in CUT_AT:
                                    cut(b + 1, *CUT_AT[e])
                                if e == STAGE_AT:
                                    stage_values(b + 1, 1)
                        if more:
                            keep_values(b + 1, b)
                            front_stack(b + 1, range(1, 2 * SU, 2))
                        if rotary:
                            for i in range(QT):
                                act.wait_ge(attn_flipped, turn * QT + (i + 1))
                                nc.scalar.activation(aT[:, :, i * P:(i + 1) * P], ps[:, 6 + i, :].rearrange("p (k t) -> p k t", k=KC),
                                                     ACT.Copy).then_inc(aT_ready, 1)

                    norm_scalar(act, sub, 0, xT, 6)
                    for i in range(QT):
                        stage_values(0, i)
                        for part in range(3):
                            cut(0, i, part)
                    keep_values(0, None)
                    front_stack(0, range(1, 2 * SU, 2))
                    with act.Fori(0, BATCH - 1) as b:
                        back(b, True)
                    back(BATCH - 1, False)

                @block.tensor
                def _(pe):
                    def project_q(b, i):
                        if i == 0:
                            pe.wait_ge(xT_ready, (b + sub * BATCH) * QT + QT)
                        else:
                            pe.wait_ge(v_staged, (b + t0) * QT + 1)
                            pe.wait_ge(qk_float, (b + t0) * QT + 1)
                        for k in range(KC):
                            nc.tensor.matmul(ps[:, 6, :], xT[:, k, i * P:(i + 1) * P], wqkv[:, k, 0:DIM], start=(k == 0), stop=(k == KC - 1))

                    def project_kv(b, i):
                        for k in range(KC):
                            last = nc.tensor.matmul(ps[:, 7, 0:2 * kvd], xT[:, k, i * P:(i + 1) * P], wqkv[:, k, DIM:DIM + 2 * kvd],
                                                    start=(k == 0), stop=(k == KC - 1))
                        last.then_inc(qkv_done, 1)

                    def flip_stack(b, us):
                        for u in us:
                            i, kind, c = SORDER[u]
                            if u % SU == 0:
                                pe.wait_ge(part_cut, (b + t0) * 6 + 3 * (i + 1))
                            if u >= 4:
                                kept = stackT_scalar if u % 2 else stackT_vector
                                pe.wait_ge(kept, b * SU + (su0 + (u - 4) // 2 + 1))
                            src = ks if kind == "k" else qs
                            for h in range(8):
                                last = nc.tensor.transpose(ps_bf[0:STACK, u % 4, h * P:(h + 1) * P],
                                                           src[:, i, 8 * c + h, :], ident_bf[:, :])
                            last.then_inc(stack_flipped, 1)

                    def score(b, i, hg):
                        turn, keys, v = b + t0, (i + 1) * P, i * UNITS + hg
                        if v >= 2:
                            pe.wait_ge(maxed, turn * (2 * UNITS) + (v - 1))
                        for half in range(2):
                            bank = ps[:, 2 * (v % 2) + half, :].rearrange("p (h t) -> p h t", h=2)
                            nc.tensor.matmul(bank[:, :, i * P:keys], ident_bf[:, :], masks[:, 0:1, :].to_broadcast([P, 2, P]),
                                             start=True, stop=False, skip_group_check=True)
                            for j in range(2):
                                h = 4 * hg + 2 * half + j
                                last = nc.tensor.matmul(bank[:, j, 0:keys], qsT[0:STACK, h, i * P:(i + 1) * P],
                                                        ksT[0:STACK, h // rep, 0:keys], start=False, stop=(j == 1),
                                                        skip_group_check=True)
                        last.then_inc(scored, 1)

                    def flip_maxima(b, i):
                        pe.wait_ge(negmax_ready, (b + t0) * QT + (i + 1))
                        nc.tensor.transpose(ps_bf[0:96, 4 + i, 0:P], negmax[:, i, :, :].rearrange("p c h -> p (c h)"),
                                            ident_bf[:, :]).then_inc(negmax_flipped, 1)

                    def key_score(b, e):
                        turn = b + t0
                        if e >= 2:
                            pe.wait_ge(exped, turn * PAIRS + (e - 1))
                        bank = 2 * (e % 2)
                        for j, n in ((0, SEQ), (1, P)):
                            o = ps[:, bank + j, 0:2 * n].rearrange("p (h t) -> p h t", h=2)
                            nc.tensor.matmul(o[:, :, 0:P], ident_bf[:, :], masks[:, 1:2, :].to_broadcast([P, 2, P]),
                                             start=True, stop=False, skip_group_check=True)
                            for c in range(2):
                                h = 2 * e + c
                                last = nc.tensor.matmul(o[:, c, :], ksT[0:SHIFT + 3, h // rep, j * P:(j + 1) * P],
                                                        qsT[0:SHIFT + 3, h, SEQ - n:SEQ], start=False, stop=(c == 1),
                                                        skip_group_check=True)
                        last.then_inc(key_scored, 1)

                    def attend(b, e):
                        turn = b + t0
                        pe.wait_ge(exped, turn * PAIRS + (2 * e + 2))
                        if e >= 2:
                            pe.wait_ge(oT_ready, turn * UNITS + (e - 1))
                        for kt in range(QT):
                            for j in range(4):
                                slot, c = (2 * e + j // 2) % 4, j % 2
                                pr = probT[:, slot, c * SEQ:(c + 1) * SEQ] if kt == 0 else probT[:, slot, 2 * SEQ + c * P:2 * SEQ + (c + 1) * P]
                                last = nc.tensor.matmul(ps[32 * j:32 * j + 32, 4 + e % 2, kt * P:SEQ], val[:, kt, (4 * e + j) // rep, :],
                                                        pr, start=(kt == 0), stop=(kt == 1))
                        last.then_inc(attended, 1)

                    def flip_output(b, c):
                        half, i = c // 2, c % 2
                        pe.wait_ge(oT_ready, (b + t0) * UNITS + 4 * (half + 1))
                        for e in range(4 * half, 4 * half + 4):
                            last = nc.tensor.transpose(ps[:, (6, 7, 4, 5)[c], (e % 4) * P:(e % 4 + 1) * P], oT[:, e, i * P:(i + 1) * P],
                                                       ident[:, :])
                        last.then_inc(o_flipped, 1)

                    def output_piece(b, i, k):
                        if k == 0:
                            pe.wait_ge(aT_ready, (b + t0) * QT + (i + 1))
                        ins = nc.tensor.matmul(ps[:, 4 + i, :], aT[:, k, i * P:(i + 1) * P], wo[:, k, :],
                                               start=(k == 0), stop=(k == KC - 1))
                        if k == KC - 1:
                            ins.then_inc(out_done, 1)

                    def back(b, more, before):
                        turn = b + t0
                        for hg in range(UNITS):
                            score(b, 0, hg)
                            if hg == 1 and more:
                                if before:
                                    pe.wait_ge(aT_ready, turn * QT)
                                norm_tensor(pe, sub, b + 1, xn, 6)
                            if hg % 2 and before:
                                output_piece(b - 1, 0, hg // 2)
                        for hg in range(UNITS):
                            score(b, 1, hg)
                            if hg < KC and before:
                                output_piece(b - 1, 1, hg)
                            if hg == 5:
                                if before:
                                    pe.wait_ge(residual, updates(sub, b - 1) + 1)
                                flip_maxima(b, 0)
                        if more:
                            project_q(b + 1, 0)
                        if before:
                            pe.wait_ge(residual, updates(sub, b - 1) + 2)
                        flip_maxima(b, 1)
                        if more:
                            project_kv(b + 1, 0)
                        pe.wait_ge(shift_in, turn * 16 + 16)
                        pe.wait_ge(maxed, turn * (2 * UNITS) + 2 * UNITS)
                        pe.wait_ge(val_ready, turn + 1)
                        for e in range(PAIRS):
                            key_score(b, e)
                            if e >= 3 and e % 2 == 1:
                                attend(b, (e - 3) // 2)
                            if more and e == 5:
                                project_q(b + 1, 1)
                                project_kv(b + 1, 1)
                            if e == 12:
                                if more:
                                    pe.wait_ge(v_staged, (b + 1 + t0) * QT + QT)
                                    pe.wait_ge(qk_float, (b + 1 + t0) * QT + QT)
                                flip_output(b, 0)
                                flip_output(b, 1)
                        attend(b, UNITS - 1)
                        if more:
                            pe.wait_ge(exped, turn * PAIRS + PAIRS)
                            flip_stack(b + 1, range(0, 4))
                        flip_output(b, 2)
                        flip_output(b, 3)
                        if more:
                            flip_stack(b + 1, range(4, 2 * SU))
                        if rotary:
                            for i in range(QT):
                                pe.wait_ge(attn_ready, turn * 4 + (3 + i))
                                for k in range(KC):
                                    last = nc.tensor.transpose(ps[:, 6 + i, k * P:(k + 1) * P], attn[:, i, k * P:(k + 1) * P], ident[:, :])
                                last.then_inc(attn_flipped, 1)
                        if more:
                            pe.wait_ge(stackT_vector, (b + 1) * SU + (su0 + SU))
                            pe.wait_ge(stackT_scalar, (b + 1) * SU + (su0 + SU))

                    await_group(pe, weights)
                    norm_tensor(pe, sub, 0, xn, 6)
                    for i in range(QT):
                        project_q(0, i)
                        project_kv(0, i)
                    flip_stack(0, range(2 * SU))
                    pe.wait_ge(stackT_vector, su0 + SU)
                    pe.wait_ge(stackT_scalar, su0 + SU)
                    pe.wait_ge(val_set, 3 * a + 3)
                    back(0, True, False)
                    with pe.Fori(1, BATCH - 1) as b:
                        back(b, True, rotary)
                    back(BATCH - 1, False, rotary)
                    if rotary:
                        for i in range(QT):
                            for k in range(KC):
                                output_piece(BATCH - 1, i, k)

        top[0] = work + QT * DIM * 4 + KC * SEQ * 4
        logits, _ = place("logits", [P, QT, E1])
        beats, _ = place("beats", [P, QT, E1 * E1])
        ties, _ = place("ties", [P, QT, E1 * E1])
        ranks, _ = place("ranks", [P, QT, E1])
        here = top[0]
        logits0, beats0, ties0, ranks0, gates0 = (place(f"{name}0", [P, TILES, n])[0] for name, n in (
            ("logits", E0), ("beats", E0 * E0), ("ties", E0 * E0), ("ranks", E0), ("gates", E0)))
        top_logit, _ = place("top_logit", [P, TILES])
        gate_sum, _ = place("gate_sum", [P, TILES])
        mid, _ = place("mid", [P, TILES, P])
        midT, _ = place("midT", [P, TILES, P])
        top[0] = here
        tmp1, _ = place("tmp1", [P, TILES, E1 * RANK])
        midT1, _ = place("midT1", [P, TILES, P])
        chosen, _ = place("chosen", [P, TILES, 2, E1])
        topg, _ = place("topg", [P, TILES, 2])
        weighed, _ = place("weighed", [P, TILES, 2, E1])
        wexp, _ = place("wexp", [P, TILES, E1])
        counts, _ = place("counts", [P, 2 * E1])
        ones, _ = place("ones", [P, P])
        hid, _ = place("hid", [P, QT, 4 * E1])
        hidT, _ = place("hidT", [4 * E1, SEQ])
        hstats, _ = place("hstats", [P, QT, 6])
        hmv, _ = place("hmv", [P, QT, 2])
        hrstd, _ = place("hrstd", [P, QT, 1])
        gap, _ = place("gap", [P, QT, 2])
        parts = after + (DIM + 2 * KV_HEADS[2] * HD) * KC * 4
        top[0] = parts
        w13_hi, _ = place("w13_hi", [P, KC, 2 * HID2], F32R)
        w2_hi, _ = place("w2_hi", [P, HC2, DIM], F32R)
        a13_hi, _ = place("a13_hi", [P, KC, 96], F32R)
        a2_hi, _ = place("a2_hi", [P, HC2, RANK], F32R)
        b13_parts, _ = place("b13_parts", [96, HID2], F32R)
        w13_lo, w2_lo, a13_lo, a2_lo = (place(f"{n}_lo", shape, F32R, at=at)[0] for n, shape, at in (
            ("w13", [P, KC, 2 * HID2], where["l2_w13"]), ("w2", [P, HC2, DIM], where["l2_w2"]),
            ("a13", [P, KC, 96], where["l2_a13"]), ("a2", [P, HC2, RANK], where["l2_a2"])))
        xn2, _ = place("xn2", [P, QT, DIM])
        xT2_hi, _ = place("xT2_hi", [P, KC, SEQ], F32R)
        xT2_lo, _ = place("xT2_lo", [P, KC, SEQ], F32R)
        lowT, _ = place("lowT", [96, 2, SEQ], F32R)
        low2T, _ = place("low2T", [96, SEQ])
        lmask, _ = place("lmask", [96, 2])
        tanh_, _ = place("tanh_", [P, 2, SEQ])
        gate_, _ = place("gate_", [P, 2, SEQ])
        g_hi, _ = place("g_hi", [P, 4, SEQ], F32R)
        g_lo, _ = place("g_lo", [P, 4, SEQ], F32R)
        top[0] = behind3
        up_hi, _ = place("up_hi", [P, KC, INT3], F32R)
        down_hi, _ = place("down_hi", [P, IC3, DIM], F32R)
        fc1_hi, _ = place("fc1_hi", [P, KC, LAT3 + E3], F32R)
        expert_hi, _ = place("expert_hi", [P, LC3, LAT3], F32R)
        fc2_hi, _ = place("fc2_hi", [P, LC3, DIM], F32R)
        up_lo, down_lo, fc1_lo, expert_lo, fc2_lo = (place(f"{n}_lo", shape, F32R, at=at)[0] for n, shape, at in (
            ("up", [P, KC, INT3], where["l3_up"]), ("down", [P, IC3, DIM], where["l3_down"]),
            ("fc1", [P, KC, LAT3 + E3], where["l3_fc1"]), ("expert", [P, LC3, LAT3], where["l3_expert"]),
            ("fc2", [P, LC3, DIM], where["l3_fc2"])))
        xn3, _ = place("xn3", [P, QT, DIM])
        xT3_hi, _ = place("xT3_hi", [P, KC, SEQ], F32R)
        xT3_lo, _ = place("xT3_lo", [P, KC, SEQ], F32R)
        lat_hi, _ = place("lat_hi", [P, LC3, SEQ], F32R)
        lat_lo, _ = place("lat_lo", [P, LC3, SEQ], F32R)
        exp_hi, _ = place("exp_hi", [P, LC3, SEQ], F32R)
        exp_lo, _ = place("exp_lo", [P, LC3, SEQ], F32R)
        logitsT, _ = place("logitsT", [E3, SEQ])
        logits3, _ = place("logits3", [P, QT, E3])
        top8, _ = place("top8", [P, QT, E3])
        routing, _ = place("routing", [P, QT])
        relu_, _ = place("relu_", [P, 2, SEQ])
        square, _ = place("square", [P, 2, SEQ])
        h_hi, _ = place("h_hi", [P, 4, SEQ], F32R)
        h_lo, _ = place("h_lo", [P, 4, SEQ], F32R)
        shared, _ = place("shared", [P, QT, DIM])
        ystats, _ = place("ystats", [P, QT, 6])
        ymv, _ = place("ymv", [P, QT, 2])
        yrstd, _ = place("yrstd", [P, QT, 1])
        tensors["lmask"] = lmask
        lo_ready = sem("xT_lo_ready")

        def each_turn(eng, turn_of):
            turn_of(0, True, True)
            with eng.Fori(1, BATCH - 1) as b:
                turn_of(b, False, True)
            turn_of(BATCH - 1, False, False)

        def tile_of(b, i):
            return x[:, bass.ds(b * QT + i, 1), :].rearrange("p a d -> p (a d)")

        def rank_experts(chain, E, lower, logits=logits, beats=beats, ties=ties, ranks=ranks):
            tiles = logits.shape[1]
            lg = logits[:, :, 0:E]
            f = lg.unsqueeze(2).to_broadcast([P, tiles, E, E])
            e = lg.unsqueeze(3).to_broadcast([P, tiles, E, E])
            bt = beats[:, :, 0:E * E].rearrange("p i (e f) -> p i e f", f=E)
            ti = ties[:, :, 0:E * E].rearrange("p i (e f) -> p i e f", f=E)
            for i in range(tiles):
                nc.vector.tensor_tensor(bt[:, i], f[:, i], e[:, i], ALU.is_gt)
                last = nc.vector.tensor_tensor(ti[:, i], f[:, i], e[:, i], ALU.is_equal)
            chain.link(last)
            low = lower[:, :].unsqueeze(1).to_broadcast([P, tiles, E * E])
            chain.link(nc.vector.tensor_tensor(ties[:, :, 0:E * E], ties[:, :, 0:E * E], low, ALU.mult))
            chain.link(nc.vector.tensor_tensor(beats[:, :, 0:E * E], beats[:, :, 0:E * E], ties[:, :, 0:E * E], ALU.add))
            chain.link(nc.vector.reduce_sum(ranks[:, :, 0:E], bt, AX.X))

        def each_but_last(eng, turn_of):
            with eng.Fori(0, BATCH - 1) as b:
                turn_of(b, True)
            turn_of(BATCH - 1, False)

        def layer0_feed_forward(sub):
            mid_done = sem("f0_mid_done")
            mid_kept = sem("f0_mid_kept")
            chain_sem = sem("f0_chain")
            shifted = sem("f0_shifted")
            exped0 = sem("f0_exped")
            gated = sem("f0_gated")
            mid_flipped = sem("f0_mid_flipped")
            midT_ready = sem("f0_midT_ready")
            done = sem("f0_done")
            EA = E0 * RANK

            with nc.Block() as block:
                @block.sync
                def _(sp):
                    load_groups(sp, "a1")

                @block.gpsimd
                def _(pool):
                    nc.gpsimd.memset(mid[:, :, :], 0.0).then_inc(val_set0, 1)
                    norm_gpsimd(pool, sub, 0)
                    with pool.Fori(1, BATCH) as b:
                        norm_gpsimd(pool, sub, b)
                    norm_gpsimd(pool, sub + 1, 0)

                @block.vector
                def _(dve):
                    def turn_of(b, more):
                        if more:
                            norm_stats(dve, sub, b + 1)
                            dve.wait_ge(flipped, (b + sub * BATCH) * QT + QT)
                            norm_apply(dve, sub, b + 1, xn)
                        dve.wait_ge(mid_done, b + 1)
                        nc.vector.tensor_copy(logits0[:, bass.ds(b * QT, QT), :], ps[:, 2:4, EA:EA + E0])
                        nc.vector.tensor_copy(mid[:, bass.ds(b * QT, QT), 0:EA], ps[:, 2:4, 0:EA]).then_inc(mid_kept, 1)

                    await_group(dve, "f0")
                    dve.wait_ge(val_set0, 1)
                    norm_vector(dve, sub, 0, xn)
                    each_but_last(dve, turn_of)
                    dve.wait_ge(mid_kept, BATCH)
                    chain = Chain(dve, chain_sem, 9)
                    chain.start(0)
                    rank_experts(chain, E0, lower4, logits0, beats0, ties0, ranks0)
                    chain.link(nc.vector.tensor_scalar(ranks0[:, :, :], ranks0[:, :, :], 1.5, None, ALU.is_lt))
                    chain.link(nc.vector.reduce_max(top_logit[:, :], logits0[:, :, :], AX.X))
                    nc.vector.tensor_tensor(gates0[:, :, :], logits0[:, :, :], top_logit[:, :].unsqueeze(2).to_broadcast([P, TILES, E0]),
                                            ALU.subtract).then_inc(shifted, 1)
                    dve.wait_ge(exped0, 1)
                    chain.link(nc.vector.tensor_tensor(gates0[:, :, :], gates0[:, :, :], ranks0[:, :, :], ALU.mult))
                    chain.link(nc.vector.reduce_sum(gate_sum[:, :], gates0[:, :, :], AX.X))
                    chain.link(nc.vector.reciprocal(gate_sum[:, :], gate_sum[:, :]))
                    chain.end()
                    nc.vector.scalar_tensor_tensor(gates0[:, :, :], gates0[:, :, :], 4.0, gate_sum[:, :].unsqueeze(2).to_broadcast([P, TILES, E0]),
                                                   ALU.mult, ALU.mult).then_inc(shifted, 1)
                    dve.wait_ge(shifted, 2)
                    for half in range(2):
                        m3 = mid[:, 4 * half:4 * half + 4, 0:EA].rearrange("p t (e r) -> p t e r", r=RANK)
                        for t in range(4):
                            last = nc.vector.tensor_tensor(m3[:, t], m3[:, t], gates0[:, 4 * half + t, :].unsqueeze(2).to_broadcast([P, E0, RANK]),
                                                           ALU.mult)
                        last.then_inc(gated, 1)
                    for T in range(TILES):
                        dve.wait_ge(done, T + 1)
                        nc.vector.tensor_tensor(x[:, T, :], ps[:, 4 + T % 4, :], x[:, T, :], ALU.add).then_inc(residual, 1)
                        if T == 3:
                            norm_stats(dve, sub + 1, 0, updates(sub, 1))
                        if T == 5:
                            norm_apply(dve, sub + 1, 0, xn)

                @block.scalar
                def _(act):
                    norm_scalar(act, sub, 0, xT)
                    with act.Fori(1, BATCH) as b:
                        norm_scalar(act, sub, b, xT)
                    act.wait_ge(shifted, 1)
                    nc.scalar.activation(gates0[:, :, :], gates0[:, :, :], ACT.Exp).then_inc(exped0, 1)
                    for half in range(2):
                        act.wait_ge(mid_flipped, half + 1)
                        nc.scalar.activation(midT[:, 4 * half:4 * half + 4, :], ps[:, half, :].rearrange("p (t c) -> p t c", t=4),
                                             ACT.Copy).then_inc(midT_ready, 1)

                @block.tensor
                def _(pe):
                    def turn_of(b, more, first=False):
                        pe.wait_ge(xT_ready, (b + sub * BATCH) * QT + QT)
                        if not first:
                            pe.wait_ge(mid_kept, b)
                        for i in range(QT):
                            for k in range(KC):
                                last = nc.tensor.matmul(ps[:, 2 + i, 0:EA + E0], xT[:, k, i * P:(i + 1) * P], l0_ar[:, k, :],
                                                        start=(k == 0), stop=(k == KC - 1))
                        last.then_inc(mid_done, 1)
                        if more:
                            norm_tensor(pe, sub, b + 1, xn)

                    await_group(pe, "f0")
                    norm_tensor(pe, sub, 0, xn)
                    turn_of(0, True, True)
                    with pe.Fori(1, BATCH - 1) as b:
                        turn_of(b, True)
                    turn_of(BATCH - 1, False)
                    for half in range(2):
                        pe.wait_ge(gated, half + 1)
                        for T in range(4 * half, 4 * half + 4):
                            last = nc.tensor.transpose(ps[:, half, (T % 4) * P:(T % 4 + 1) * P], mid[:, T, :], ident[:, :])
                        last.then_inc(mid_flipped, 1)
                    for T in range(TILES):
                        pe.wait_ge(midT_ready, T // 4 + 1)
                        if T >= 4:
                            pe.wait_ge(residual, updates(sub) + T - 3)
                        nc.tensor.matmul(ps[:, 4 + T % 4, :], midT[:, T, :], l0_b[:, :], start=True, stop=True).then_inc(done, 1)

        def layer1_feed_forward(sub):
            low_done = sem("f1_low_done")
            low_kept = sem("f1_low_kept")
            main_done = sem("f1_main_done")
            main_added = sem("f1_main_added")
            logits_kept = sem("f1_logits_kept")
            chain_sem = sem("f1_chain")
            hvar = sem("f1_hvar")
            pool_chain = sem("f1_pool_chain")
            hrstd_ready = sem("f1_hrstd_ready")
            hid_ready = sem("f1_hid_ready")
            hid_flipped = sem("f1_hid_flipped")
            hidT_ready = sem("f1_hidT_ready")
            logits_done = sem("f1_logits_done")
            gap_ready = sem("f1_gap_ready")
            gap_exped = sem("f1_gap_exped")
            turn_over = sem("f1_turn_over")
            ones_set = sem("f1_ones_set")
            counted = sem("f1_counted")
            tail_chain = sem("f1_tail_chain")
            weighted = sem("f1_weighted")
            mid_flipped = sem("f1_mid_flipped")
            midT_ready = sem("f1_midT_ready")
            done = sem("f1_done")
            EA, HG = E1 * RANK, 4 * E1

            with nc.Block() as block:
                @block.gpsimd
                def _(pool):
                    nc.gpsimd.memset(ones[:, :], 1.0).then_inc(ones_set, 1)
                    def turn_of(b, more):
                        pool.wait_ge(hvar, b + 1)
                        nc.gpsimd.tensor_tensor(hrstd[:, :, 0], hmv[:, :, 1], eps[:, :].to_broadcast([P, QT]), ALU.add).then_inc(pool_chain, 1)
                        pool.wait_ge(pool_chain, b + 1)
                        nc.gpsimd.tensor_tensor(hrstd[:, :, 0], hrstd[:, :, 0], minus_half[:, :].to_broadcast([P, QT]),
                                                ALU.pow).then_inc(hrstd_ready, 1)
                        if more:
                            norm_gpsimd(pool, sub, b + 1)

                    each_but_last(pool, turn_of)
                    norm_gpsimd(pool, sub + 1, 0)

                @block.vector
                def _(dve):
                    await_group(dve, "f1")
                    chain = Chain(dve, chain_sem, 14)
                    gb1, gamma, beta, gb2 = (l1_gvec[:, HG * j:HG * j + (HG if j < 3 else E1)] for j in range(4))
                    def turn_of(b, more):
                        chain.start(b)
                        dve.wait_ge(low_done, b + 1)
                        for i in range(QT):
                            nc.vector.tensor_tensor(hid[:, i, :], ps[:, 4 + i, EA:EA + HG], gb1, ALU.add)
                        dve.drain()
                        for i in range(QT):
                            nc.vector.bn_stats(hstats[:, i, :], hid[:, i, :])
                        dve.drain()
                        for i in range(QT):
                            last = nc.vector.bn_aggr(hmv[:, i, :], hstats[:, i, :])
                        last.then_inc(hvar, 1)
                        for i in range(QT):
                            last = nc.vector.tensor_copy(tmp1[:, bass.ds(b * QT + i, 1), :].rearrange("p a d -> p (a d)"), ps[:, 4 + i, 0:EA])
                        last.then_inc(low_kept, 1)
                        if more:
                            norm_stats(dve, sub, b + 1)
                        dve.wait_ge(hrstd_ready, b + 1)
                        for i in range(QT):
                            last = nc.vector.tensor_scalar(hid[:, i, :], hid[:, i, :], hmv[:, i, 0:1], hrstd[:, i, :],
                                                           ALU.subtract, ALU.mult)
                        chain.link(last)
                        chain.link(nc.vector.tensor_tensor(hid[:, :, :], hid[:, :, :], gamma.unsqueeze(1).to_broadcast([P, QT, HG]), ALU.mult))
                        chain.link(nc.vector.tensor_tensor(hid[:, :, :], hid[:, :, :], beta.unsqueeze(1).to_broadcast([P, QT, HG]), ALU.add))
                        nc.vector.tensor_scalar(hid[:, :, :], hid[:, :, :], 0.0, None, ALU.max).then_inc(hid_ready, 1)
                        if more:
                            norm_apply(dve, sub, b + 1, xn)
                        dve.wait_ge(main_done, b + 1)
                        for i in range(QT):
                            nc.vector.tensor_tensor(tile_of(b, i), ps[:, 2 + i, :], tile_of(b, i), ALU.add).then_inc(main_added, 1)
                        dve.wait_ge(logits_done, b + 1)
                        nc.vector.tensor_tensor(logits[:, :, :], ps[:, 7, 0:QT * E1].rearrange("p (i e) -> p i e", e=E1),
                                                gb2.unsqueeze(1).to_broadcast([P, QT, E1]), ALU.add).then_inc(logits_kept, 1)
                        dve.wait_ge(logits_kept, b + 1)
                        rank_experts(chain, E1, lower8)
                        pick = [chosen[:, bass.ds(b * QT, QT), c, :] for c in range(2)]
                        for c in range(2):
                            last = nc.vector.tensor_scalar(pick[c], ranks[:, :, :], float(c), None, ALU.is_equal)
                        chain.link(last)
                        for c in range(2):
                            last = nc.vector.tensor_tensor(beats[:, :, c * E1:(c + 1) * E1], pick[c], logits[:, :, :], ALU.mult)
                        chain.link(last)
                        chain.link(nc.vector.reduce_sum(gap[:, :, :], beats[:, :, 0:2 * E1].rearrange("p i (c e) -> p i c e", c=2), AX.X))
                        nc.vector.tensor_tensor(gap[:, :, 1], gap[:, :, 1], gap[:, :, 0], ALU.subtract).then_inc(gap_ready, 1)
                        dve.wait_ge(gap_exped, b + 1)
                        chain.link(nc.vector.tensor_scalar(gap[:, :, 0], gap[:, :, 1], 1.0, None, ALU.add))
                        chain.link(nc.vector.reciprocal(gap[:, :, 0], gap[:, :, 0]))
                        chain.link(nc.vector.tensor_copy(topg[:, bass.ds(b * QT, QT), 0], gap[:, :, 0]))
                        chain.link(nc.vector.tensor_tensor(topg[:, bass.ds(b * QT, QT), 1], gap[:, :, 0], gap[:, :, 1], ALU.mult))
                        chain.end()

                    each_but_last(dve, turn_of)
                    dve.wait_ge(main_added, TILES)
                    tail = Chain(dve, tail_chain, 6)
                    tail.start(0)
                    dve.wait_ge(counted, 1)
                    tail.link(nc.vector.reduce_sum(counts[:, :], ps[:, 0, 0:TILES * 2 * E1].rearrange("p (t c) -> p c t", t=TILES), AX.X))
                    tail.link(nc.vector.tensor_scalar(counts[:, :], counts[:, :], float(CAPACITY) + 0.5, 1.0 / RANK, ALU.is_lt, ALU.mult))
                    tail.link(nc.vector.tensor_tensor(weighed[:, :, :, :].rearrange("p t c e -> p t (c e)"),
                                                      chosen[:, :, :, :].rearrange("p t c e -> p t (c e)"),
                                                      counts[:, :].unsqueeze(1).to_broadcast([P, TILES, 2 * E1]), ALU.mult))
                    tail.link(nc.vector.tensor_tensor(weighed[:, :, :, :].rearrange("p t c e -> p (t c) e"),
                                                      weighed[:, :, :, :].rearrange("p t c e -> p (t c) e"),
                                                      topg[:, :, :].rearrange("p t c -> p (t c)").unsqueeze(2).to_broadcast([P, TILES * 2, E1]),
                                                      ALU.mult))
                    tail.link(nc.vector.tensor_tensor(wexp[:, :, :], weighed[:, :, 0, :], weighed[:, :, 1, :], ALU.add))
                    t3 = tmp1[:, :, :].rearrange("p t (e r) -> p (t e) r", r=RANK)
                    nc.vector.tensor_tensor(t3, t3, wexp[:, :, :].rearrange("p t e -> p (t e)").unsqueeze(2)
                                            .to_broadcast([P, TILES * E1, RANK]), ALU.mult).then_inc(weighted, 1)
                    tail.k += 1
                    tail.end()
                    for T in range(TILES):
                        dve.wait_ge(done, T + 1)
                        nc.vector.tensor_tensor(x[:, T, :], ps[:, 4 + T % 4, :], x[:, T, :], ALU.add).then_inc(residual, 1)
                        if T == 3:
                            norm_stats(dve, sub + 1, 0, updates(sub, 1))
                        if T == 5:
                            norm_apply(dve, sub + 1, 0, xn)

                @block.scalar
                def _(act):
                    def turn_of(b, more):
                        act.wait_ge(hid_flipped, b + 1)
                        nc.scalar.activation(hidT[:, :], ps[0:HG, 6, 0:SEQ], ACT.Copy).then_inc(hidT_ready, 1)
                        if more:
                            norm_scalar(act, sub, b + 1, xT)
                        act.wait_ge(gap_ready, b + 1)
                        nc.scalar.activation(gap[:, :, 1], gap[:, :, 1], ACT.Exp).then_inc(gap_exped, 1)

                    norm_scalar(act, sub, 0, xT)
                    each_but_last(act, turn_of)
                    for half in range(2):
                        act.wait_ge(mid_flipped, half + 1)
                        nc.scalar.activation(midT1[:, 4 * half:4 * half + 4, :], ps[:, 1 + half, :].rearrange("p (t c) -> p t c", t=4),
                                             ACT.Copy).then_inc(midT_ready, 1)

                @block.tensor
                def _(pe):
                    await_group(pe, "f1")
                    def times_x(b, w, bank):
                        for i in range(QT):
                            n = w.shape[2]
                            for k in range(KC):
                                last = nc.tensor.matmul(ps[:, bank + i, 0:n], xT[:, k, i * P:(i + 1) * P], w[:, k, :],
                                                        start=(k == 0), stop=(k == KC - 1))
                        return last

                    def turn_of(b, more, first=False):
                        pe.wait_ge(xT_ready, (b + sub * BATCH) * QT + QT)
                        if not first:
                            pe.wait_ge(low_kept, b)
                        times_x(b, l1_ag, 4).then_inc(low_done, 1)
                        if not first:
                            pe.wait_ge(main_added, b * QT)
                        times_x(b, l1_w, 2).then_inc(main_done, 1)
                        pe.wait_ge(hid_ready, b + 1)
                        for i in range(QT):
                            last = nc.tensor.transpose(ps[0:HG, 6, i * P:(i + 1) * P], hid[:, i, :], ident[:, :])
                        last.then_inc(hid_flipped, 1)
                        if more:
                            norm_tensor(pe, sub, b + 1, xn)
                        pe.wait_ge(hidT_ready, b + 1)
                        if not first:
                            pe.wait_ge(logits_kept, b)
                        for i in range(QT):
                            last = nc.tensor.matmul(ps[:, 7, i * E1:(i + 1) * E1], hidT[:, i * P:(i + 1) * P], l1_gw2[:, :], start=True, stop=True)
                        last.then_inc(logits_done, 1)

                    norm_tensor(pe, sub, 0, xn)
                    turn_of(0, True, True)
                    with pe.Fori(1, BATCH - 1) as b:
                        turn_of(b, True)
                    turn_of(BATCH - 1, False)
                    pe.wait_ge(ones_set, 1)
                    pe.wait_ge(chain_sem, BATCH * 14)
                    nc.tensor.matmul(ps[:, 0, 0:TILES * 2 * E1], ones[:, :], chosen[:, :, :, :].rearrange("p t c e -> p (t c e)"),
                                     start=True, stop=True).then_inc(counted, 1)
                    pe.wait_ge(weighted, 1)
                    for half in range(2):
                        for T in range(4 * half, 4 * half + 4):
                            last = nc.tensor.transpose(ps[:, 1 + half, (T % 4) * P:(T % 4 + 1) * P], tmp1[:, T, :], ident[:, :])
                        last.then_inc(mid_flipped, 1)
                    for T in range(TILES):
                        pe.wait_ge(midT_ready, T // 4 + 1)
                        if T >= 4:
                            pe.wait_ge(residual, updates(sub) + T - 3)
                        nc.tensor.matmul(ps[:, 4 + T % 4, :], midT1[:, T, :], l1_b[:, :], start=True, stop=True).then_inc(done, 1)

        def layer2_feed_forward(sub):
            low_done = sem("f2_low_done")
            low_hi_ready = sem("f2_low_hi_ready")
            lowT_ready = sem("f2_lowT_ready")
            zeroed = sem("f2_zeroed")
            hi_cut = sem("f2_hi_cut")
            lo_cut = sem("f2_lo_cut")
            up_done = sem("f2_up_done")
            tanhed = sem("f2_tanhed")
            half_done = sem("f2_half_done")
            g_ready = sem("f2_g_ready")
            g_hi_ready = sem("f2_g_hi_ready")
            g_lo_ready = sem("f2_g_lo_ready")
            down_done = sem("f2_down_done")
            low2_ready = sem("f2_low2_ready")
            done = sem("f2_done")
            AHEAD = 3
            XBANK = 5

            def rows(c):
                return P if c < HC2 - 1 else HLAST2

            def chunk_of(w, c):
                return w[:, :, :].rearrange("p k (j h) -> p k j h", j=2)[:, :, :, c * P:c * P + rows(c)]

            with nc.Block() as block:
                @block.sync
                def _(sp):
                    load_groups(sp, "f2_mask", "a3")

                @block.gpsimd
                def _(pool):
                    nc.gpsimd.memset(low2T[:, :], 0.0).then_inc(zeroed, 1)
                    norm_gpsimd(pool, sub, 0)

                    def turn_of(b, first, more):
                        for c in range(HC2):
                            r = rows(c)
                            pool.wait_ge(g_hi_ready, b * HC2 + (c + 1))
                            subtract_high(nc.gpsimd, g_lo[0:r, c % 4, :], gate_[0:r, c % 2, :], g_hi[0:r, c % 4, :]).then_inc(g_lo_ready, 1)
                            if more and c == 4:
                                norm_gpsimd(pool, sub, b + 1)

                    each_turn(pool, turn_of)

                @block.vector
                def _(dve):
                    def cut_chunk(c):
                        r = rows(c)
                        dve.wait_ge(hi_cut, c + 2)
                        for k in range(KC):
                            subtract_high(nc.vector, chunk_of(w13_lo, c)[:, k], chunk_of(l2_w13, c)[:, k], chunk_of(w13_hi, c)[:, k])
                        subtract_high(nc.vector, a2_lo[0:r, c, :], l2_a2[0:r, c, :], a2_hi[0:r, c, :])
                        subtract_high(nc.vector, w2_lo[0:r, c, :], l2_w2[0:r, c, :], w2_hi[0:r, c, :]).then_inc(lo_cut, 1)

                    def turn_of(b, first, more):
                        dve.wait_ge(low_hi_ready, b + 1)
                        for j in range(2):
                            last = nc.vector.scalar_tensor_tensor(lowT[32:64, j, :], ps[32:64, 6, 0:SEQ], lmask[32:64, j:j + 1],
                                                                  lowT[32:64, j, :].bitcast(F32), ALU.mult, ALU.subtract)
                        last.then_inc(lowT_ready, 1)
                        for c in range(HC2):
                            r, s, bank = rows(c), c % 2, 2 + c % 4
                            if first and c + AHEAD < HC2:
                                cut_chunk(c + AHEAD)
                            dve.wait_ge(tanhed, b * HC2 + (c + 1))
                            nc.vector.scalar_tensor_tensor(tanh_[0:r, s, :], tanh_[0:r, s, :], 1.0, ps[0:r, bank, 0:SEQ],
                                                           ALU.add, ALU.mult).then_inc(half_done, 1)
                            dve.wait_ge(half_done, b * HC2 + (c + 1))
                            if not (first and c < 2):
                                dve.wait_ge(g_lo_ready, b * HC2 + (c - 1))
                            nc.vector.scalar_tensor_tensor(gate_[0:r, s, :], tanh_[0:r, s, :], 0.5, ps[0:r, bank, SEQ:2 * SEQ],
                                                           ALU.mult, ALU.mult).then_inc(g_ready, 1)
                            if more and c == 4:
                                norm_stats(dve, sub, b + 1)
                            if more and c == 6:
                                norm_apply(dve, sub, b + 1, xn2)
                        if more:
                            split_xT(dve, sub, b + 1, xT2_hi, xT2_lo, XBANK, lo_ready)
                        dve.wait_ge(done, b + 1)
                        for i in range(QT):
                            nc.vector.tensor_tensor(tile_of(b, i), ps[:, i, :], tile_of(b, i), ALU.add).then_inc(residual, 1)

                    await_group(dve, "f2")
                    await_group(dve, "f2_mask")
                    norm_stats(dve, sub, 0)
                    norm_apply(dve, sub, 0, xn2)
                    dve.wait_ge(hi_cut, 1)
                    subtract_high(nc.vector, a13_lo[:, :, :], l2_a13[:, :, :], a13_hi[:, :, :])
                    subtract_high(nc.vector, b13_parts[64:96, :], l2_b13[64:96, :], b13_parts[64:96, :]).then_inc(lo_cut, 1)
                    split_xT(dve, sub, 0, xT2_hi, xT2_lo, XBANK, lo_ready)
                    for c in range(AHEAD):
                        cut_chunk(c)
                    each_turn(dve, turn_of)

                @block.scalar
                def _(act):
                    def cut_chunk(c):
                        r = rows(c)
                        for k in range(KC):
                            nc.scalar.activation(chunk_of(w13_hi, c)[:, k], chunk_of(l2_w13, c)[:, k], ACT.Copy)
                        nc.scalar.activation(a2_hi[0:r, c, :], l2_a2[0:r, c, :], ACT.Copy)
                        nc.scalar.activation(w2_hi[0:r, c, :], l2_w2[0:r, c, :], ACT.Copy).then_inc(hi_cut, 1)

                    def high_gate(b, c):
                        r = rows(c)
                        act.wait_ge(g_ready, b * HC2 + (c + 1))
                        if c >= 4:
                            act.wait_ge(down_done, b * HC2 + (c - 3))
                        else:
                            act.wait_ge(residual, updates(sub, b))
                        nc.scalar.activation(g_hi[0:r, c % 4, :], gate_[0:r, c % 2, :], ACT.Copy).then_inc(g_hi_ready, 1)

                    def turn_of(b, first, more):
                        act.wait_ge(low_done, b + 1)
                        for j in range(2):
                            last = nc.scalar.activation(lowT[:, j, :], ps[0:96, 6, 0:SEQ], ACT.Copy, scale=lmask[:, j:j + 1])
                        last.then_inc(low_hi_ready, 1)
                        for c in range(HC2):
                            r, s, bank = rows(c), c % 2, 2 + c % 4
                            if first and c + AHEAD < HC2:
                                cut_chunk(c + AHEAD)
                            act.wait_ge(up_done, b * HC2 + (c + 1))
                            if not (first and c < 2):
                                act.wait_ge(g_ready, b * HC2 + (c - 1))
                            nc.scalar.activation(tanh_[0:r, s, :], ps[0:r, bank, 0:SEQ], ACT.Tanh, scale=0.5).then_inc(tanhed, 1)
                            if c >= 1:
                                high_gate(b, c - 1)
                        if more:
                            norm_scalar(act, sub, b + 1, xT2_hi, XBANK)
                        high_gate(b, HC2 - 1)
                        act.wait_ge(down_done, b * HC2 + HC2)
                        nc.scalar.activation(low2T[0:RANK, :], ps[0:RANK, 7, 0:SEQ], ACT.Copy, scale=2.0).then_inc(low2_ready, 1)

                    await_group(act, "f2")
                    await_group(act, "f2_mask")
                    act.wait_ge(zeroed, 1)
                    nc.scalar.activation(a13_hi[:, :, :], l2_a13[:, :, :], ACT.Copy)
                    nc.scalar.activation(b13_parts[:, :], l2_b13[:, :], ACT.Copy).then_inc(hi_cut, 1)
                    norm_scalar(act, sub, 0, xT2_hi, XBANK)
                    for c in range(AHEAD):
                        cut_chunk(c)
                    each_turn(act, turn_of)

                @block.tensor
                def _(pe):
                    def xT_parts(k):
                        return xT2_hi[:, k, :], xT2_lo[:, k, :]

                    def turn_of(b, first, more):
                        pe.wait_ge(lo_ready, b * QT + QT)
                        if first:
                            pe.wait_ge(lo_cut, 1)
                        for k in range(KC):
                            last = product(ps[0:96, 6, 0:SEQ], (a13_hi[:, k, :], a13_lo[:, k, :]), xT_parts(k), k == 0, k == KC - 1)
                        last.then_inc(low_done, 1)

                        def up(c):
                            r = rows(c)
                            if first:
                                pe.wait_ge(lo_cut, c + 2)
                            if c >= 4:
                                pe.wait_ge(g_ready, b * HC2 + (c - 3))
                            for j in range(2):
                                o = ps[0:r, 2 + c % 4, j * SEQ:(j + 1) * SEQ]
                                for k in range(KC):
                                    at = slice(j * HID2 + c * P, j * HID2 + c * P + r)
                                    product(o, (w13_hi[:, k, at], w13_lo[:, k, at]), xT_parts(k), k == 0, False)
                                if c == 0 and j == 0:
                                    pe.wait_ge(lowT_ready, b + 1)
                                last = nc.tensor.matmul(o, b13_parts[:, c * P:c * P + r], lowT[:, j, :], start=False, stop=True)
                            last.then_inc(up_done, 1)

                        def down(c):
                            r, s = rows(c), c % 4
                            pe.wait_ge(g_lo_ready, b * HC2 + (c + 1))
                            if c == 0:
                                pe.wait_ge(residual, updates(sub, b))
                            for i in range(QT):
                                at = slice(i * P, (i + 1) * P)
                                product(ps[:, i, :], (g_hi[0:r, s, at], g_lo[0:r, s, at]), (w2_hi[0:r, c, :], w2_lo[0:r, c, :]), c == 0, False)
                            last = product(ps[0:RANK, 7, 0:SEQ], (a2_hi[0:r, c, :], a2_lo[0:r, c, :]), (g_hi[0:r, s, :], g_lo[0:r, s, :]),
                                           c == 0, c == HC2 - 1)
                            last.then_inc(down_done, 1)

                        for c in range(HC2 + 2):
                            if c < HC2:
                                up(c)
                            if c == HC2 and more:
                                norm_tensor(pe, sub, b + 1, xn2, XBANK)
                            if c >= 2:
                                down(c - 2)
                        pe.wait_ge(low2_ready, b + 1)
                        for i in range(QT):
                            last = nc.tensor.matmul(ps[:, i, :], low2T[:, i * P:(i + 1) * P], l2_b2[:, :], start=False, stop=True)
                        last.then_inc(done, 1)

                    await_group(pe, "f2")
                    pe.wait_ge(zeroed, 1)
                    norm_tensor(pe, sub, 0, xn2, XBANK)
                    each_turn(pe, turn_of)

        def layer3_feed_forward(sub):
            hi_cut = sem("f3_hi_cut")
            lo_cut = sem("f3_lo_cut")
            lat_done = sem("f3_lat_done")
            lat_hi_ready = sem("f3_lat_hi_ready")
            lat_lo_ready = sem("f3_lat_lo_ready")
            logitsT_ready = sem("f3_logitsT_ready")
            logits_done = sem("f3_logits_done")
            expert_done = sem("f3_expert_done")
            exp_hi_ready = sem("f3_exp_hi_ready")
            exp_lo_ready = sem("f3_exp_lo_ready")
            up_done = sem("f3_up_done")
            relued = sem("f3_relued")
            squared = sem("f3_squared")
            h_hi_ready = sem("f3_h_hi_ready")
            h_lo_ready = sem("f3_h_lo_ready")
            down_done = sem("f3_down_done")
            shared_kept = sem("f3_shared_kept")
            summed = sem("f3_summed")
            chain_sem = sem("f3_chain")
            logits_kept = sem("f3_logits_kept")
            routing_ready = sem("f3_routing_ready")
            yvar = sem("f3_yvar")
            pool_chain = sem("f3_pool_chain")
            yrstd_ready = sem("f3_yrstd_ready")
            stored = sem("f3_stored")
            final = sem("f3_final")
            XBANK = 5, -3
            AHEAD = 2

            def bank_of(c):
                return 2 + (c + 3) % 4

            with nc.Block() as block:
                @block.sync
                def _(sp):
                    with sp.Fori(0, BATCH) as b:
                        for i in range(QT):
                            sp.wait_ge(final, b * QT + (i + 1))
                            sp.dma_start(out[bass.ds(b * QT + i, 1), :, :].rearrange("a p d -> p (a d)"), tile_of(b, i)).then_inc(stored, 16)
                    sp.wait_ge(stored, 16 * TILES)

                @block.gpsimd
                def _(pool):
                    norm_gpsimd(pool, sub, 0)

                    def turn_of(b, first, more):
                        for c in range(IC3):
                            pool.wait_ge(relued, b * IC3 + (c + 1))
                            if not (first and c < 2):
                                pool.wait_ge(h_lo_ready, b * IC3 + (c - 1))
                            nc.gpsimd.tensor_tensor(square[:, c % 2, :], relu_[:, c % 2, :], relu_[:, c % 2, :], ALU.mult).then_inc(squared, 1)
                            if more and c == 4:
                                norm_gpsimd(pool, sub, b + 1)
                        pool.wait_ge(yvar, b + 1)
                        nc.gpsimd.tensor_tensor(yrstd[:, :, 0], ymv[:, :, 1], eps[:, :].to_broadcast([P, QT]), ALU.add).then_inc(pool_chain, 1)
                        pool.wait_ge(pool_chain, b + 1)
                        nc.gpsimd.tensor_tensor(yrstd[:, :, 0], yrstd[:, :, 0], minus_half[:, :].to_broadcast([P, QT]),
                                                ALU.pow).then_inc(yrstd_ready, 1)

                    each_turn(pool, turn_of)

                @block.vector
                def _(dve):
                    gamma, beta = (l3_gb[:, j * DIM:(j + 1) * DIM].unsqueeze(1).to_broadcast([P, QT, DIM]) for j in range(2))

                    def cut_chunk(c):
                        dve.wait_ge(hi_cut, c + 2)
                        at = slice(c * P, (c + 1) * P)
                        subtract_high(nc.vector, up_lo[:, :, at], l3_up[:, :, at], up_hi[:, :, at])
                        subtract_high(nc.vector, down_lo[:, c, :], l3_down[:, c, :], down_hi[:, c, :]).then_inc(lo_cut, 1)

                    def scale_out(b, step):
                        turn = b * 3
                        if step == 0:
                            dve.wait_ge(yrstd_ready, b + 1)
                            for i in range(QT):
                                last = nc.vector.tensor_scalar(shared[:, i, :], shared[:, i, :], ymv[:, i, 0:1], yrstd[:, i, :],
                                                               ALU.subtract, ALU.mult)
                            last.then_inc(chain_sem, 1)
                        elif step == 1:
                            dve.wait_ge(chain_sem, turn + 1)
                            nc.vector.tensor_tensor(shared[:, :, :], shared[:, :, :], gamma, ALU.mult).then_inc(chain_sem, 1)
                        elif step == 2:
                            dve.wait_ge(chain_sem, turn + 2)
                            nc.vector.tensor_tensor(shared[:, :, :], shared[:, :, :], beta, ALU.add).then_inc(chain_sem, 1)
                        elif step == 3:
                            dve.wait_ge(chain_sem, turn + 3)
                            for i in range(QT):
                                nc.vector.tensor_tensor(tile_of(b, i), shared[:, i, :], tile_of(b, i), ALU.add).then_inc(final, 1)

                    def turn_of(b, first, more):
                        dve.wait_ge(lat_hi_ready, b + 1)
                        subtract_high(nc.vector, lat_lo[:, :, :], ps[:, 2, :].rearrange("p (m t) -> p m t", m=LC3), lat_hi[:, :, :])\
                            .then_inc(lat_lo_ready, 1)
                        dve.wait_ge(exp_hi_ready, b + 1)
                        subtract_high(nc.vector, exp_lo[:, :, :], ps[:, 4, :].rearrange("p (m t) -> p m t", m=LC3), exp_hi[:, :, :])\
                            .then_inc(exp_lo_ready, 1)
                        dve.wait_ge(logits_done, b + 1)
                        nc.vector.tensor_copy(logits3[:, :, :], ps[:, 3, 0:QT * E3].rearrange("p (i e) -> p i e", i=QT)).then_inc(logits_kept, 1)
                        dve.drain()
                        for i in range(QT):
                            nc.vector.max(top8[:, i, :], logits3[:, i, :])
                        dve.drain()
                        nc.vector.tensor_tensor(routing[:, :], top8[:, :, 0], top8[:, :, 1], ALU.add).then_inc(routing_ready, 1)
                        for c in range(IC3):
                            if first and c + AHEAD < IC3:
                                cut_chunk(c + AHEAD)
                            dve.wait_ge(h_hi_ready, b * IC3 + (c + 1))
                            subtract_high(nc.vector, h_lo[:, c % 4, :], square[:, c % 2, :], h_hi[:, c % 4, :]).then_inc(h_lo_ready, 1)
                            if not first:
                                scale_out(b - 1, c)
                            if more and c == 4:
                                norm_stats(dve, sub, b + 1)
                            if more and c == 6:
                                norm_apply(dve, sub, b + 1, xn3)
                        if more:
                            split_xT(dve, sub, b + 1, xT3_hi, xT3_lo, XBANK[0], lo_ready, XBANK[1])
                        dve.wait_ge(routing_ready, b + 1)
                        for i in range(QT):
                            dve.wait_ge(shared_kept, b * QT + (i + 1))
                            nc.vector.scalar_tensor_tensor(shared[:, i, :], ps[:, 6 + i, :], routing[:, i:i + 1], shared[:, i, :],
                                                           ALU.mult, ALU.add).then_inc(summed, 1)
                        dve.drain()
                        for i in range(QT):
                            nc.vector.bn_stats(ystats[:, i, :], shared[:, i, :])
                        dve.drain()
                        for i in range(QT):
                            last = nc.vector.bn_aggr(ymv[:, i, :], ystats[:, i, :])
                        last.then_inc(yvar, 1)

                    await_group(dve, "f3")
                    norm_stats(dve, sub, 0)
                    norm_apply(dve, sub, 0, xn3)
                    dve.wait_ge(hi_cut, 1)
                    subtract_high(nc.vector, fc1_lo[:, :, :], l3_fc1[:, :, :], fc1_hi[:, :, :])
                    split_xT(dve, sub, 0, xT3_hi, xT3_lo, XBANK[0], lo_ready, XBANK[1])
                    subtract_high(nc.vector, expert_lo[:, :, :], l3_expert[:, :, :], expert_hi[:, :, :])
                    subtract_high(nc.vector, fc2_lo[:, :, :], l3_fc2[:, :, :], fc2_hi[:, :, :]).then_inc(lo_cut, 1)
                    for c in range(AHEAD):
                        cut_chunk(c)
                    each_turn(dve, turn_of)
                    for step in range(4):
                        scale_out(BATCH - 1, step)

                @block.scalar
                def _(act):
                    def cut_chunk(c):
                        at = slice(c * P, (c + 1) * P)
                        nc.scalar.activation(up_hi[:, :, at], l3_up[:, :, at], ACT.Copy)
                        nc.scalar.activation(down_hi[:, c, :], l3_down[:, c, :], ACT.Copy).then_inc(hi_cut, 1)

                    def high_square(b, first, c):
                        act.wait_ge(squared, b * IC3 + (c + 1))
                        if not (first and c < 4):
                            act.wait_ge(down_done, b * IC3 + (c - 3))
                        nc.scalar.activation(h_hi[:, c % 4, :], square[:, c % 2, :], ACT.Copy).then_inc(h_hi_ready, 1)

                    def turn_of(b, first, more):
                        act.wait_ge(lat_done, b + 1)
                        nc.scalar.activation(lat_hi[:, :, :], ps[:, 2, :].rearrange("p (m t) -> p m t", m=LC3), ACT.Copy).then_inc(lat_hi_ready, 1)
                        nc.scalar.activation(logitsT[:, :], ps[0:E3, 3, 0:SEQ], ACT.Copy).then_inc(logitsT_ready, 1)
                        act.wait_ge(expert_done, b + 1)
                        nc.scalar.activation(exp_hi[:, :, :], ps[:, 4, :].rearrange("p (m t) -> p m t", m=LC3), ACT.Copy).then_inc(exp_hi_ready, 1)
                        for c in range(IC3):
                            if first and c + AHEAD < IC3:
                                cut_chunk(c + AHEAD)
                            act.wait_ge(up_done, b * IC3 + (c + 1))
                            if not (first and c < 2):
                                act.wait_ge(squared, b * IC3 + (c - 1))
                            nc.scalar.activation(relu_[:, c % 2, :], ps[:, bank_of(c), 0:SEQ], ACT.Relu).then_inc(relued, 1)
                            if c >= 1:
                                high_square(b, first, c - 1)
                        if more:
                            norm_scalar(act, sub, b + 1, xT3_hi, *XBANK)
                        high_square(b, first, IC3 - 1)
                        act.wait_ge(down_done, b * IC3 + IC3)
                        if not first:
                            act.wait_ge(final, b * QT)
                        for i in range(QT):
                            nc.scalar.activation(shared[:, i, :], ps[:, i, :], ACT.Copy).then_inc(shared_kept, 1)

                    await_group(act, "f3")
                    nc.scalar.activation(fc1_hi[:, :, :], l3_fc1[:, :, :], ACT.Copy)
                    nc.scalar.activation(expert_hi[:, :, :], l3_expert[:, :, :], ACT.Copy)
                    nc.scalar.activation(fc2_hi[:, :, :], l3_fc2[:, :, :], ACT.Copy).then_inc(hi_cut, 1)
                    norm_scalar(act, sub, 0, xT3_hi, *XBANK)
                    for c in range(AHEAD):
                        cut_chunk(c)
                    each_turn(act, turn_of)

                @block.tensor
                def _(pe):
                    def xT_parts(k):
                        return xT3_hi[:, k, :], xT3_lo[:, k, :]

                    def turn_of(b, first, more):
                        pe.wait_ge(lo_ready, (BATCH + b) * QT + QT)
                        if first:
                            pe.wait_ge(lo_cut, 1)
                        for m in range(LC3):
                            for k in range(KC):
                                at = slice(m * P, (m + 1) * P)
                                product(ps[:, 2, m * SEQ:(m + 1) * SEQ], (fc1_hi[:, k, at], fc1_lo[:, k, at]), xT_parts(k), k == 0, k == KC - 1)
                        for k in range(KC):
                            at = slice(LAT3, LAT3 + E3)
                            last = product(ps[0:E3, 3, 0:SEQ], (fc1_hi[:, k, at], fc1_lo[:, k, at]), xT_parts(k), k == 0, k == KC - 1)
                        last.then_inc(lat_done, 1)

                        def up(c):
                            if first:
                                pe.wait_ge(lo_cut, c + 2)
                            if c >= 4:
                                pe.wait_ge(relued, b * IC3 + (c - 3))
                            for k in range(KC):
                                at = slice(c * P, (c + 1) * P)
                                last = product(ps[:, bank_of(c), 0:SEQ], (up_hi[:, k, at], up_lo[:, k, at]), xT_parts(k), k == 0, k == KC - 1)
                            last.then_inc(up_done, 1)

                        def down(c):
                            pe.wait_ge(h_lo_ready, b * IC3 + (c + 1))
                            for i in range(QT):
                                at = slice(i * P, (i + 1) * P)
                                last = product(ps[:, i, :], (h_hi[:, c % 4, at], h_lo[:, c % 4, at]), (down_hi[:, c, :], down_lo[:, c, :]),
                                               c == 0, c == IC3 - 1)
                            last.then_inc(down_done, 1)

                        def expert():
                            pe.wait_ge(lat_lo_ready, b + 1)
                            for m in range(LC3):
                                for l in range(LC3):
                                    at = slice(m * P, (m + 1) * P)
                                    last = product(ps[:, 4, m * SEQ:(m + 1) * SEQ], (expert_hi[:, l, at], expert_lo[:, l, at]),
                                                   (lat_hi[:, l, :], lat_lo[:, l, :]), l == 0, l == LC3 - 1)
                            last.then_inc(expert_done, 1)

                        def flip_logits():
                            pe.wait_ge(logitsT_ready, b + 1)
                            for i in range(QT):
                                last = nc.tensor.matmul(ps[:, 3, i * E3:(i + 1) * E3], logitsT[:, i * P:(i + 1) * P], ident[0:E3, 0:E3],
                                                        start=True, stop=True)
                            last.then_inc(logits_done, 1)

                        def routed():
                            pe.wait_ge(exp_lo_ready, b + 1)
                            if not first:
                                pe.wait_ge(summed, b * QT)
                            for i in range(QT):
                                for l in range(LC3):
                                    at = slice(i * P, (i + 1) * P)
                                    product(ps[:, 6 + i, :], (exp_hi[:, l, at], exp_lo[:, l, at]), (fc2_hi[:, l, :], fc2_lo[:, l, :]),
                                            l == 0, l == LC3 - 1)

                        up(0)
                        expert()
                        flip_logits()
                        up(1)
                        routed()
                        pe.wait_ge(logits_kept, b + 1)
                        for c in range(2, IC3 + 2):
                            if c < IC3:
                                up(c)
                            if c == IC3 and more:
                                norm_tensor(pe, sub, b + 1, xn3, *XBANK)
                            down(c - 2)

                    norm_tensor(pe, sub, 0, xn3, *XBANK)
                    each_turn(pe, turn_of)

        val_set0 = sem("mid_zeroed")

        layer0_attention()
        layer0_feed_forward(1)
        attention(0, 2, l1_qkv, l1_wo, "a1", None, ("f1", "a2"), normed_before=True, norm_after=True)
        layer1_feed_forward(3)
        attention(1, 4, l2_qkv, l2_wo, "a2", None, ("f2",), normed_before=True)
        layer2_feed_forward(5)
        attention(2, 6, l3_qkv, None, "a3", "a3_bias", ("a3_bias", "f3"))
        layer3_feed_forward(7)

def _chunks(w, k):
    return w.reshape(k, 128, w.shape[1]).transpose(1, 0, 2)


def _tables():
    import numpy as np

    def bf16(v):
        return (np.ascontiguousarray(v, np.float32).view(np.uint32) >> 16).astype(np.uint16)
    t = {}
    pos = np.arange(256, dtype=np.float32)
    inv = 1.0 / 500000.0 ** (np.arange(0, 128, 2, dtype=np.float32) / 128)
    wavelen = 2.0 * np.pi / inv
    scaled = np.where(wavelen > 1024 / 1.0, inv / 8.0, inv)
    smooth = (1024 / wavelen - 1.0) / (4.0 - 1.0)
    smoothed = (1.0 - smooth) / 8.0 * inv + smooth * inv
    medium = (wavelen <= 1024 / 1.0) & (wavelen >= 1024 / 4.0)
    inv0 = np.where(medium, smoothed, scaled).astype(np.float32)
    ang = (pos[:, None] * inv0[None, :]).astype(np.float32)
    t["l0_cos"] = np.concatenate([np.cos(ang), np.cos(ang)], 1).T.astype(np.float32)
    t["l0_sin"] = np.concatenate([-np.sin(ang), np.sin(ang)], 1).T.astype(np.float32)
    f = (1.0 / 10000.0 ** (np.arange(0, 16, 2, dtype=np.float32) / 16)).astype(np.float32)
    ang = (pos[:, None] * f[None, :]).astype(np.float32)
    cs = np.stack([np.concatenate([np.cos(ang), np.cos(ang)], 1),
                   np.concatenate([-np.sin(ang), np.sin(ang)], 1)], 1)
    t["rope"] = cs.reshape(2, 128, 2, 16).transpose(1, 0, 2, 3).astype(np.float32)
    t["ident"] = np.eye(128, dtype=np.float32)
    t["ident_bf"] = bf16(np.eye(128))
    i = np.arange(128)
    rows_q = np.where(i[None, :] > i[:, None], -1.0e30, 0.0)
    t["masks"] = bf16(np.stack([rows_q, rows_q.T], 1))
    t["lmask"] = np.tile(np.repeat(np.eye(2, dtype=np.float32) * 2.0, 16, axis=0), (3, 1))
    for e in (4, 8):
        low = np.tril(np.ones((e, e), np.float32), -1).reshape(1, e * e)
        t[f"lower{e}"] = np.ascontiguousarray(np.broadcast_to(low, (128, e * e)))
    return {k: np.ascontiguousarray(v) for k, v in t.items()}


def _rows(v):
    import numpy as np
    return np.ascontiguousarray(np.broadcast_to(v.reshape(1, -1), (128, v.size)))


def _layout(a):
    import numpy as np
    o = {}
    o["x"] = a["L0_attn_x"].reshape(8, 128, 512)
    o["l0_wq"] = _chunks(a["L0_attn_Wq"].T, 4).reshape(128, 4, 8, 512).transpose(2, 0, 1, 3)
    o["l0_wk"] = _chunks(a["L0_attn_Wk"].T, 4).reshape(128, 4, 8, 128).transpose(2, 0, 1, 3)
    o["l0_wv"] = _chunks(a["L0_attn_Wv"].T, 4).reshape(128, 4, 4, 256).transpose(2, 0, 1, 3)
    o["l0_wo"] = a["L0_attn_Wo"].T.reshape(8, 4, 128, 512).transpose(0, 2, 1, 3)
    o["l0_ar"] = _chunks(np.concatenate([a["L0_ffn_A"].reshape(64, 512), a["L0_ffn_router_w"]], 0).T, 4)
    o["l0_b"] = np.concatenate([a["L0_ffn_B"].transpose(0, 2, 1).reshape(64, 512), np.zeros((64, 512), np.float32)], 0)
    def halves(w, n):
        return w.reshape(512, n, 8, 2).transpose(0, 1, 3, 2).reshape(512, n * 16)
    o["l1_qkv"] = _chunks(np.concatenate([halves(a["L1_attn_wq"], 32), halves(a["L1_attn_wk"], 8), a["L1_attn_wv"]], 1), 4)
    o["l1_wo"] = _chunks(a["L1_attn_wo"], 4)
    o["l1_w"] = _chunks(a["L1_ffn_weight"].T, 4)
    o["l1_ag"] = _chunks(np.concatenate([a["L1_ffn_lora_A"].transpose(1, 0, 2).reshape(512, 128), a["L1_ffn_gw1"].T], 1), 4)
    o["l1_b"] = a["L1_ffn_lora_B"].reshape(128, 512)
    o["l1_gvec"] = np.concatenate([_rows(a["L1_ffn_gb1"]), _rows(a["L1_ffn_ln_gamma"]), _rows(a["L1_ffn_ln_beta"]), _rows(a["L1_ffn_gb2"])], 1)
    o["l1_gw2"] = a["L1_ffn_gw2"].T
    o["l2_qkv"] = _chunks(np.concatenate([a["L2_attn_wq"].T, a["L2_attn_wk"].T, a["L2_attn_wv"].T], 1), 4)
    o["l2_wo"] = _chunks(a["L2_attn_wo"].T, 4)
    o["l2_w13"] = np.concatenate([_chunks(a["L2_ffn_w1"].T, 4), _chunks(a["L2_ffn_w3"].T, 4)], 2)
    w2 = np.zeros((11 * 128, 512), np.float32)
    w2[:1376] = a["L2_ffn_w2"].T
    o["l2_w2"] = _chunks(w2, 11)
    o["l2_a13"] = _chunks(np.concatenate([a["L2_ffn_lora_A1"], a["L2_ffn_lora_A3"]] * 3, 0).T, 4)
    o["l2_b13"] = np.concatenate([a["L2_ffn_lora_B1"].T, a["L2_ffn_lora_B3"].T] * 3, 0)
    a2 = np.zeros((11 * 128, 16), np.float32)
    a2[:1376] = a["L2_ffn_lora_A2"].T
    o["l2_a2"] = _chunks(a2, 11)
    o["l2_b2"] = np.concatenate([a["L2_ffn_lora_B2"].T, np.zeros((80, 512), np.float32)], 0)
    wq3 = a["L3_attn_Wq"].reshape(2, 16, 16, 512).transpose(1, 0, 2, 3).reshape(512, 512)
    bq3 = a["L3_attn_bq"].reshape(2, 16, 16).transpose(1, 0, 2).reshape(512)
    o["l3_qkv"] = _chunks(np.concatenate([wq3.T, a["L3_attn_Wk"].T, a["L3_attn_Wv"].T], 1), 4)
    o["l3_bias"] = _rows(np.concatenate([bq3, a["L3_attn_bk"], a["L3_attn_bv"]]))
    o["l3_up"] = _chunks(a["L3_ffn_up_w"], 4)
    o["l3_down"] = _chunks(a["L3_ffn_down_w"], 8)
    o["l3_fc1"] = _chunks(np.concatenate([a["L3_ffn_fc1_w"], a["L3_ffn_gate_w"]], 1), 4)
    o["l3_expert"] = _chunks(a["L3_ffn_expert_w"], 2)
    o["l3_fc2"] = _chunks(a["L3_ffn_fc2_w"], 2)
    o["l3_gb"] = np.concatenate([_rows(a["L3_ffn_ln_gamma"]), _rows(a["L3_ffn_ln_beta"])], 1)
    return {k: np.ascontiguousarray(v) for k, v in o.items()}


def kernel(**inputs):
    import numpy as np
    import concourse.bacc as bacc
    from concourse import mybir as mb
    from concourse.bass_utils import run_bass_kernel_spmd

    nc = bacc.Bacc("TRN2", target_bir_lowering=False, num_devices=1)
    laid = _layout({k: np.asarray(v) for k, v in inputs.items()})
    laid.update(_tables())
    arrays, dram = {}, {}
    for name, v in laid.items():
        arrays[f"{name}_dram"] = v
        dram[name] = nc.dram_tensor(f"{name}_dram", v.shape, mb.dt.from_np(v.dtype), kind="ExternalInput").ap()
    out = nc.dram_tensor("out_dram", (8, 128, 512), mb.dt.float32, kind="ExternalOutput").ap()
    four_layers(nc, dram, out)
    r = run_bass_kernel_spmd(nc, [arrays], core_ids=[0])
    return r.results[0]["out_dram"].reshape(4, 256, 512)
```
